# Optimizing a Trainium2 kernel written in Bass

```python
import numpy as np
import jax
import jax.numpy as jnp

def _softmax(x, axis=-1):
    return jax.nn.softmax(x, axis=axis)

def _gelu(x):
    return jax.nn.gelu(x, approximate=True)

def _silu(x):
    return jax.nn.silu(x)

def _sigmoid(x):
    return jax.nn.sigmoid(x)

def _layernorm(x, axis=-1, eps=1e-05):
    m = jnp.mean(x, axis=axis, keepdims=True)
    v = jnp.var(x, axis=axis, keepdims=True)
    return (x - m) / jnp.sqrt(v + eps)

def _scatter_add(tgt, idx, src, axis=0):
    return tgt.at[idx].add(src)

def _segment_sum(src, seg, n):
    return jax.ops.segment_sum(src, seg, n)
kernel_name = 'mk_gnn_preln_d4_gnn_r64_5ccac7'

def setup_inputs(seed: int=0):
    np.random.seed(seed)
    _w = jnp.asarray

    def _rec_inputs():
        import jax
        import jax.numpy as jnp
        _gk = jax.random.key(seed)
        x = -0.0005121 + 1.001 * jax.random.normal(jax.random.fold_in(_gk, 1), (100000, 32), jnp.float32)
        src = jax.random.randint(jax.random.fold_in(_gk, 2), (50000,), 0, 100000, jnp.int32)
        dst = jax.random.randint(jax.random.fold_in(_gk, 3), (50000,), 0, 100000, jnp.int32)
        _o = jnp.argsort(dst, stable=True)
        src = src[_o]
        dst = dst[_o]
        edge_attr_32 = -9.77346e-05 + 0.999888 * jax.random.normal(jax.random.fold_in(_gk, 12), (50000, 32), jnp.float32)
        edge_weight = jax.random.uniform(jax.random.fold_in(_gk, 14), (50000,), jnp.float32, 0.0, 1)
        return (x, src, dst, edge_attr_32, edge_weight)
    x, src, dst, edge_attr_32, edge_weight = _rec_inputs()

    def _L0_gnn_setup():
        import jax, jax.numpy as jnp
        import numpy as np
        N_NODES = 100000
        N_EDGES = 25000
        EMB_DIM = 32
        NUM_LAYERS = 3
        key = jax.random.key(seed)
        k_emb, k_w, k_row, k_col = jax.random.split(key, 4)
        emb = jax.random.normal(k_emb, (N_NODES, EMB_DIM), dtype=jnp.float32)
        edge_weight = jax.random.uniform(k_w, (N_EDGES,), dtype=jnp.float32)
        row = jax.random.randint(k_row, (N_EDGES,), 0, N_NODES, dtype=jnp.int32)
        col = jax.random.randint(k_col, (N_EDGES,), 0, N_NODES, dtype=jnp.int32)
        return {'emb': emb, 'edge_weight': edge_weight, 'row': row, 'col': col, 'num_layers': NUM_LAYERS}
    _L0_gnn_all = _L0_gnn_setup()
    _L0_gnn_in = {k: v for k, v in _L0_gnn_all.items() if k in ()}
    del _L0_gnn_all

    def _L1_gnn_setup():
        import jax, jax.numpy as jnp
        import numpy as np
        N_NODES = 100000
        N_EDGES = 25000
        IN_C, HID_C, OUT_C = (32, 64, 32)

        def _sage_conv(x, src, dst, W_l, b_l, W_r):
            n = x.shape[0]
            agg = jax.ops.segment_sum(x[src], dst, num_segments=n)
            cnt = jax.ops.segment_sum(jnp.ones_like(dst, dtype=x.dtype), dst, num_segments=n)
            agg = agg / jnp.maximum(cnt, 1.0)[:, None]
            return agg @ W_l + b_l + x @ W_r
        key = jax.random.key(seed)
        ks = jax.random.split(key, 8)
        x = jax.random.normal(ks[0], (N_NODES, IN_C), dtype=jnp.float32)
        edge_index = jax.random.randint(ks[1], (2, N_EDGES), 0, N_NODES, dtype=jnp.int64)
        s = 1.0 / np.sqrt(IN_C)
        W1_l = jax.random.uniform(ks[2], (IN_C, HID_C), jnp.float32, -s, s)
        W1_r = jax.random.uniform(ks[3], (IN_C, HID_C), jnp.float32, -s, s)
        b1 = jnp.zeros((HID_C,), jnp.float32)
        s2 = 1.0 / np.sqrt(HID_C)
        W2_l = jax.random.uniform(ks[4], (HID_C, OUT_C), jnp.float32, -s2, s2)
        W2_r = jax.random.uniform(ks[5], (HID_C, OUT_C), jnp.float32, -s2, s2)
        b2 = jnp.zeros((OUT_C,), jnp.float32)
        return {'x': x, 'edge_index': edge_index, 'W1_l': W1_l, 'b1': b1, 'W1_r': W1_r, 'W2_l': W2_l, 'b2': b2, 'W2_r': W2_r}
    _L1_gnn_all = _L1_gnn_setup()
    _L1_gnn_in = {k: v for k, v in _L1_gnn_all.items() if k in ('W1_l', 'b1', 'W1_r', 'W2_l', 'b2', 'W2_r')}
    del _L1_gnn_all

    def _L2_gnn_setup():
        import jax, jax.numpy as jnp
        import numpy as np
        N_NODES = 50000
        N_EDGES = 25000
        D_FEAT = 32
        key = jax.random.key(seed)
        k1, k2, k3, k4 = jax.random.split(key, 4)
        node_feat = jax.random.normal(k1, (N_NODES, D_FEAT), dtype=jnp.float32)
        edge_feat = jax.random.normal(k2, (N_EDGES, D_FEAT), dtype=jnp.float32)
        eps = jnp.zeros((1,), dtype=jnp.float32)
        src = jax.random.randint(k3, (N_EDGES,), 0, N_NODES, dtype=jnp.int64)
        dst = jax.random.randint(k4, (N_EDGES,), 0, N_NODES, dtype=jnp.int64)
        return {'node_feat': node_feat, 'edge_feat': edge_feat, 'eps': eps, 'src': src, 'dst': dst}
    _L2_gnn_all = _L2_gnn_setup()
    _L2_gnn_in = {k: v for k, v in _L2_gnn_all.items() if k in ('eps',)}
    del _L2_gnn_all

    def _L3_gnn_setup():
        import jax, jax.numpy as jnp
        import numpy as np
        N_NODES = 100000
        N_EDGES = 25000
        D_FEAT = 32
        key = jax.random.key(seed)
        k1, k2, k3 = jax.random.split(key, 3)
        x = jax.random.normal(k1, (N_NODES, D_FEAT), dtype=jnp.float32)
        a = jax.random.randint(k2, (2, N_EDGES), 0, N_NODES, dtype=jnp.int64)
        e = jax.random.normal(k3, (N_EDGES,), dtype=jnp.float32)
        return {'x': x, 'a': a, 'e': e}
    _L3_gnn_all = _L3_gnn_setup()
    _L3_gnn_in = {k: v for k, v in _L3_gnn_all.items() if k in ()}
    del _L3_gnn_all
    return {'x': x, 'src': src, 'dst': dst, 'edge_attr_32': edge_attr_32, 'edge_weight': edge_weight, 'L1_gnn_W1_l': _L1_gnn_in['W1_l'], 'L1_gnn_b1': _L1_gnn_in['b1'], 'L1_gnn_W1_r': _L1_gnn_in['W1_r'], 'L1_gnn_W2_l': _L1_gnn_in['W2_l'], 'L1_gnn_b2': _L1_gnn_in['b2'], 'L1_gnn_W2_r': _L1_gnn_in['W2_r'], 'L2_gnn_eps': _L2_gnn_in['eps']}

def reference(x, src, dst, edge_attr_32, edge_weight, L1_gnn_W1_l, L1_gnn_b1, L1_gnn_W1_r, L1_gnn_W2_l, L1_gnn_b2, L1_gnn_W2_r, L2_gnn_eps):
    import jax
    import jax.numpy as jnp

    def _L0_gnn_ref(emb, edge_weight, row, col, num_layers):
        import jax, jax.numpy as jnp
        import numpy as np
        N_NODES = 100000
        N_EDGES = 25000
        EMB_DIM = 32
        NUM_LAYERS = 3
        n = emb.shape[0]
        w = edge_weight[:, None]
        X = emb
        for _ in range(num_layers):
            msgs = w * X[col]
            X = jax.ops.segment_sum(msgs, row, num_segments=n)
        return X

    def _L1_gnn_ref(x, edge_index, W1_l, b1, W1_r, W2_l, b2, W2_r):
        import jax, jax.numpy as jnp
        import numpy as np
        N_NODES = 100000
        N_EDGES = 25000
        IN_C, HID_C, OUT_C = (32, 64, 32)

        def _sage_conv(x, src, dst, W_l, b_l, W_r):
            n = x.shape[0]
            agg = jax.ops.segment_sum(x[src], dst, num_segments=n)
            cnt = jax.ops.segment_sum(jnp.ones_like(dst, dtype=x.dtype), dst, num_segments=n)
            agg = agg / jnp.maximum(cnt, 1.0)[:, None]
            return agg @ W_l + b_l + x @ W_r
        src, dst = (edge_index[0], edge_index[1])
        h = jax.nn.relu(_sage_conv(x, src, dst, W1_l, b1, W1_r))
        out = _sage_conv(h, src, dst, W2_l, b2, W2_r)
        return out

    def _L2_gnn_ref(node_feat, edge_feat, eps, src, dst):
        import jax, jax.numpy as jnp
        import numpy as np
        N_NODES = 50000
        N_EDGES = 25000
        D_FEAT = 32
        m = jax.nn.relu(node_feat[src] + edge_feat)
        neigh = jax.ops.segment_sum(m, dst, num_segments=node_feat.shape[0])
        return (1.0 + eps[0]) * node_feat + neigh

    def _L3_gnn_ref(x, a, e):
        import jax, jax.numpy as jnp
        import numpy as np
        N_NODES = 100000
        N_EDGES = 25000
        D_FEAT = 32
        src = a[0]
        tgt = a[1]
        msgs = x[src] * e[:, None]
        out = jax.ops.segment_sum(msgs, tgt, num_segments=x.shape[0])
        return out
    edge_index = jnp.stack([src, dst])
    h = jnp.maximum(_layernorm(x, axis=-1), 0.0)
    x = x + _L0_gnn_ref(h, edge_weight, src, dst, 3)
    h = jnp.maximum(_layernorm(x, axis=-1), 0.0)
    x = x + _L1_gnn_ref(h, edge_index, L1_gnn_W1_l, L1_gnn_b1, L1_gnn_W1_r, L1_gnn_W2_l, L1_gnn_b2, L1_gnn_W2_r)
    h = jnp.maximum(_layernorm(x, axis=-1), 0.0)
    x = x + _L2_gnn_ref(h, edge_attr_32, L2_gnn_eps, src, dst)
    h = jnp.maximum(_layernorm(x, axis=-1), 0.0)
    x = x + _L3_gnn_ref(h, edge_index, edge_weight)
    return x

_drawn_inputs = setup_inputs


def setup_inputs(seed=0):
    import zlib

    import numpy as np

    out = dict(_drawn_inputs(seed))
    spreads = {'L1_gnn_b1': (0.0, 0.1), 'L1_gnn_b2': (0.0, 0.1)}
    factors = {}
    for name, (base, spread) in spreads.items():
        noise = np.random.default_rng([zlib.crc32(name.encode()), seed]).standard_normal(out[name].shape)
        drawn = base * np.exp(spread * noise) if base else spread * noise
        out[name] = jnp.asarray(drawn.astype(out[name].dtype))
    for name, factor in factors.items():
        out[name] = (out[name] * factor).astype(out[name].dtype)
    return out
```

```python
import concourse.bass as bass
from concourse import mybir
from contextlib import ExitStack

FP32 = mybir.dt.float32
I32 = mybir.dt.int32
ALU = mybir.AluOpType
ACT = mybir.ActivationFunctionType
AX = mybir.AxisListType

P = 128
N, F = 100000, 32
E = 50000
HID = 64
COLS = -(-E // (P * 28)) * 28
EP = P * COLS
CC = 28
NCH = COLS // CC
PAIRS = NCH // 2
FULL_P = E // COLS
REST = E - FULL_P * COLS
ROW = F + 2
ZROWS = 80
CARRY_ROWS = EP
ZERO_ROW = EP + P
TROWS = EP + P + ZROWS
NP_, NPP = 125, 800
NOWHERE = float(1 << 20)
SB = 6250
LN_EPS = 1e-5
ADDS = 3
TO_DST = ADDS
R0 = ADDS + 1
ROUNDS = R0 + 4
BLK = 4
AROW = BLK * F
AROWS = N + P
ZW = AROWS * AROW // P // 16
NB = 40
TILES4 = CC // 4
DC_LAST = NPP - 2 * NCH * CC


class Steps:

    def __init__(self, eng, sem):
        self.eng, self.sem, self.base, self.reg, self.per, self.n = eng, sem, 0, None, 0, 0

    def loop(self, reg, per):
        self.reg, self.per, self.n = reg, per, 0

    def end(self, times, where):
        assert self.n == self.per, (where, self.n, self.per)
        self.base, self.reg, self.n = self.base + times * self.per, None, 0

    def done(self, ins):
        ins.then_inc(self.sem, 1)
        self.n += 1
        self.eng.wait_ge(self.sem, self.base + self.n if self.reg is None else self.reg * self.per + (self.base + self.n))
        if self.reg is None:
            self.base, self.n = self.base + self.n, 0


def gnn_kernel(nc, x, src, dst, ea, w, W1l, b1, W1r, W2l, b2, W2r, eps, out):
    with ExitStack() as ctx:
        def sb(name, shape, dt=FP32):
            return ctx.enter_context(nc.sbuf_tensor(name, shape, dt))

        def ps(name, shape):
            return ctx.enter_context(nc.psum_tensor(name, shape, FP32))

        def sem(name):
            return ctx.enter_context(nc.semaphore(name))

        adds = [nc.dram_tensor(f"adds{r}", [AROWS * BLK, F], FP32) for r in range(ADDS)]
        by_node = [a[:, :].rearrange("(n b) f -> n (b f)", b=BLK) for a in adds]
        pos_tab = nc.dram_tensor("pos_tab", [N, 2], FP32)
        node_tab = nc.dram_tensor("node_tab", [N, ROW], FP32)
        sums = {r: nc.dram_tensor(f"sums{r}", [TROWS, F], FP32) for r in range(R0, ROUNDS - 1)}
        ea_pad = nc.dram_tensor("ea_pad", [EP, F], FP32)
        ea_perm = nc.dram_tensor("ea_perm", [EP, F], FP32)
        rec_perm = nc.dram_tensor("rec_perm", [EP, 4], I32)

        xs = sb("xs", [P, COLS * F])
        xd = sb("xd", [P, COLS * F])
        W = CC * F
        late = sb("late", [P, 7 * W + 3 * COLS])
        cut = lambda k, n=1: late[:, k * W:(k + n) * W]
        msg, km, sc, tout = cut(0), [cut(1), cut(2)], [cut(3), cut(4)], [cut(5), cut(6)]
        zeros = late[:, 0:ZW]
        prep = [late[:, 7 * W + k * COLS:7 * W + (k + 1) * COLS] for k in range(3)]
        last, cnt, ones = prep
        nx = [late[:, k * NB * F:(k + 1) * NB * F] for k in range(2)]
        nt = [late[:, 2 * NB * F + k * NB * ROW:2 * NB * F + (k + 1) * NB * ROW] for k in range(2)]
        sel = xs[:, 0:CC * P]
        arow = [xs[:, CC * P + k * W:CC * P + (k + 1) * W] for k in range(2)]
        low = xs[:, CC * P + 2 * W:CC * P + 2 * W + 4 * P]
        lowsel = xs[:, CC * P + 2 * W + 4 * P:CC * P + 2 * W + 8 * P]
        amsg = xs[:, CC * P + 2 * W + 8 * P:CC * P + 3 * W + 8 * P]
        na = [xs[:, k * NB * AROW:(k + 1) * NB * AROW] for k in range(2)]
        npt = [xs[:, 2 * NB * AROW + k * 2 * NB:2 * NB * AROW + (k + 1) * 2 * NB] for k in range(2)]
        src_i, dst_i = sb("src_i", [P, COLS], I32), sb("dst_i", [P, COLS], I32)
        wt = sb("wt", [P, COLS])
        dprev, dnext = sb("dprev", [P, COLS], I32), sb("dnext", [P, COLS], I32)
        keep, keepz = sb("keep", [P, COLS]), sb("keepz", [P, COLS])
        pm = sb("pm", [P, COLS])
        ic_s = sb("ic_s", [P, COLS])
        ic_d = sb("ic_d", [P, COLS])
        epos = sb("epos", [P, COLS])
        sidx = sb("sidx", [P, COLS])
        gdst = sb("gdst", [P, COLS + 2 * CC])
        gidx = sb("gidx", [P, 3 * COLS + 2 * CC])
        aidx = sb("aidx", [P, COLS])
        idxst = [sb(f"idxst{s}", [P, CC], I32) for s in range(2)]
        aidxst = [sb(f"aidxst{s}", [P, CC], I32) for s in range(2)]
        srcst = sb("srcst", [P, CC])
        b4, rep = sb("b4", [P, CC]), sb("rep", [P, CC])
        g = [sb(f"g{s}", [P, CC * AROW]) for s in range(2)]
        td = [g[s][:, CC * ROW:CC * ROW + W] for s in range(2)]
        eat = [g[s][:, CC * ROW + W:CC * ROW + 2 * W] for s in range(2)]
        state = sb("state", [P, F])
        carry = sb("carry", [P, F])
        carry_t = sb("carry_t", [F, P + 1])
        last_t = sb("last_t", [F, P])
        pm_t = sb("pm_t", [F, P])
        pm_b = sb("pm_b", [P, F])
        cidx_f, cidx = sb("cidx_f", [P, 1]), sb("cidx", [P, 1], I32)
        small = sb("small", [P, 8])
        first = sb("first", [P, 8])
        flag = sb("flag", [1, 1], I32)
        xc, sq = sb("xc", [P, W]), sb("sq", [P, W])
        s1, mean = sb("s1", [P, CC]), sb("mean", [P, CC])
        var, sd, rs = sb("var", [P, CC]), sb("sd", [P, CC]), sb("rs", [P, CC])
        ah = sb("ah", [P, CC * 2 * F])
        aht, h1t = sb("aht", [P, 512]), sb("h1t", [P, 512])
        w1b, w2b = sb("w1b", [P, P]), sb("w2b", [P, P])
        b1b, b2b, eps1, lneps = sb("b1b", [P, 1]), sb("b2b", [P, F]), sb("eps1", [P, 1]), sb("lneps", [P, 1])
        ident = sb("ident", [P, P])
        zrow = sb("zrow", [P, F])
        dn = eat[0]
        pp = g[0][0:NP_, 0:2 * NPP]
        ocol, pcol = sb("ocol", [P, 1]), sb("pcol", [P, 1])

        tp, m1, cp = ps("tp", [P, 512]), ps("m1", [P, 512]), ps("cp", [P, 512])
        m2 = ps("m2", [P, 2048])
        dup = [tp, m1]

        edges_in, edges_0 = sem("edges_in"), sem("edges_0")
        weights_in, weights_0, consts = sem("weights_in"), sem("weights_0"), sem("consts")
        prev_in, next_in, dst_ready = sem("prev_in"), sem("next_in"), sem("dst_ready")
        bad_ready, bad_sum, flag_ready = sem("bad_ready"), sem("bad_sum"), sem("flag_ready")
        ea_copied, zeros_in, zero_rows = sem("ea_copied"), sem("zeros_in"), sem("zero_rows")
        iotas, sort_in, ranks_ready, block_used, sorted_ready = (sem("iotas"), sem("sort_in"), sem("ranks_ready"),
                                                                 sem("block_used"), sem("sorted_ready"))
        sort_dma, rank_steps = sem("sort_dma"), sem("rank_steps")
        dve_s, act_s, pool_s = sem("dve_s"), sem("act_s"), sem("pool_s")
        meta_ready = sem("meta_ready")
        adds_clear = [sem(f"adds_clear{r}") for r in range(ADDS)]
        adds_done = [sem(f"adds_done{b}") for b in range(BLK)]
        low_ready, srcst_ready, dup_ready, sel_ready, amsg_ready, merged, arow_ready, arow_free = (
            sem("low_ready"), sem("srcst_ready"), sem("dup_ready"), sem("sel_ready"), sem("amsg_ready"), sem("merged"),
            sem("arow_ready"), sem("arow_free"))
        aidx_staged, added = sem("aidx_staged"), sem("added")
        pp_preset, pos_init, pos_dma, pos_ready = sem("pp_preset"), sem("pos_init"), sem("pos_dma"), sem("pos_ready")
        nx_in = [sem(f"nx_in{s}") for s in range(2)]
        nsum_ready, nsum_used, nt_ready, nt_out = sem("nsum_ready"), sem("nsum_used"), sem("nt_ready"), sem("nt_out")
        node_ready = sem("node_ready")
        dn_in, dn_done, dn_out = sem("dn_in"), sem("dn_done"), sem("dn_out")
        var_ready, sd_ready = sem("var_ready"), sem("sd_ready")
        ah_ready, tp_ready, aht_ready, m1_ready, h1t_ready, m2_ready, m2_free = (
            sem("ah_ready"), sem("tp_ready"), sem("aht_ready"), sem("m1_ready"), sem("h1t_ready"), sem("m2_ready"), sem("m2_free"))
        g_full = [sem(f"g_full{s}") for s in range(2)]
        g_free, idx_staged = sem("g_free"), sem("idx_staged")
        km_ready, scan_done, tout_ready, tout_free = sem("km_ready"), sem("scan_done"), sem("tout_ready"), sem("tout_free")
        tout_dma = sem("tout_dma")
        td_dma, td_full, td_free = sem("td_dma"), sem("td_full"), sem("td_free")
        cl_ready, clt_ready, ct_ready, cc_ready, carry_ready, carry_done = (
            sem("cl_ready"), sem("clt_ready"), sem("ct_ready"), sem("cc_ready"), sem("carry_ready"), sem("carry_done"))
        xd_ready, node_dma, rows_ready, rows_free, out_dma = (
            sem("xd_ready"), sem("node_dma"), sem("rows_ready"), sem("rows_free"), sem("out_dma"))

        LN = {0: "D", R0: "SNN", R0 + 1: "SD", R0 + 2: "SD", R0 + 3: "SNN"}
        MM = {R0: "N", R0 + 1: "SD", R0 + 3: "N"}
        D_SIDE = (R0 + 1, R0 + 2, R0 + 3)
        LOADS = {R0 + 1: 1, R0 + 2: 2, R0 + 3: 1}
        ALL_NODES = {R0: 0, R0 + 3: NCH}
        ln_base, mm_base, td_base = {}, {}, {}
        a, b, c = 0, 0, 0
        for r in range(ROUNDS):
            ln_base[r], mm_base[r], td_base[r] = a, b, c
            a, b, c = a + NCH * len(LN.get(r, "")), b + NCH * len(MM.get(r, "")), c + NCH * LOADS.get(r, 0)
            if r == R0:
                ln_base["last"], mm_base["last"] = a, b
                a, b = a + 2, b + 1
        BATCHES = {CC: (4, 4, 4, 2), DC_LAST: (2, 2, 2, 2)}
        QE = 4

        def v3(ap, inner):
            return ap.rearrange("p (t f) -> p t f", f=inner)

        def bc(ap, n, parts=P):
            return ap.unsqueeze(2).to_broadcast([parts, ap.shape[1], n])

        block = ctx.enter_context(nc.Block())

        @block.sync
        def _(sp):
            sp.wait_ge(edges_0, 3)
            for tile, dram in ((src_i, src), (dst_i, dst), (wt, w)):
                sp.dma_start(tile[0:FULL_P, :], dram[0:FULL_P * COLS].rearrange("(p t) -> p t", t=COLS)).then_inc(edges_in, 16)
                sp.dma_start(tile[FULL_P:FULL_P + 1, 0:REST],
                             dram[FULL_P * COLS:E].rearrange("(p t) -> p t", p=1)).then_inc(edges_in, 16)
            sp.wait_ge(weights_0, 1)
            for t in range(2):
                o = t * 2 * F
                sp.dma_start(w1b[o:o + F, t * HID:(t + 1) * HID], W1l).then_inc(weights_in, 16)
                sp.dma_start(w1b[o + F:o + 2 * F, t * HID:(t + 1) * HID], W1r).then_inc(weights_in, 16)
                sp.dma_start(w2b[t * HID:(t + 1) * HID, o:o + F], W2l).then_inc(weights_in, 16)
                sp.dma_start(w2b[t * HID:(t + 1) * HID, o + F:o + 2 * F], W2r).then_inc(weights_in, 16)
                sp.dma_start(b1b[t * HID:(t + 1) * HID, :], b1.rearrange("(p a) -> p a", a=1)).then_inc(weights_in, 16)
            sp.dma_start(b2b[:, :], b2.rearrange("(a f) -> a f", a=1).to_broadcast([P, F])).then_inc(weights_in, 16)
            sp.dma_start(eps1[:, :], eps.rearrange("(a f) -> a f", a=1).to_broadcast([P, 1])).then_inc(weights_in, 16)
            sp.wait_ge(pp_preset, 2)
            sp.dma_start(pos_tab[:, :].rearrange("(p n) f -> p (n f)", p=NP_), pp).then_inc(pos_init, 16)
            sp.wait_ge(zeros_in, 2)

            def clear(r):
                av = adds[r][:, :].rearrange("(p n) f -> p (n f)", p=P)
                for k in range(16):
                    sp.dma_start(av[:, k * ZW:(k + 1) * ZW], zeros).then_inc(adds_clear[r], 16)

            sp.wait_ge(dst_ready, 1)
            sp.dma_start(dprev[1:P, 0:1], dst_i[0:P - 1, COLS - 1:COLS]).then_inc(prev_in, 16)
            sp.dma_start(ea_pad[0:E, :], ea).then_inc(ea_copied, 16)
            sp.dma_start(ea_pad[E:E + P, :], zrow[:, :]).then_inc(ea_copied, 16)
            sp.dma_start(ea_pad[E + P:EP, :], zrow[0:EP - E - P, :]).then_inc(ea_copied, 16)
            sp.wait_ge(dst_ready, 2)
            sp.dma_start(dprev[1:P, 0:1], dst_i[0:P - 1, COLS - 1:COLS]).then_inc(prev_in, 16)
            sp.dma_start(dnext[0:P - 1, COLS - 1:COLS], dst_i[1:P, 0:1]).then_inc(next_in, 16)
            for t in sums.values():
                sp.dma_start(t[ZERO_ROW:TROWS, :], zrow[0:ZROWS, :]).then_inc(zero_rows, 16)
                sp.dma_start(t[CARRY_ROWS:CARRY_ROWS + P, :], zrow[:, :]).then_inc(zero_rows, 16)
            for r in range(ADDS):
                clear(r)

            sp.wait_ge(added, ADDS)
            sp.wait_ge(pos_ready, 1)
            xv, tv = x.rearrange("(p n) f -> p n f", p=NP_), node_tab[:, :].rearrange("(p n) f -> p n f", p=NP_)
            av = by_node[ADDS - 1][0:N, :].rearrange("(p n) f -> p (n f)", p=NP_)
            pv = pos_tab[:, :].rearrange("(p n) f -> p (n f)", p=NP_)
            with sp.Fori(0, NPP // NB // 2) as i:
                for s in range(2):
                    n = bass.ds(i * 2 * NB + s * NB, NB)
                    sp.wait_ge(nt_ready, i * 2 + (s + 1))
                    sp.dma_start(na[s][0:NP_, :], av[:, bass.ds(i * (2 * NB * AROW) + s * NB * AROW, NB * AROW)]).then_inc(nx_in[s], 16)
                    sp.dma_start(v3(nx[s][0:NP_, :], F), xv[:, n, :]).then_inc(nx_in[s], 16)
                    sp.dma_start(npt[s][0:NP_, :], pv[:, bass.ds(i * (4 * NB) + 2 * s * NB, 2 * NB)]).then_inc(nx_in[s], 16)

            ov = out.rearrange("(p n) f -> p n f", p=NP_)

            for r in range(R0, ROUNDS):
                loads, tb = LOADS.get(r, 0), td_base[r]
                if r == R0:
                    sp.wait_ge(node_ready, 1)
                    sp.wait_ge(g_free, NCH * R0 + 2)
                if r in D_SIDE:
                    sp.wait_ge(carry_done, 16 * (r - R0))
                with sp.Fori(0, PAIRS) as i:
                    for s in range(2):
                        if loads:
                            dv = sums[r - 1][0:EP, :].rearrange("(p t) f -> p (t f)", p=P)
                            ev = ea_pad[:, :].rearrange("(p t) f -> p (t f)", p=P)
                            at = bass.ds(i * (2 * CC * F) + s * CC * F, CC * F)
                            base = tb + s * loads
                            sp.wait_ge(td_free, i * 2 + (NCH * (r - R0 - 1) + s + 1))
                            sp.dma_start(td[s], dv[:, at]).then_inc(td_dma, 16)
                            if loads == 2:
                                sp.dma_start(eat[s], ev[:, at]).then_inc(td_dma, 16)
                            sp.wait_ge(td_dma, i * (32 * loads) + 16 * (base + loads))
                            sp.sem_inc(td_full, 1)
                        if r in ALL_NODES:
                            first_n = ALL_NODES[r]
                            k = min(r - R0, 1) * NCH + min(r - R0, 1) + s
                            nodes = bass.ds(i * (2 * CC) + (first_n + s) * CC, CC)
                            sp.dma_start(v3(dn[0:NP_, 0:W], F), tv[:, nodes, 0:F]).then_inc(dn_in, 16)
                        if r < ROUNDS - 1:
                            sp.wait_ge(tout_ready, i * 2 + (NCH * (r - R0) + s + 1))
                            sv = sums[r][0:EP, :].rearrange("(p t) f -> p (t f)", p=P)
                            sp.dma_start(sv[:, bass.ds(i * (2 * CC * F) + s * CC * F, CC * F)], tout[s]).then_inc(tout_dma, 16)
                            sp.wait_ge(tout_dma, i * 32 + 16 * (NCH * (r - R0) + s + 1))
                            sp.sem_inc(tout_free, 1)
                        if r in ALL_NODES:
                            sp.wait_ge(dn_done, i * 2 + (k + 1))
                            sp.dma_start(ov[:, nodes, :], v3(dn[0:NP_, 0:W], F)).then_inc(dn_out, 16)
                            sp.wait_ge(dn_out, i * 32 + 16 * (k + 1))
                            sp.nop(nofuse=True)
                if r == R0:
                    nodes = slice(NPP - DC_LAST, NPP)
                    sp.dma_start(v3(dn[0:NP_, 0:DC_LAST * F], F), tv[:, nodes, 0:F]).then_inc(dn_in, 16)
                    sp.wait_ge(dn_done, NCH + 1)
                    sp.dma_start(ov[:, nodes, :], v3(dn[0:NP_, 0:DC_LAST * F], F)).then_inc(dn_out, 16)
                    sp.wait_ge(dn_out, 16 * (NCH + 1))
            sp.wait_ge(out_dma, 16 * COLS)

        @block.gpsimd
        def _(pool):
            st = Steps(pool, pool_s)
            pool.iota(epos[:, :], [[1, COLS]], base=0, channel_multiplier=COLS, allow_small_or_imprecise_dtypes=True).then_inc(iotas, 1)
            st.done(pool.memset(ident[:, :], 0.0))
            pool.affine_select(out=ident[:, :], in_=ident[:, :], compare_op=ALU.not_equal, fill=1.0, base=0,
                               pattern=[[-1, P]], channel_multiplier=1).then_inc(consts, 1)
            pool.iota(ocol[:, :], [[0, 1]], base=CARRY_ROWS, channel_multiplier=1, allow_small_or_imprecise_dtypes=True).then_inc(iotas, 1)
            pool.iota(b4[:, :], [[0, TILES4], [1, 4]], base=0, channel_multiplier=0, allow_small_or_imprecise_dtypes=True).then_inc(iotas, 1)
            pool.iota(pcol[:, :], [[0, 1]], base=N, channel_multiplier=1, allow_small_or_imprecise_dtypes=True).then_inc(iotas, 1)
            ppv = pp.rearrange("p (a n f) -> p a n f", n=ZROWS, f=2)
            pool.iota(ppv[:, :, :, 0], [[0, NPP // ZROWS], [1, ZROWS]], base=ZERO_ROW, channel_multiplier=0,
                      allow_small_or_imprecise_dtypes=True).then_inc(pp_preset, 1)
            pool.memset(ppv[:, :, :, 1], 1.0).then_inc(pp_preset, 1)

            pool.wait_ge(flag_ready, 1)
            pool.wait_ge(ea_copied, 48)
            bad = pool.value_load(flag[0:1, 0:1], min_val=0, max_val=1)
            with pool.If(bad > 0):
                fb = Steps(pool, sort_in)
                db = xs[:, 0:SB].bitcast(I32)
                gi = xs[:, 2 * SB - SB:2 * SB].bitcast(I32)
                fb.done(pool.iota(gi, [[1, SB]], base=0, channel_multiplier=0))
                for k in range(E // SB):
                    if k:
                        pool.wait_ge(block_used, k)
                    pool.dma_start(db, dst[k * SB:(k + 1) * SB].rearrange("(a f) -> a f", a=1).to_broadcast([P, SB])).then_inc(sort_dma, 16)
                    pool.wait_ge(sort_dma, 16 * (k + 1))
                pool.wait_ge(ranks_ready, 1)
                rank, rec = xs[:, 0:COLS], xs[:, COLS:COLS + CC * 4]
                ear, ri = xs[:, 2 * COLS:2 * COLS + CC * F], idxst[0]
                rec3 = v3(rec, 4)
                fb.done(pool.memset(rec, 0.0))
                eav = ea_pad[:, :].rearrange("(p t) f -> p (t f)", p=P)
                fbase, dbase = fb.base, 16 * (E // SB)
                moved = 16 * (2 * CC + 1)
                with pool.Fori(0, NCH) as i:
                    fb.loop(i, 4)
                    cols = bass.ds(i * CC, CC)
                    pool.dma_start(ear, eav[:, bass.ds(i * (CC * F), CC * F)]).then_inc(sort_dma, 16)
                    fb.done(pool.tensor_copy(ri[:, :], rank[:, cols]))
                    fb.done(pool.tensor_copy(rec3[:, :, 0].bitcast(I32), src_i[:, cols]))
                    fb.done(pool.tensor_copy(rec3[:, :, 1].bitcast(I32), dst_i[:, cols]))
                    fb.done(pool.tensor_copy(rec3[:, :, 2], wt[:, cols]))
                    pool.wait_ge(sort_dma, i * moved + (dbase + 16))
                    pool.nop(nofuse=True)
                    for k in range(CC):
                        at = bass.IndirectOffsetOnAxis(ri[:, k:k + 1], 0)
                        pool.indirect_dma_start(ea_perm[:, :], at, ear[:, k * F:(k + 1) * F], None).then_inc(sort_dma, 16)
                        pool.indirect_dma_start(rec_perm[:, :], at, rec[:, 4 * k:4 * k + 4].bitcast(I32), None).then_inc(sort_dma, 16)
                    pool.wait_ge(sort_dma, i * moved + (dbase + moved))
                    pool.nop(nofuse=True)
                fb.end(NCH, "sort")
                total = dbase + moved * NCH
                pool.dma_start(ea_pad[:, :], ea_perm[:, :]).then_inc(sort_dma, 16)
                pool.dma_start(xd[:, 0:4 * COLS].bitcast(I32), rec_perm[:, :].rearrange("(p t) f -> p (t f)", p=P)).then_inc(sort_dma, 16)
                pool.wait_ge(sort_dma, total + 32)
                got = v3(xd[:, 0:4 * COLS], 4)
                fb.done(pool.tensor_copy(src_i[:, :], got[:, :, 0].bitcast(I32)))
                fb.done(pool.tensor_copy(dst_i[:, :], got[:, :, 1].bitcast(I32)))
                fb.done(pool.tensor_copy(wt[:, :], got[:, :, 2]))
            pool.drain().then_inc(sorted_ready, 1)

            st.done(pool.memset(low, 1.0))
            pool.affine_select(out=v3(low, P), in_=v3(low, P), compare_op=ALU.is_gt, fill=0.0, base=0,
                               pattern=[[0, 4], [-1, P]], channel_multiplier=1).then_inc(low_ready, 1)

            pool.wait_ge(meta_ready, 1)
            pool.wait_ge(pos_init, 16)
            with pool.Fori(0, PAIRS) as i:
                st.loop(i, 6)
                for s in range(2):
                    cols = bass.ds(i * 2 * CC + s * CC, CC)
                    gv = v3(g[s][:, 0:2 * CC], 2)
                    st.done(pool.tensor_copy(aidxst[s][:, :], sidx[:, cols]))
                    st.done(pool.tensor_copy(gv[:, :, 0], epos[:, cols]))
                    st.done(pool.tensor_copy(gv[:, :, 1], ic_d[:, cols]))
                pool.nop(nofuse=True)
                for s in range(2):
                    for k in range(CC):
                        pool.indirect_dma_start(pos_tab[:, :], bass.IndirectOffsetOnAxis(aidxst[s][:, k:k + 1], 0),
                                                g[s][:, 2 * k:2 * k + 2], None,
                                                bounds_check=N - 1, oob_is_err=False).then_inc(pos_dma, 16)
                pool.wait_ge(pos_dma, i * (32 * CC) + 32 * CC)
                pool.nop(nofuse=True)
            st.end(PAIRS, "positions")
            pool.drain().then_inc(pos_ready, 1)

            def gather(r, s, i, c):
                tab, width, pitch = ((x[:, :], F, AROW) if r == 0 else (by_node[r - 1], AROW, AROW) if r <= TO_DST
                                     else (node_tab[:, :], ROW, ROW) if r == R0 else (sums[r - 1][:, :], F, ROW))
                n = NCH * r + c
                pool.wait_ge(idx_staged, i * 2 + (n + 1))
                pool.wait_ge(g_free, i * 2 + (n + 1))
                pool.nop(nofuse=True)
                for k in range(CC):
                    pool.indirect_dma_start(g[s][:, k * pitch:k * pitch + width], None, tab,
                                            bass.IndirectOffsetOnAxis(idxst[s][:, k:k + 1], 0)).then_inc(g_full[s], 16)

            def settle(r, i, c):
                for b in range(BLK):
                    pool.wait_ge(adds_done[b], i * (32 * TILES4) + 16 * TILES4 * (NCH * r + c + 1))
                pool.nop(nofuse=True)
                pool.sem_inc(arow_free, 1)

            def add(r, s, i, c):
                n = NCH * r + c
                pool.wait_ge(aidx_staged, i * 2 + (n + 1))
                pool.wait_ge(arow_ready, i * 2 + (n + 2))
                pool.nop(nofuse=True)
                for k in range(CC):
                    b = k % BLK
                    if k >= BLK:
                        pool.wait_ge(adds_done[b], i * (32 * TILES4) + 16 * (TILES4 * n + k // BLK))
                        pool.nop(nofuse=True)
                    pool.indirect_dma_start(adds[r][:, :], bass.IndirectOffsetOnAxis(aidxst[s][:, k:k + 1], 0),
                                            arow[s][:, k * F:(k + 1) * F], None, bounds_check=AROWS * BLK - 1,
                                            oob_is_err=True, compute_op=ALU.add).then_inc(adds_done[b], 16)

            for r in range(ADDS):
                gather(r, 0, 0, 0)
                pool.wait_ge(adds_clear[r], 16 * 16)
                with pool.Fori(0, PAIRS - 1) as i:
                    gather(r, 1, i, 1)
                    add(r, 0, i, 0)
                    gather(r, 0, i, 2)
                    settle(r, i, 0)
                    add(r, 1, i, 1)
                    settle(r, i, 1)
                gather(r, 1, 0, NCH - 1)
                add(r, 0, 0, NCH - 2)
                settle(r, 0, NCH - 2)
                add(r, 1, 0, NCH - 1)
                settle(r, 0, NCH - 1)
                pool.sem_inc(added, 1)

            for r in range(TO_DST, ROUNDS):
                if r == R0:
                    pool.wait_ge(nt_out, 16 * (NPP // NB))
                    pool.sem_inc(node_ready, 1)
                with pool.Fori(0, PAIRS) as i:
                    for s in range(2):
                        gather(r, s, i, s)
                if R0 <= r < ROUNDS - 1:
                    if r == R0:
                        pool.wait_ge(zero_rows, 32 * len(sums))
                    pool.wait_ge(carry_ready, r - R0 + 1)
                    pool.wait_ge(tout_dma, 16 * NCH * (r - R0 + 1))
                    pool.indirect_dma_start(sums[r][:, :], bass.IndirectOffsetOnAxis(cidx[:, :], 0),
                                            carry[:, :], None, bounds_check=TROWS - 1, oob_is_err=True,
                                            compute_op=ALU.add).then_inc(carry_done, 16)
                    pool.wait_ge(carry_done, 16 * (r - R0 + 1))

            pool.wait_ge(dn_out, 16 * (2 * NCH + 1))
            pool.wait_ge(idx_staged, NCH * ROUNDS + 2)
            for s in range(2):
                pool.wait_ge(g_full[s], 16 * CC * PAIRS * ROUNDS)
            with pool.Fori(0, PAIRS) as i:
                st.loop(i, 2)
                for s in range(2):
                    st.done(pool.tensor_copy(idxst[s][:, :], sidx[:, bass.ds(i * 2 * CC + s * CC, CC)]))
                for s in range(2):
                    pool.wait_ge(rows_ready, i * 2 + (s + 1))
                    pool.nop(nofuse=True)
                    for k in range(CC):
                        pool.indirect_dma_start(out[:, :], bass.IndirectOffsetOnAxis(idxst[s][:, k:k + 1], 0),
                                                g[s][:, k * ROW:k * ROW + F], None,
                                                bounds_check=N - 1, oob_is_err=False).then_inc(out_dma, 16)
                pool.wait_ge(out_dma, i * (32 * CC) + 32 * CC)
                pool.nop(nofuse=True)
                pool.drain().then_inc(rows_free, 1)
            st.end(PAIRS, "out rows")
            pool.wait_ge(out_dma, 16 * COLS)

        @block.scalar
        def _(act):
            def root(base, i, per, j, parts, cols):
                act.wait_ge(var_ready, i * per + (base + j + 1))
                nc.scalar.activation(sd[0:parts, 0:cols], var[0:parts, 0:cols], ACT.Sqrt,
                                     bias=lneps[0:parts, :], scale=1.0 / F).then_inc(sd_ready, 1)

            def sage(base, i, per, j, parts, cols):
                for q, n in enumerate(BATCHES[cols]):
                    k = QE * (base + j) + q + 1
                    act.wait_ge(tp_ready, i * (QE * per) + k)
                    nc.scalar.activation(aht[:, 0:n * P], tp[:, 0:n * P], ACT.Copy).then_inc(aht_ready, 1)
                    act.wait_ge(m1_ready, i * (QE * per) + k)
                    nc.scalar.activation(h1t[:, 0:n * P], m1[:, 0:n * P], ACT.Relu, bias=b1b[:, :]).then_inc(h1t_ready, 1)

            act.wait_ge(consts, 3)
            act.wait_ge(weights_in, 16 * 12)
            for r in range(ADDS):
                with act.Fori(0, PAIRS) as i:
                    for s in range(2):
                        n = NCH * r + s
                        if r == 0:
                            root(0, i, 2, s, P, CC)
                        act.wait_ge(merged, i * 2 + (n + 1))
                        act.wait_ge(arow_free, i * 2 + (n + 1))
                        nc.scalar.activation(arow[s], m2[:, 0:CC * F], ACT.Copy).then_inc(arow_ready, 1)
            act.sem_inc(nt_ready, 2)
            with act.Fori(0, NPP // NB // 2) as i:
                for s in range(2):
                    act.wait_ge(nsum_ready, i * 2 + (s + 1))
                    ntv = v3(nt[s][0:NP_, :], ROW)
                    nc.scalar.activation(ntv[:, :, 0:F], v3(m2[0:NP_, 0:NB * F], F), ACT.Copy).then_inc(nsum_used, 1)
                    nc.scalar.activation(ntv[:, :, F:F + 2], v3(npt[s][0:NP_, :], 2), ACT.Copy).then_inc(nt_ready, 1)
                    act.wait_ge(nt_ready, i * 2 + (s + 3))
                    act.wait_ge(nsum_used, i * 2 + (s + 2))
                    act.dma_start(node_tab[:, :].rearrange("(p n) f -> p (n f)", p=NP_)[:, bass.ds(i * (2 * NB * ROW) + s * NB * ROW, NB * ROW)],
                                  nt[s][0:NP_, :]).then_inc(nt_out, 16)
                    act.wait_ge(nt_out, i * 32 + 16 * (s + 1))
                    act.nop(nofuse=True)
            for r in range(R0, ROUNDS):
                ln, mm = LN[r], MM.get(r, "")
                with act.Fori(0, PAIRS) as i:
                    for s in range(2):
                        nc.scalar.activation(km[s].rearrange("p (f t) -> p f t", t=CC),
                                             keepz[:, bass.ds(i * 2 * CC + s * CC, CC)].unsqueeze(1).to_broadcast([P, F, CC]),
                                             ACT.Copy).then_inc(km_ready, 1)
                    for s in range(2):
                        n = NCH * (r - R0) + s

                        def side(which):
                            parts = NP_ if which == "N" else P
                            js = [j for j, x_ in enumerate(ln) if x_ == which]
                            if js:
                                root(ln_base[r], i, 2 * len(ln), len(ln) * s + js[0], parts, CC)
                            if which in mm:
                                sage(mm_base[r], i, 2 * len(mm), len(mm) * s + mm.index(which), parts, CC)
                            for j in js[1:]:
                                root(ln_base[r], i, 2 * len(ln), len(ln) * s + j, parts, CC)

                        side("S")
                        act.wait_ge(scan_done, i * 2 + (n + 1))
                        if r < ROUNDS - 1:
                            act.wait_ge(tout_free, i * 2 + (n + 1))
                            nc.scalar.activation(v3(tout[s], F), sc[s].rearrange("p (f t) -> p t f", t=CC),
                                                 ACT.Copy).then_inc(tout_ready, 1)
                        side("D")
                        side("N")
                if r == R0:
                    root(ln_base["last"], 0, 0, 0, NP_, DC_LAST)
                    sage(mm_base["last"], 0, 0, 0, NP_, DC_LAST)
                    root(ln_base["last"], 0, 0, 1, NP_, DC_LAST)

        @block.tensor
        def _(pe):
            pe.wait_ge(bad_ready, 1)
            nc.tensor.matmul(cp[0:1, 0:1], small[:, 0:1], ones[:, 0:1], start=True, stop=True).then_inc(bad_sum, 1)

            def sage(base, i, per, j, cols):
                pe.wait_ge(ah_ready, i * per + (base + j + 1))
                col = 0
                for q, n in enumerate(BATCHES[cols]):
                    k = QE * (base + j) + q + 1
                    for u in range(n):
                        ins = nc.tensor.transpose(tp[:, u * P:(u + 1) * P], ah[:, (col + u) * P:(col + u + 1) * P], ident[:, :])
                    ins.then_inc(tp_ready, 1)
                    pe.wait_ge(aht_ready, i * (QE * per) + k)
                    nc.tensor.matmul(m1[:, 0:n * P], w1b[:, :], aht[:, 0:n * P], start=True, stop=True).then_inc(m1_ready, 1)
                    pe.wait_ge(h1t_ready, i * (QE * per) + k)
                    if q == 0:
                        pe.wait_ge(m2_free, i * per + (base + j + 1))
                    for u in range(n):
                        ins = nc.tensor.matmul(m2[:, (col + u) * P:(col + u + 1) * P], h1t[:, u * P:(u + 1) * P], w2b[:, :],
                                               start=True, stop=True)
                    col += n
                ins.then_inc(m2_ready, 1)

            pe.wait_ge(consts, 3)
            pe.wait_ge(cl_ready, 1)
            nc.tensor.transpose(cp[0:F, 128:256], pm_b[:, :], ident[:, :]).then_inc(clt_ready, 1)
            nc.tensor.transpose(cp[0:F, 0:P], state[:, :], ident[:, :]).then_inc(clt_ready, 1)
            pe.wait_ge(ct_ready, 1)
            nc.tensor.transpose(cp[:, 256:256 + F], carry_t[:, 0:P], ident[0:F, 0:F]).then_inc(cc_ready, 1)
            for r in range(ADDS):
                with pe.Fori(0, PAIRS) as i:
                    for s in range(2):
                        n = NCH * r + s
                        pe.wait_ge(srcst_ready, i * 2 + (n + 1))
                        for q in range(TILES4):
                            pe.wait_ge(sel_ready, i * (2 * TILES4) + (TILES4 * n + q + 1))
                            for u in range(4):
                                ins = nc.tensor.transpose(dup[(s + q) % 2][:, u * P:(u + 1) * P],
                                                          srcst[:, 4 * q + u:4 * q + u + 1].to_broadcast([P, P]), ident[:, :])
                            ins.then_inc(dup_ready, 1)
                        pe.wait_ge(amsg_ready, i * 2 + (n + 1))
                        pe.wait_ge(arow_ready, i * 2 + (n + 1))
                        for k in range(CC):
                            ins = nc.tensor.matmul(m2[:, k * F:(k + 1) * F], sel[:, k * P:(k + 1) * P], amsg[:, k * F:(k + 1) * F],
                                                   start=True, stop=True)
                        ins.then_inc(merged, 1)
            pe.wait_ge(arow_ready, NCH * ADDS + 1)
            with pe.Fori(0, NPP // NB // 2) as i:
                for s in range(2):
                    pe.wait_ge(nx_in[s], i * 48 + 48)
                    pe.wait_ge(nsum_used, i * 2 + (s + 1))
                    for o in range(0, NB, 16):
                        n = min(16, NB - o)
                        for b in range(BLK + 1):
                            rhs = (v3(nx[s][0:NP_, :], F)[:, o:o + n, :] if b == BLK else
                                   v3(na[s][0:NP_, :], AROW)[:, o:o + n, b * F:(b + 1) * F])
                            ins = nc.tensor.matmul(m2[0:NP_, o * F:(o + n) * F], ident[0:NP_, 0:NP_], rhs, start=b == 0, stop=b == BLK)
                    ins.then_inc(nsum_ready, 1)
            pe.wait_ge(weights_in, 16 * 12)
            for r in range(R0, ROUNDS):
                if r in MM:
                    with pe.Fori(0, PAIRS) as i:
                        for s in range(2):
                            for j in range(len(MM[r])):
                                sage(mm_base[r], i, 2 * len(MM[r]), len(MM[r]) * s + j, CC)
                if r == R0:
                    sage(mm_base["last"], 0, 0, 0, DC_LAST)
                pe.wait_ge(cl_ready, r - R0 + 2)
                nc.tensor.transpose(cp[0:F, 0:P], state[:, :], ident[:, :]).then_inc(clt_ready, 1)
                pe.wait_ge(ct_ready, r - R0 + 2)
                nc.tensor.transpose(cp[:, 256:256 + F], carry_t[:, 0:P], ident[0:F, 0:F]).then_inc(cc_ready, 1)

        @block.vector
        def _(dve):
            V = nc.vector
            st = Steps(dve, dve_s)
            done = st.done
            V.memset(src_i[:, :], 0).then_inc(edges_0, 1)
            V.memset(dst_i[:, :], N).then_inc(edges_0, 1)
            V.memset(wt[:, :], 0.0).then_inc(edges_0, 1)
            V.memset(zeros, 0.0).then_inc(zeros_in, 1)
            V.memset(zrow[:, :], 0.0).then_inc(zeros_in, 1)
            done(V.memset(w1b[:, :], 0.0))
            done(V.memset(w2b[:, :], 0.0))
            V.memset(ah[:, :], 0.0).then_inc(weights_0, 1)
            V.memset(lneps[:, :], LN_EPS).then_inc(consts, 1)
            done(V.memset(carry_t[:, :], 0.0))
            V.memset(state[:, :], 0.0).then_inc(consts, 1)
            dve.sem_inc(g_free, 2)
            dve.sem_inc(sel_ready, 2)
            dve.sem_inc(arow_ready, 1)
            dve.sem_inc(arow_free, 2)
            dve.sem_inc(nsum_used, 1)
            dve.sem_inc(m2_free, 1)
            dve.sem_inc(tout_free, 2)
            dve.sem_inc(td_free, 2)
            done(V.memset(ones, 1.0))
            done(V.memset(dprev[:, :], -1))
            done(V.memset(dnext[:, :], -1))
            dve.wait_ge(edges_in, 16 * 6)

            def neighbours(k):
                done(V.tensor_copy(dprev[:, 1:COLS], dst_i[:, 0:COLS - 1]))
                if k:
                    done(V.tensor_copy(dnext[:, 0:COLS - 1], dst_i[:, 1:COLS]))
                dve.sem_inc(dst_ready, 1)
                dve.wait_ge(prev_in, 16 * (k + 1))
                if k:
                    dve.wait_ge(next_in, 16)

            neighbours(0)
            done(V.tensor_tensor(keep[:, :], dprev[:, :], dst_i[:, :], ALU.is_gt))
            V.tensor_reduce(small[:, 0:1], keep[:, :], axis=AX.X, op=ALU.add).then_inc(bad_ready, 1)
            dve.wait_ge(bad_sum, 1)
            done(V.tensor_scalar(small[0:1, 1:2], cp[0:1, 0:1], 0.5, None, ALU.is_gt))
            V.tensor_copy(flag[:, :], small[0:1, 1:2]).then_inc(flag_ready, 1)
            dve.wait_ge(flag_ready, 1)
            dve.wait_ge(iotas, 4)

            bad = dve.value_load(flag[0:1, 0:1], min_val=0, max_val=1)
            with dve.If(bad > 0):
                fb = Steps(dve, rank_steps)
                db = xs[:, 0:SB].bitcast(I32)
                gi = xs[:, SB:2 * SB].bitcast(I32)
                gf, cmpd = xd[:, 0:SB], xd[:, SB:2 * SB]
                dstf, thr, acc, rk = keep, keepz, last, cnt
                dve.wait_ge(sort_in, 1)
                fb.done(V.tensor_scalar(gf, gi, 2.0 ** -16, None, ALU.mult))
                fb.done(V.tensor_copy(dstf[:, :], dst_i[:, :]))
                fb.done(V.tensor_scalar(acc, epos[:, :], float(E), None, ALU.subtract))
                fb.done(V.scalar_tensor_tensor(rk, dstf[:, :], float(N), acc, ALU.is_equal, ALU.mult))
                for k in range(E // SB):
                    fb.done(V.tensor_scalar(thr[:, :], epos[:, :], float(-k * SB), 2.0 ** -16, ALU.add, ALU.mult))
                    dve.wait_ge(sort_dma, 16 * (k + 1))
                    with dve.Fori(0, COLS) as t:
                        fb.loop(t, 2)
                        one = bass.ds(t, 1)
                        fb.done(V.scalar_tensor_tensor(cmpd, db, dstf[:, one], gf, ALU.subtract, ALU.add))
                        fb.done(V.tensor_scalar(cmpd, cmpd, thr[:, one], None, ALU.is_lt, ALU.add, accum_out=acc[:, one]))
                    fb.end(COLS, "rank")
                    fb.done(V.tensor_tensor(rk, rk, acc, ALU.add))
                    dve.sem_inc(block_used, 1)
                V.tensor_copy(xs[:, 0:COLS], rk).then_inc(ranks_ready, 1)
                dve.wait_ge(ranks_ready, 1)
            dve.wait_ge(sorted_ready, 1)

            neighbours(1)
            done(V.tensor_tensor(keep[:, :], dprev[:, :], dst_i[:, :], ALU.is_equal))
            done(V.tensor_copy(keepz[:, :], keep[:, :]))
            done(V.memset(v3(keepz[:, :], CC)[:, :, 0], 0.0))
            done(V.tensor_tensor(last, dnext[:, :], dst_i[:, :], ALU.not_equal))
            done(V.tensor_tensor_scan(pm[:, :], keep[:, :], keep[:, :], 1.0, ALU.mult, ALU.mult))
            done(V.tensor_tensor_scan(cnt, keep[:, :], ones, 0.0, ALU.mult, ALU.add))
            done(V.tensor_copy(pm_b[:, :], pm[:, COLS - 1:COLS].to_broadcast([P, F])))
            V.tensor_copy(state[:, 0:1], cnt[:, COLS - 1:COLS]).then_inc(cl_ready, 1)

            def carries(n):
                dve.wait_ge(clt_ready, n + 2)
                if n == 0:
                    done(V.tensor_copy(pm_t[:, :], cp[0:F, 128:256]))
                done(V.tensor_copy(last_t[:, :], cp[0:F, 0:P]))
                V.tensor_tensor_scan(carry_t[:, 1:P + 1], pm_t[:, :], last_t[:, :], 0.0, ALU.mult, ALU.add).then_inc(ct_ready, 1)
                dve.wait_ge(cc_ready, n + 1)
                if n > 1:
                    dve.wait_ge(carry_done, 16 * (n - 1))
                done(V.tensor_copy(carry[:, :], cp[:, 256:256 + F]))

            carries(0)
            done(V.scalar_tensor_tensor(cnt, pm[:, :], carry[:, 0:1], cnt, ALU.mult, ALU.add))
            done(V.reciprocal(ic_d[:, :], cnt))
            done(V.tensor_reduce(small[:, 2:3], pm[:, :], axis=AX.X, op=ALU.add))
            done(V.tensor_scalar(small[:, 3:4], last[:, COLS - 1:COLS], -1.0, 1.0, ALU.mult, ALU.add))
            done(V.scalar_tensor_tensor(small[:, 4:5], small[:, 2:3], float(COLS), small[:, 3:4], ALU.is_equal, ALU.mult))
            done(V.tensor_scalar(small[:, 4:5], small[:, 4:5], -1.0, 1.0, ALU.mult, ALU.add))
            done(V.scalar_tensor_tensor(small[:, 4:5], small[:, 2:3], 0.5, small[:, 4:5], ALU.is_gt, ALU.mult))
            done(V.scalar_tensor_tensor(small[:, 5:6], epos[:, 0:1], -1.0, small[:, 2:3], ALU.add, ALU.add))
            done(V.tensor_tensor(small[:, 5:6], small[:, 5:6], ocol[:, :], ALU.subtract))
            done(V.scalar_tensor_tensor(cidx_f[:, :], small[:, 5:6], small[:, 4:5], ocol[:, :], ALU.mult, ALU.add))
            done(V.tensor_copy(cidx[:, :], cidx_f[:, :]))
            done(V.tensor_scalar(sidx[:, :], last, -NOWHERE, NOWHERE, ALU.mult, ALU.add))
            done(V.tensor_tensor(sidx[:, :], sidx[:, :], dst_i[:, :], ALU.add))
            done(V.tensor_scalar(gidx[:, 0:COLS], dst_i[:, :], float(N - 1), None, ALU.min))
            done(V.tensor_copy(gdst[:, 0:COLS], gidx[:, 0:COLS]))
            done(V.tensor_copy(gdst[:, COLS:], gidx[:, 0:2 * CC]))
            done(V.tensor_copy(gidx[:, COLS:2 * COLS], src_i[:, :]))
            for s in range(2):
                V.tensor_copy(idxst[s][:, :], gdst[:, s * CC:(s + 1) * CC]).then_inc(idx_staged, 1)
            dve.wait_ge(weights_in, 16 * 12)
            done(V.tensor_scalar(eps1[:, :], eps1[:, :], 1.0, None, ALU.add))
            dve.sem_inc(meta_ready, 1)

            def layernorm(xv, base, i, per, j, parts, cols):
                dve.nop(nofuse=True)
                xc3, sq3 = v3(xc[0:parts, 0:cols * F], F), v3(sq[0:parts, 0:cols * F], F)
                c = slice(0, cols)
                done(V.tensor_reduce(s1[0:parts, c], xv, axis=AX.X, op=ALU.add))
                done(V.tensor_scalar(mean[0:parts, c], s1[0:parts, c], 1.0 / F, None, ALU.mult))
                done(V.tensor_tensor(xc3, xv, bc(mean[0:parts, c], F, parts), ALU.subtract))
                done(V.tensor_tensor(sq3, xc3, xc3, ALU.mult))
                V.tensor_reduce(var[0:parts, c], sq3, axis=AX.X, op=ALU.add).then_inc(var_ready, 1)
                dve.wait_ge(sd_ready, i * per + (base + j + 1))
                done(V.reciprocal(rs[0:parts, c], sd[0:parts, c]))
                done(V.tensor_tensor(sq3, xc3, bc(rs[0:parts, c], F, parts), ALU.mult))
                return sq3

            def m2_out(half, parts, cols):
                return m2[0:parts, 0:cols * 2 * F].rearrange("p (t f) -> p t f", f=2 * F)[:, :, half * F:(half + 1) * F]

            def b2_cols(parts, cols):
                return b2b[0:parts, :].unsqueeze(1).to_broadcast([parts, cols, F])

            def sage_in(xn, agg, parts, cols):
                ahv = v3(ah[0:parts, 0:cols * 2 * F], 2 * F)
                if agg is not None:
                    done(agg(ahv[:, :, 0:F]))
                V.tensor_scalar(ahv[:, :, F:2 * F], xn, 0.0, None, ALU.max).then_inc(ah_ready, 1)

            def sage_root(xv, parts, cols):
                t3 = v3(xc[0:parts, 0:cols * F], F)
                done(V.tensor_tensor(t3, m2_out(1, parts, cols), b2_cols(parts, cols), ALU.add))
                done(V.tensor_tensor(xv, xv, t3, ALU.add))

            def all_nodes(i, ln_at, mm_at, cols, k):
                dn3 = v3(dn[0:NP_, 0:cols * F], F)
                dve.wait_ge(dn_in, i * 32 + 16 * (k + 1))
                xn = layernorm(dn3, *ln_at(0), NP_, cols)
                sage_in(xn, None, NP_, cols)
                dve.wait_ge(m2_ready, mm_at[0] * i + mm_at[1])
                sage_root(dn3, NP_, cols)
                dve.sem_inc(m2_free, 1)
                xn = layernorm(dn3, *ln_at(1), NP_, cols)
                done(V.tensor_scalar(xn, xn, 0.0, eps1[0:NP_, :], ALU.max, ALU.mult))
                done(V.tensor_tensor(dn3, dn3, xn, ALU.add))
                dve.sem_inc(dn_done, 1)

            def copy(o, i_):
                return V.tensor_scalar(o, i_, 1.0, None, ALU.mult)

            per = {0: 27, 1: 2, 2: 2, 3: 2, 4: 29, 5: 22, 6: 25, 7: 29}
            srcf = gidx[:, COLS:2 * COLS]
            for r in range(ADDS):
                with dve.Fori(0, PAIRS) as i:
                    st.loop(i, 2 * per[r])
                    for s in range(2):
                        n = NCH * r + s
                        off = lambda wdt, o=0: bass.ds(i * (2 * CC * wdt) + (s * CC * wdt + o), CC * wdt)
                        D, wb = v3(xd[:, off(F)], F), bc(wt[:, off(1)], F)
                        gv, am, xc3 = v3(g[s][:, :], AROW), v3(amsg, F), v3(xc[:, :], F)
                        dve.wait_ge(g_full[s], i * (16 * CC) + 16 * CC * (PAIRS * r + 1))
                        copy(idxst[s][:, :], gdst[:, off(1, 2 * CC)]).then_inc(idx_staged, 1)
                        copy(srcst[:, :], srcf[:, off(1)]).then_inc(srcst_ready, 1)
                        if r == 0:
                            done(copy(D, gv[:, :, 0:F]))
                            dve.sem_inc(g_free, 1)
                            xn = layernorm(D, 0, i, 2, s, P, CC)
                            dve.wait_ge(arow_ready, i * 2 + (n + 1))
                            done(V.scalar_tensor_tensor(am, xn, 0.0, wb, ALU.max, ALU.mult))
                        else:
                            done(V.tensor_reduce(xc3, gv.rearrange("p t (b f) -> p t f b", f=F), axis=AX.X, op=ALU.add))
                            dve.sem_inc(g_free, 1)
                            dve.wait_ge(arow_ready, i * 2 + (n + 1))
                            done(V.tensor_tensor(am, xc3, wb, ALU.mult))
                        for q in range(TILES4):
                            batch = TILES4 * n + q
                            dve.wait_ge(dup_ready, i * (2 * TILES4) + (batch + 1))
                            V.tensor_tensor(v3(sel[:, 4 * q * P:4 * (q + 1) * P], P), v3(dup[(s + q) % 2][:, :], P),
                                            bc(srcst[:, 4 * q:4 * q + 4], P), ALU.is_equal).then_inc(sel_ready, 1)
                            dve.wait_ge(sel_ready, i * (2 * TILES4) + (batch + 3))
                            if r == 0:
                                done(V.tensor_tensor(lowsel, sel[:, 4 * q * P:4 * (q + 1) * P], low, ALU.mult))
                                done(V.tensor_reduce(rep[:, 4 * q:4 * q + 4], v3(lowsel, P), axis=AX.X, op=ALU.add))
                        if r == 0:
                            done(V.tensor_scalar(s1[:, :], srcst[:, :], pcol[:, :], None, ALU.subtract))
                            done(V.scalar_tensor_tensor(s1[:, :], rep[:, :], 0.0, s1[:, :], ALU.is_equal, ALU.mult))
                            done(V.tensor_scalar(s1[:, :], s1[:, :], pcol[:, :], None, ALU.add))
                            done(V.tensor_scalar(s1[:, :], s1[:, :], float(BLK), None, ALU.mult))
                            done(V.tensor_tensor(aidx[:, off(1)], s1[:, :], b4[:, :], ALU.add))
                        dve.sem_inc(amsg_ready, 1)
                        dve.wait_ge(arow_free, i * 2 + (n + 1))
                        copy(aidxst[s][:, :], aidx[:, off(1)]).then_inc(aidx_staged, 1)
                st.end(PAIRS, f"round {r}")

            with dve.Fori(0, PAIRS) as i:
                st.loop(i, 2 * per[TO_DST])
                for s in range(2):
                    off = lambda wdt, o=0: bass.ds(i * (2 * CC * wdt) + (s * CC * wdt + o), CC * wdt)
                    D, xc3 = v3(xd[:, off(F)], F), v3(xc[:, :], F)
                    dve.wait_ge(g_full[s], i * (16 * CC) + 16 * CC * (PAIRS * TO_DST + 1))
                    copy(idxst[s][:, :], gidx[:, off(1, 2 * CC)]).then_inc(idx_staged, 1)
                    done(V.tensor_reduce(xc3, g[s][:, :].rearrange("p (t b f) -> p t f b", f=F, b=BLK), axis=AX.X, op=ALU.add))
                    dve.sem_inc(g_free, 1)
                    done(V.tensor_tensor(D, D, xc3, ALU.add))
            st.end(PAIRS, f"round {TO_DST}")

            msg_tf = msg.rearrange("p (f t) -> p t f", t=CC)
            msg_ft = msg.rearrange("p (f t) -> p f t", t=CC)
            for r in range(R0, ROUNDS):
                ln, mm = LN[r], MM.get(r, "")
                done(V.memset(state[:, :], 0.0))
                if r == R0 + 3:
                    done(V.memset(ah[:, :], 0.0))
                with dve.Fori(0, PAIRS) as i:
                    st.loop(i, 2 * per[r])
                    for s in range(2):
                        n = NCH * (r - R0) + s
                        off = lambda wdt, o=0: bass.ds(i * (2 * CC * wdt) + (s * CC * wdt + o), CC * wdt)
                        cols = off(1)
                        gx = v3(g[s][:, 0:CC * ROW], ROW)
                        gv = gx[:, :, 0:F]
                        X, D, xc3 = v3(xs[:, off(F)], F), v3(xd[:, off(F)], F), v3(xc[:, :], F)
                        wb = bc(wt[:, cols], F)

                        def ln_at(which, k=0):
                            j = [j for j, x_ in enumerate(ln) if x_ == which][k]
                            return ln_base[r], i, 2 * len(ln), len(ln) * s + j

                        def mm_at(which):
                            return i * (2 * len(mm)) + (mm_base[r] + len(mm) * s + mm.index(which) + 1)

                        dve.wait_ge(g_full[s], i * (16 * CC) + 16 * CC * (PAIRS * r + 1))
                        copy(idxst[s][:, :], gidx[:, off(1, (COLS if r == R0 else 2 * COLS) + 2 * CC)]).then_inc(idx_staged, 1)
                        if r == R0:
                            done(copy(X, gv))
                            done(copy(ic_s[:, cols], gx[:, :, F + 1]))
                            done(copy(gidx[:, off(1, 2 * COLS)], gx[:, :, F]))
                        elif r == R0 + 2:
                            done(V.tensor_tensor(xc3, gv, bc(ic_s[:, cols], F), ALU.mult))
                            done(V.tensor_tensor(X, X, xc3, ALU.add))
                        elif r == R0 + 3:
                            done(V.tensor_tensor(X, X, gv, ALU.add))
                        if r != R0 + 1:
                            dve.sem_inc(g_free, 1)
                        xn = layernorm(X, *ln_at("S"), P, CC)
                        if r == R0:
                            done(V.tensor_scalar(msg_tf, xn, 0.0, None, ALU.max))
                        elif r == R0 + 1:
                            sage_in(xn, lambda o: V.tensor_tensor(o, gv, bc(ic_s[:, cols], F), ALU.mult), P, CC)
                            dve.sem_inc(g_free, 1)
                            dve.wait_ge(m2_ready, mm_at("S"))
                            done(copy(msg_tf, m2_out(0, P, CC)))
                            sage_root(X, P, CC)
                            dve.sem_inc(m2_free, 1)
                        elif r == R0 + 2:
                            dve.wait_ge(td_full, i * 2 + (NCH * (r - R0 - 1) + s + 1))
                            done(V.scalar_tensor_tensor(xc3, xn, 0.0, v3(eat[s], F), ALU.max, ALU.add))
                            done(V.tensor_scalar(msg_tf, xc3, 0.0, None, ALU.max))
                            done(V.tensor_scalar(xn, xn, 0.0, eps1[:, :], ALU.max, ALU.mult))
                            done(V.tensor_tensor(X, X, xn, ALU.add))
                        else:
                            done(V.scalar_tensor_tensor(msg_tf, xn, 0.0, wb, ALU.max, ALU.mult))
                        done(V.scalar_tensor_tensor(msg_ft[:, :, 0], state[:, :], keep[:, bass.ds(i * 2 * CC + s * CC, 1)],
                                                    msg_ft[:, :, 0], ALU.mult, ALU.add))
                        dve.wait_ge(km_ready, i * 2 + (n + 1))
                        if r < ROUNDS - 1:
                            dve.wait_ge(tout_free, i * 2 + (n + 1))
                        done(V.tensor_tensor_scan(sc[s], km[s], msg, 0.0, ALU.mult, ALU.add))
                        done(V.tensor_copy(state[:, :], sc[s].rearrange("p (f t) -> p f t", t=CC)[:, :, CC - 1]))
                        if r == ROUNDS - 1:
                            done(V.tensor_tensor(D, D, sc[s].rearrange("p (f t) -> p t f", t=CC), ALU.add))
                        dve.sem_inc(scan_done, 1)
                        if r in D_SIDE:
                            tv = v3(td[s], F)
                            dve.wait_ge(td_full, i * 2 + (NCH * (r - R0 - 1) + s + 1))
                            if r == R0 + 3:
                                done(V.tensor_tensor(D, D, tv, ALU.add))
                            elif r == R0 + 1:
                                xn = layernorm(D, *ln_at("D"), P, CC)
                                sage_in(xn, lambda o: V.tensor_tensor(o, tv, bc(ic_d[:, cols], F), ALU.mult), P, CC)
                                dve.wait_ge(m2_ready, mm_at("D"))
                                sage_root(D, P, CC)
                                dve.sem_inc(m2_free, 1)
                            else:
                                done(V.tensor_tensor(tv, tv, bc(ic_d[:, cols], F), ALU.mult))
                                done(V.tensor_tensor(D, D, tv, ALU.add))
                                xn = layernorm(D, *ln_at("D"), P, CC)
                                done(V.tensor_scalar(xn, xn, 0.0, eps1[:, :], ALU.max, ALU.mult))
                                done(V.tensor_tensor(D, D, xn, ALU.add))
                            dve.sem_inc(td_free, 1)
                        if r in ALL_NODES:
                            k = (0 if r == R0 else NCH + 1) + s
                            all_nodes(i, lambda q: ln_at("N", q), (2 * len(mm), mm_base[r] + len(mm) * s + mm.index("N") + 1), CC, k)
                st.end(PAIRS, f"round {r}")
                if r == R0:
                    done(V.tensor_copy(gidx[:, 3 * COLS:], gidx[:, 2 * COLS:2 * COLS + 2 * CC]))
                    all_nodes(0, lambda q: (ln_base["last"], 0, 0, q), (0, mm_base["last"] + 1), DC_LAST, NCH)
                dve.sem_inc(cl_ready, 1)
                carries(r - R0 + 1)
                if r < ROUNDS - 1:
                    dve.sem_inc(carry_ready, 1)

            dve.sem_inc(rows_free, 1)
            with dve.Fori(0, PAIRS) as i:
                st.loop(i, 4)
                for s in range(2):
                    if s == 0:
                        dve.wait_ge(rows_free, i + 1)
                    D = v3(xd[:, bass.ds(i * (2 * CC * F) + s * CC * F, CC * F)], F)
                    xc3 = v3(xc[:, :], F)
                    done(V.tensor_tensor(xc3, bc(pm[:, bass.ds(i * 2 * CC + s * CC, CC)], F),
                                         carry[:, :].unsqueeze(1).to_broadcast([P, CC, F]), ALU.mult))
                    done(V.tensor_tensor(v3(g[s][:, 0:CC * ROW], ROW)[:, :, 0:F], D, xc3, ALU.add))
                    dve.sem_inc(rows_ready, 1)
            st.end(PAIRS, "rows")


_INS = ['x', 'src', 'dst', 'edge_attr_32', 'edge_weight', 'L1_gnn_W1_l', 'L1_gnn_b1', 'L1_gnn_W1_r',
        'L1_gnn_W2_l', 'L1_gnn_b2', 'L1_gnn_W2_r', 'L2_gnn_eps']
_OUTS = [((100000, 32), 'float32')]


def kernel(**inputs):
    import numpy as _np
    import concourse.bacc as _bacc
    from concourse import mybir as _mybir
    from concourse.bass_utils import run_bass_kernel_spmd as _run

    nc = _bacc.Bacc("TRN2", target_bir_lowering=False, num_devices=1)
    arrays, args = {}, []
    for name in _INS:
        a = _np.ascontiguousarray(inputs[name])
        arrays[f"in_{name}_dram"] = a
        args.append(nc.dram_tensor(f"in_{name}_dram", a.shape, _mybir.dt.from_np(a.dtype), kind="ExternalInput").ap())
    for i, (shape, dtype) in enumerate(_OUTS):
        dt = _mybir.dt.from_np(_np.dtype(dtype))
        args.append(nc.dram_tensor(f"out_{i}_dram", shape, dt, kind="ExternalOutput").ap())
    gnn_kernel(nc, *args)
    r = _run(nc, [arrays], core_ids=[0])
    return r.results[0]["out_0_dram"]
```

```python
import concourse.bass as bass
from concourse import mybir
from contextlib import ExitStack

FP32 = mybir.dt.float32
I32 = mybir.dt.int32
ALU = mybir.AluOpType
ACT = mybir.ActivationFunctionType
AX = mybir.AxisListType

P = 128
N, F = 100000, 32
E = 50000
HID = 64
COLS = -(-E // (P * 28)) * 28
EP = P * COLS
CC = 28
NCH = COLS // CC
PAIRS = NCH // 2
FULL_P = E // COLS
REST = E - FULL_P * COLS
ROW = F + 2
ZROWS = 80
CARRY_ROWS = EP
ZERO_ROW = EP + P
TROWS = EP + P + ZROWS
NP_, NPP = 125, 800
NOWHERE = float(1 << 20)
SB = 6250
LN_EPS = 1e-5
ADDS = 3
TO_DST = ADDS
R0 = ADDS + 1
ROUNDS = R0 + 4
BLK = 4
AROW = BLK * F
AROWS = N + P
ZW = AROWS * AROW // P // 16
NB = 40
TILES4 = CC // 4
DC_LAST = NPP - 2 * NCH * CC


class Steps:

    def __init__(self, eng, sem):
        self.eng, self.sem, self.base, self.reg, self.per, self.n = eng, sem, 0, None, 0, 0

    def loop(self, reg, per):
        self.reg, self.per, self.n = reg, per, 0

    def end(self, times, where):
        assert self.n == self.per, (where, self.n, self.per)
        self.base, self.reg, self.n = self.base + times * self.per, None, 0

    def done(self, ins):
        ins.then_inc(self.sem, 1)
        self.n += 1
        self.eng.wait_ge(self.sem, self.base + self.n if self.reg is None else self.reg * self.per + (self.base + self.n))
        if self.reg is None:
            self.base, self.n = self.base + self.n, 0


def gnn_kernel(nc, x, src, dst, ea, w, W1l, b1, W1r, W2l, b2, W2r, eps, out):
    with ExitStack() as ctx:
        def sb(name, shape, dt=FP32):
            return ctx.enter_context(nc.sbuf_tensor(name, shape, dt))

        def ps(name, shape):
            return ctx.enter_context(nc.psum_tensor(name, shape, FP32))

        def sem(name):
            return ctx.enter_context(nc.semaphore(name))

        adds = [nc.dram_tensor(f"adds{r}", [AROWS * BLK, F], FP32) for r in range(ADDS)]
        by_node = [a[:, :].rearrange("(n b) f -> n (b f)", b=BLK) for a in adds]
        pos_tab = nc.dram_tensor("pos_tab", [N, 2], FP32)
        node_tab = nc.dram_tensor("node_tab", [N, ROW], FP32)
        sums = {r: nc.dram_tensor(f"sums{r}", [TROWS, F], FP32) for r in range(R0, ROUNDS)}
        ea_pad = nc.dram_tensor("ea_pad", [EP, F], FP32)
        ea_perm = nc.dram_tensor("ea_perm", [EP, F], FP32)
        rec_perm = nc.dram_tensor("rec_perm", [EP, 4], I32)

        xs = sb("xs", [P, COLS * F])
        xd = sb("xd", [P, COLS * F])
        W = CC * F
        late = sb("late", [P, 7 * W + 3 * COLS])
        cut = lambda k, n=1: late[:, k * W:(k + n) * W]
        msg, km, sc, tout = cut(0), [cut(1), cut(2)], [cut(3), cut(4)], [cut(5), cut(6)]
        zeros = late[:, 0:ZW]
        prep = [late[:, 7 * W + k * COLS:7 * W + (k + 1) * COLS] for k in range(3)]
        last, cnt, ones = prep
        nx = [late[:, k * NB * F:(k + 1) * NB * F] for k in range(2)]
        nt = [late[:, 2 * NB * F + k * NB * ROW:2 * NB * F + (k + 1) * NB * ROW] for k in range(2)]
        sel = xs[:, 0:CC * P]
        arow = [xs[:, CC * P + k * W:CC * P + (k + 1) * W] for k in range(2)]
        low = xs[:, CC * P + 2 * W:CC * P + 2 * W + 4 * P]
        lowsel = xs[:, CC * P + 2 * W + 4 * P:CC * P + 2 * W + 8 * P]
        amsg = xs[:, CC * P + 2 * W + 8 * P:CC * P + 3 * W + 8 * P]
        na = [xs[:, k * NB * AROW:(k + 1) * NB * AROW] for k in range(2)]
        npt = [xs[:, 2 * NB * AROW + k * 2 * NB:2 * NB * AROW + (k + 1) * 2 * NB] for k in range(2)]
        src_i, dst_i = sb("src_i", [P, COLS], I32), sb("dst_i", [P, COLS], I32)
        wt = sb("wt", [P, COLS])
        keep, keepz = sb("keep", [P, COLS]), sb("keepz", [P, COLS])
        pm = sb("pm", [P, COLS])
        ic_s = sb("ic_s", [P, COLS])
        ic_d = sb("ic_d", [P, COLS])
        epos = sb("epos", [P, COLS])
        sidx = sb("sidx", [P, COLS])
        gdst = sb("gdst", [P, COLS + 2 * CC])
        gidx = sb("gidx", [P, 3 * COLS + 2 * CC])
        aidx = sb("aidx", [P, COLS])
        idxst = [sb(f"idxst{s}", [P, CC], I32) for s in range(2)]
        aidxst = [sb(f"aidxst{s}", [P, CC], I32) for s in range(2)]
        srcst = sb("srcst", [P, CC])
        b4, rep = sb("b4", [P, CC]), sb("rep", [P, CC])
        g = [sb(f"g{s}", [P, CC * AROW]) for s in range(2)]
        dprev, dnext = (g[1][:, 2 * W + k * COLS:2 * W + (k + 1) * COLS].bitcast(I32) for k in range(2))
        td = [g[s][:, CC * ROW:CC * ROW + W] for s in range(2)]
        eat = [g[s][:, CC * ROW + W:CC * ROW + 2 * W] for s in range(2)]
        state = sb("state", [P, F])
        carry = sb("carry", [P, F])
        carry_t = sb("carry_t", [F, P + 1])
        last_t = sb("last_t", [F, P])
        pm_t = sb("pm_t", [F, P])
        pm_b = sb("pm_b", [P, F])
        cidx_f, cidx = sb("cidx_f", [P, 1]), sb("cidx", [P, 1], I32)
        small = sb("small", [P, 8])
        first = sb("first", [P, 8])
        flag = sb("flag", [1, 1], I32)
        xc, sq = sb("xc", [P, W]), sb("sq", [P, W])
        s1, mean = sb("s1", [P, CC]), sb("mean", [P, CC])
        var, sd, rs = sb("var", [P, CC]), sb("sd", [P, CC]), sb("rs", [P, CC])
        ah = sb("ah", [P, CC * 2 * F])
        aht, h1t = [sb(f"aht{k}", [P, 512]) for k in range(2)], [sb(f"h1t{k}", [P, 512]) for k in range(2)]
        w1b, w2b = sb("w1b", [P, P]), sb("w2b", [P, P])
        b1b, b2b, eps1, lneps = sb("b1b", [P, 1]), sb("b2b", [P, F]), sb("eps1", [P, 1]), sb("lneps", [P, 1])
        ident = sb("ident", [P, P])
        zrow = sb("zrow", [P, F])
        dn = eat
        fin = sc
        pp = g[0][0:NP_, 0:2 * NPP]
        ocol, pcol = sb("ocol", [P, 1]), sb("pcol", [P, 1])

        tp, m1 = [ps(f"tp{k}", [P, 512]) for k in range(2)], [ps(f"m1{k}", [P, 512]) for k in range(2)]
        cp = m1[1]
        m2 = ps("m2", [P, 2048])
        dup = tp

        edges_in, edges_0 = sem("edges_in"), sem("edges_0")
        weights_in, weights_0, consts = sem("weights_in"), sem("weights_0"), sem("consts")
        prev_in, next_in, dst_ready = sem("prev_in"), sem("next_in"), sem("dst_ready")
        bad_ready, bad_sum, flag_ready = sem("bad_ready"), sem("bad_sum"), sem("flag_ready")
        ea_copied, zeros_in, zero_rows = sem("ea_copied"), sem("zeros_in"), sem("zero_rows")
        iotas, sort_in, ranks_ready, block_used, sorted_ready = (sem("iotas"), sem("sort_in"), sem("ranks_ready"),
                                                                 sem("block_used"), sem("sorted_ready"))
        sort_dma, rank_steps = sem("sort_dma"), sem("rank_steps")
        dve_s, act_s, pool_s = sem("dve_s"), sem("act_s"), sem("pool_s")
        meta_ready = sem("meta_ready")
        adds_clear = [sem(f"adds_clear{r}") for r in range(ADDS)]
        adds_done = [sem(f"adds_done{b}") for b in range(BLK)]
        low_ready, srcst_ready, dup_ready, sel_ready, amsg_ready, merged, arow_ready, arow_free = (
            sem("low_ready"), sem("srcst_ready"), sem("dup_ready"), sem("sel_ready"), sem("amsg_ready"), sem("merged"),
            sem("arow_ready"), sem("arow_free"))
        aidx_staged, added = sem("aidx_staged"), sem("added")
        pp_preset, pos_init, pos_dma, pos_ready = sem("pp_preset"), sem("pos_init"), sem("pos_dma"), sem("pos_ready")
        nx_in = [sem(f"nx_in{s}") for s in range(2)]
        nsum_ready, nsum_used, nt_ready, nt_out = sem("nsum_ready"), sem("nsum_used"), sem("nt_ready"), sem("nt_out")
        node_ready = sem("node_ready")
        dn_dma, dn_in, dn_done, dn_out = sem("dn_dma"), sem("dn_in"), sem("dn_done"), sem("dn_out")
        var_ready, sd_ready = sem("var_ready"), sem("sd_ready")
        ah_ready, tp_ready, aht_ready, m1_ready, h1t_ready, m2_ready, m2_free = (
            sem("ah_ready"), sem("tp_ready"), sem("aht_ready"), sem("m1_ready"), sem("h1t_ready"), sem("m2_ready"), sem("m2_free"))
        ah_free, h1t_used = sem("ah_free"), sem("h1t_used")
        g_full = [sem(f"g_full{s}") for s in range(2)]
        g_free, idx_staged = sem("g_free"), sem("idx_staged")
        km_ready, scan_done, tout_ready, tout_free = sem("km_ready"), sem("scan_done"), sem("tout_ready"), sem("tout_free")
        tout_dma = sem("tout_dma")
        td_dma, td_full, td_free = sem("td_dma"), sem("td_full"), sem("td_free")
        cl_ready, clt_ready, ct_ready, cc_ready, carry_ready, carry_done = (
            sem("cl_ready"), sem("clt_ready"), sem("ct_ready"), sem("cc_ready"), sem("carry_ready"), sem("carry_done"))
        xd_ready, node_dma, rows_ready, rows_free, out_dma = (
            sem("xd_ready"), sem("node_dma"), sem("rows_ready"), sem("rows_free"), sem("out_dma"))

        LN = {0: "D", R0: "SNn", R0 + 1: "S", R0 + 2: "SD", R0 + 3: "SNn", ROUNDS: "D"}
        MM = {R0: "N", R0 + 1: "S", R0 + 2: "D", R0 + 3: "N"}
        ALL_NODES = {R0: 0, R0 + 3: NCH}
        NL = 2 * NCH + 1
        ln_base, mm_base = {}, {}
        a, b = 0, 0
        for r in range(ROUNDS + 1):
            ln_base[r], mm_base[r] = a, b
            a, b = a + NCH * len(LN.get(r, "")), b + NCH * len(MM.get(r, ""))
            if r == R0:
                ln_base["last"], mm_base["last"] = a, b
                a, b = a + 2, b + 1
        BATCHES = {CC: (4, 4, 4, 2), DC_LAST: (2, 2, 2, 2)}
        QE = 4

        def ln_no(r, side, c0):
            if r in ALL_NODES and side == "n":
                return ln_base[r] + 3 * c0 + (3 if c0 < NCH - 1 else 2)
            if r in ALL_NODES:
                return ln_base[r] + (0 if c0 == 0 else 2 + 3 * (c0 - 1)) + (0 if side == "S" else 1 if c0 == 0 else 2)
            return ln_base[r] + len(LN[r]) * c0 + LN[r].index(side)

        def v3(ap, inner):
            return ap.rearrange("p (t f) -> p t f", f=inner)

        def bc(ap, n, parts=P):
            return ap.unsqueeze(2).to_broadcast([parts, ap.shape[1], n])

        block = ctx.enter_context(nc.Block())

        @block.sync
        def _(sp):
            sp.wait_ge(edges_0, 3)
            for tile, dram in ((src_i, src), (dst_i, dst), (wt, w)):
                sp.dma_start(tile[0:FULL_P, :], dram[0:FULL_P * COLS].rearrange("(p t) -> p t", t=COLS)).then_inc(edges_in, 16)
                sp.dma_start(tile[FULL_P:FULL_P + 1, 0:REST],
                             dram[FULL_P * COLS:E].rearrange("(p t) -> p t", p=1)).then_inc(edges_in, 16)
            sp.wait_ge(weights_0, 1)
            for t in range(2):
                o = t * 2 * F
                sp.dma_start(w1b[o:o + F, t * HID:(t + 1) * HID], W1l).then_inc(weights_in, 16)
                sp.dma_start(w1b[o + F:o + 2 * F, t * HID:(t + 1) * HID], W1r).then_inc(weights_in, 16)
                sp.dma_start(w2b[t * HID:(t + 1) * HID, o:o + F], W2l).then_inc(weights_in, 16)
                sp.dma_start(w2b[t * HID:(t + 1) * HID, o + F:o + 2 * F], W2r).then_inc(weights_in, 16)
                sp.dma_start(b1b[t * HID:(t + 1) * HID, :], b1.rearrange("(p a) -> p a", a=1)).then_inc(weights_in, 16)
            sp.dma_start(b2b[:, :], b2.rearrange("(a f) -> a f", a=1).to_broadcast([P, F])).then_inc(weights_in, 16)
            sp.dma_start(eps1[:, :], eps.rearrange("(a f) -> a f", a=1).to_broadcast([P, 1])).then_inc(weights_in, 16)
            sp.wait_ge(pp_preset, 2)
            sp.dma_start(pos_tab[:, :].rearrange("(p n) f -> p (n f)", p=NP_), pp).then_inc(pos_init, 16)
            sp.wait_ge(zeros_in, 2)

            def clear(r):
                av = adds[r][:, :].rearrange("(p n) f -> p (n f)", p=P)
                for k in range(16):
                    sp.dma_start(av[:, k * ZW:(k + 1) * ZW], zeros).then_inc(adds_clear[r], 16)
                    sp.wait_ge(adds_clear[r], 16 * (k + 1))

            sp.wait_ge(dst_ready, 1)
            sp.dma_start(dprev[1:P, 0:1], dst_i[0:P - 1, COLS - 1:COLS]).then_inc(prev_in, 16)
            sp.dma_start(ea_pad[0:E, :], ea).then_inc(ea_copied, 16)
            sp.dma_start(ea_pad[E:E + P, :], zrow[:, :]).then_inc(ea_copied, 16)
            sp.dma_start(ea_pad[E + P:EP, :], zrow[0:EP - E - P, :]).then_inc(ea_copied, 16)
            sp.wait_ge(dst_ready, 2)
            sp.dma_start(dprev[1:P, 0:1], dst_i[0:P - 1, COLS - 1:COLS]).then_inc(prev_in, 16)
            sp.dma_start(dnext[0:P - 1, COLS - 1:COLS], dst_i[1:P, 0:1]).then_inc(next_in, 16)
            for t in sums.values():
                sp.dma_start(t[ZERO_ROW:TROWS, :], zrow[0:ZROWS, :]).then_inc(zero_rows, 16)
                sp.dma_start(t[CARRY_ROWS:CARRY_ROWS + P, :], zrow[:, :]).then_inc(zero_rows, 16)
            for r in range(ADDS):
                clear(r)

            sp.wait_ge(added, ADDS)
            sp.wait_ge(pos_ready, 1)
            xv, tv = x.rearrange("(p n) f -> p n f", p=NP_), node_tab[:, :].rearrange("(p n) f -> p n f", p=NP_)
            av = by_node[ADDS - 1][0:N, :].rearrange("(p n) f -> p (n f)", p=NP_)
            pv = pos_tab[:, :].rearrange("(p n) f -> p (n f)", p=NP_)
            with sp.Fori(0, NPP // NB // 2) as i:
                for s in range(2):
                    n = bass.ds(i * 2 * NB + s * NB, NB)
                    sp.wait_ge(nt_ready, i * 2 + (s + 1))
                    sp.dma_start(na[s][0:NP_, :], av[:, bass.ds(i * (2 * NB * AROW) + s * NB * AROW, NB * AROW)]).then_inc(nx_in[s], 16)
                    sp.dma_start(v3(nx[s][0:NP_, :], F), xv[:, n, :]).then_inc(nx_in[s], 16)
                    sp.dma_start(npt[s][0:NP_, :], pv[:, bass.ds(i * (4 * NB) + 2 * s * NB, 2 * NB)]).then_inc(nx_in[s], 16)

            ov = out.rearrange("(p n) f -> p n f", p=NP_)

            def cols_of(t):
                return t[0:EP, :].rearrange("(p t) f -> p (t f)", p=P)

            def load_nodes(s, nodes, width, i, k):
                sp.dma_start(v3(dn[s][0:NP_, 0:width * F], F), tv[:, nodes, 0:F]).then_inc(dn_dma, 16)
                sp.wait_ge(dn_dma, i * 32 + 16 * (k + 1))
                sp.sem_inc(dn_in, 1)

            def store_nodes(s, nodes, width, i, k):
                sp.wait_ge(dn_done, i * 2 + (k + 1))
                sp.dma_start(ov[:, nodes, :], v3(dn[s][0:NP_, 0:width * F], F)).then_inc(dn_out, 16)
                sp.wait_ge(dn_out, i * 32 + 16 * (k + 1))

            def store_sums(r, i, c):
                sp.wait_ge(tout_ready, i * 2 + (NCH * (r - R0) + c + 1))
                sp.dma_start(cols_of(sums[r])[:, bass.ds(i * (2 * W) + c * W, W)], tout[c % 2]).then_inc(tout_dma, 16)
                sp.wait_ge(tout_dma, i * 32 + 16 * (NCH * (r - R0) + c + 1))
                sp.sem_inc(tout_free, 1)

            def nodes_of(r, i, c):
                return bass.ds(i * (2 * CC) + (ALL_NODES[r] + c) * CC, CC)

            def step(r, i, c):
                s, k = c % 2, (ALL_NODES.get(r, 0) and NCH + 1) + c
                at = bass.ds(i * (2 * W) + c * W, W)
                if r in ALL_NODES:
                    load_nodes(s, nodes_of(r, i, c), CC, i, k)
                if r == R0 + 2:
                    sp.wait_ge(td_free, i * 2 + (c + 1))
                    sp.dma_start(td[s], cols_of(sums[R0])[:, at]).then_inc(td_dma, 16)
                    sp.dma_start(eat[s], cols_of(ea_pad)[:, at]).then_inc(td_dma, 16)
                    sp.wait_ge(td_dma, i * 64 + 32 * (c + 1))
                    sp.sem_inc(td_full, 1)
                if r != R0 + 1:
                    store_sums(r, i, c)
                elif c:
                    store_sums(r, i, c - 1)
                if r in ALL_NODES and c:
                    store_nodes((c - 1) % 2, nodes_of(r, i, c - 1), CC, i, k - 1)
                sp.nop(nofuse=True)

            for r in range(R0, ROUNDS):
                if r == R0:
                    sp.wait_ge(node_ready, 1)
                    sp.wait_ge(g_free, NCH * R0 + 2)
                step(r, 0, 0)
                with sp.Fori(0, PAIRS - 1) as i:
                    step(r, i, 1)
                    step(r, i, 2)
                step(r, 0, NCH - 1)
                if r == R0 + 1:
                    store_sums(r, 0, NCH - 1)
                if r in ALL_NODES:
                    store_nodes(1, nodes_of(r, 0, NCH - 1), CC, 0, (ALL_NODES[r] and NCH + 1) + NCH - 1)
                if r == R0:
                    nodes = slice(NPP - DC_LAST, NPP)
                    load_nodes(0, nodes, DC_LAST, 0, NCH)
                    store_nodes(0, nodes, DC_LAST, 0, NCH)
            sp.wait_ge(carry_done, 64)
            with sp.Fori(0, PAIRS) as i:
                for s in range(2):
                    at = bass.ds(i * (2 * W) + s * W, W)
                    sp.wait_ge(td_free, i * 2 + (NCH + s + 1))
                    for tile, r in ((td[s], R0 + 1), (eat[s], R0 + 2), (fin[s], R0 + 3)):
                        sp.dma_start(tile, cols_of(sums[r])[:, at]).then_inc(td_dma, 16)
                    sp.wait_ge(td_dma, i * 96 + (32 * NCH + 48 * (s + 1)))
                    sp.sem_inc(td_full, 1)
            sp.wait_ge(out_dma, 16 * COLS)

        @block.gpsimd
        def _(pool):
            st = Steps(pool, pool_s)
            pool.iota(epos[:, :], [[1, COLS]], base=0, channel_multiplier=COLS, allow_small_or_imprecise_dtypes=True).then_inc(iotas, 1)
            st.done(pool.memset(ident[:, :], 0.0))
            pool.affine_select(out=ident[:, :], in_=ident[:, :], compare_op=ALU.not_equal, fill=1.0, base=0,
                               pattern=[[-1, P]], channel_multiplier=1).then_inc(consts, 1)
            pool.iota(ocol[:, :], [[0, 1]], base=CARRY_ROWS, channel_multiplier=1, allow_small_or_imprecise_dtypes=True).then_inc(iotas, 1)
            pool.iota(b4[:, :], [[0, TILES4], [1, 4]], base=0, channel_multiplier=0, allow_small_or_imprecise_dtypes=True).then_inc(iotas, 1)
            pool.iota(pcol[:, :], [[0, 1]], base=N, channel_multiplier=1, allow_small_or_imprecise_dtypes=True).then_inc(iotas, 1)
            ppv = pp.rearrange("p (a n f) -> p a n f", n=ZROWS, f=2)
            pool.iota(ppv[:, :, :, 0], [[0, NPP // ZROWS], [1, ZROWS]], base=ZERO_ROW, channel_multiplier=0,
                      allow_small_or_imprecise_dtypes=True).then_inc(pp_preset, 1)
            pool.memset(ppv[:, :, :, 1], 1.0).then_inc(pp_preset, 1)

            pool.wait_ge(flag_ready, 1)
            pool.wait_ge(ea_copied, 48)
            bad = pool.value_load(flag[0:1, 0:1], min_val=0, max_val=1)
            with pool.If(bad > 0):
                fb = Steps(pool, sort_in)
                db = xs[:, 0:SB].bitcast(I32)
                gi = xs[:, 2 * SB - SB:2 * SB].bitcast(I32)
                fb.done(pool.iota(gi, [[1, SB]], base=0, channel_multiplier=0))
                for k in range(E // SB):
                    if k:
                        pool.wait_ge(block_used, k)
                    pool.dma_start(db, dst[k * SB:(k + 1) * SB].rearrange("(a f) -> a f", a=1).to_broadcast([P, SB])).then_inc(sort_dma, 16)
                    pool.wait_ge(sort_dma, 16 * (k + 1))
                pool.wait_ge(ranks_ready, 1)
                rank, rec = xs[:, 0:COLS], xs[:, COLS:COLS + CC * 4]
                ear, ri = xs[:, 2 * COLS:2 * COLS + CC * F], idxst[0]
                rec3 = v3(rec, 4)
                fb.done(pool.memset(rec, 0.0))
                eav = ea_pad[:, :].rearrange("(p t) f -> p (t f)", p=P)
                fbase, dbase = fb.base, 16 * (E // SB)
                moved = 16 * (2 * CC + 1)
                with pool.Fori(0, NCH) as i:
                    fb.loop(i, 4)
                    cols = bass.ds(i * CC, CC)
                    pool.dma_start(ear, eav[:, bass.ds(i * (CC * F), CC * F)]).then_inc(sort_dma, 16)
                    fb.done(pool.tensor_copy(ri[:, :], rank[:, cols]))
                    fb.done(pool.tensor_copy(rec3[:, :, 0].bitcast(I32), src_i[:, cols]))
                    fb.done(pool.tensor_copy(rec3[:, :, 1].bitcast(I32), dst_i[:, cols]))
                    fb.done(pool.tensor_copy(rec3[:, :, 2], wt[:, cols]))
                    pool.wait_ge(sort_dma, i * moved + (dbase + 16))
                    pool.nop(nofuse=True)
                    for k in range(CC):
                        at = bass.IndirectOffsetOnAxis(ri[:, k:k + 1], 0)
                        pool.indirect_dma_start(ea_perm[:, :], at, ear[:, k * F:(k + 1) * F], None).then_inc(sort_dma, 16)
                        pool.indirect_dma_start(rec_perm[:, :], at, rec[:, 4 * k:4 * k + 4].bitcast(I32), None).then_inc(sort_dma, 16)
                    pool.wait_ge(sort_dma, i * moved + (dbase + moved))
                    pool.nop(nofuse=True)
                fb.end(NCH, "sort")
                total = dbase + moved * NCH
                pool.dma_start(ea_pad[:, :], ea_perm[:, :]).then_inc(sort_dma, 16)
                pool.dma_start(xd[:, 0:4 * COLS].bitcast(I32), rec_perm[:, :].rearrange("(p t) f -> p (t f)", p=P)).then_inc(sort_dma, 16)
                pool.wait_ge(sort_dma, total + 32)
                got = v3(xd[:, 0:4 * COLS], 4)
                fb.done(pool.tensor_copy(src_i[:, :], got[:, :, 0].bitcast(I32)))
                fb.done(pool.tensor_copy(dst_i[:, :], got[:, :, 1].bitcast(I32)))
                fb.done(pool.tensor_copy(wt[:, :], got[:, :, 2]))
            pool.drain().then_inc(sorted_ready, 1)

            st.done(pool.memset(low, 1.0))
            pool.affine_select(out=v3(low, P), in_=v3(low, P), compare_op=ALU.is_gt, fill=0.0, base=0,
                               pattern=[[0, 4], [-1, P]], channel_multiplier=1).then_inc(low_ready, 1)

            pool.wait_ge(meta_ready, 1)
            pool.wait_ge(pos_init, 16)
            with pool.Fori(0, PAIRS) as i:
                st.loop(i, 6)
                for s in range(2):
                    cols = bass.ds(i * 2 * CC + s * CC, CC)
                    gv = v3(g[s][:, 0:2 * CC], 2)
                    st.done(pool.tensor_copy(aidxst[s][:, :], sidx[:, cols]))
                    st.done(pool.tensor_copy(gv[:, :, 0], epos[:, cols]))
                    st.done(pool.tensor_copy(gv[:, :, 1], ic_d[:, cols]))
                pool.nop(nofuse=True)
                for s in range(2):
                    for k in range(CC):
                        pool.indirect_dma_start(pos_tab[:, :], bass.IndirectOffsetOnAxis(aidxst[s][:, k:k + 1], 0),
                                                g[s][:, 2 * k:2 * k + 2], None,
                                                bounds_check=N - 1, oob_is_err=False).then_inc(pos_dma, 16)
                pool.wait_ge(pos_dma, i * (32 * CC) + 32 * CC)
                pool.nop(nofuse=True)
            st.end(PAIRS, "positions")
            pool.drain().then_inc(pos_ready, 1)

            def gather(r, s, i, c):
                tab, width, pitch = ((x[:, :], F, AROW) if r == 0 else (by_node[r - 1], AROW, AROW) if r <= TO_DST
                                     else (node_tab[:, :], ROW, ROW) if r == R0 else (sums[r - 1][:, :], F, ROW))
                n = NCH * r + c
                pool.wait_ge(idx_staged, i * 2 + (n + 1))
                pool.wait_ge(g_free, i * 2 + (n + 1))
                pool.nop(nofuse=True)
                for k in range(CC):
                    pool.indirect_dma_start(g[s][:, k * pitch:k * pitch + width], None, tab,
                                            bass.IndirectOffsetOnAxis(idxst[s][:, k:k + 1], 0)).then_inc(g_full[s], 16)

            def settle(r, i, c):
                for b in range(BLK):
                    pool.wait_ge(adds_done[b], i * (32 * TILES4) + 16 * TILES4 * (NCH * r + c + 1))
                pool.nop(nofuse=True)
                pool.sem_inc(arow_free, 1)

            def add(r, s, i, c):
                n = NCH * r + c
                pool.wait_ge(aidx_staged, i * 2 + (n + 1))
                pool.wait_ge(arow_ready, i * 2 + (n + 2))
                pool.nop(nofuse=True)
                for k in range(CC):
                    b = k % BLK
                    if k >= BLK:
                        pool.wait_ge(adds_done[b], i * (32 * TILES4) + 16 * (TILES4 * n + k // BLK))
                        pool.nop(nofuse=True)
                    pool.indirect_dma_start(adds[r][:, :], bass.IndirectOffsetOnAxis(aidxst[s][:, k:k + 1], 0),
                                            arow[s][:, k * F:(k + 1) * F], None, bounds_check=AROWS * BLK - 1,
                                            oob_is_err=True, compute_op=ALU.add).then_inc(adds_done[b], 16)

            for r in range(ADDS):
                gather(r, 0, 0, 0)
                pool.wait_ge(adds_clear[r], 16 * 16)
                with pool.Fori(0, PAIRS - 1) as i:
                    gather(r, 1, i, 1)
                    add(r, 0, i, 0)
                    gather(r, 0, i, 2)
                    settle(r, i, 0)
                    add(r, 1, i, 1)
                    settle(r, i, 1)
                gather(r, 1, 0, NCH - 1)
                add(r, 0, 0, NCH - 2)
                settle(r, 0, NCH - 2)
                add(r, 1, 0, NCH - 1)
                settle(r, 0, NCH - 1)
                pool.sem_inc(added, 1)

            for r in range(TO_DST, ROUNDS):
                if r == R0:
                    pool.wait_ge(nt_out, 16 * (NPP // NB))
                    pool.sem_inc(node_ready, 1)
                with pool.Fori(0, PAIRS) as i:
                    for s in range(2):
                        gather(r, s, i, s)
                if r >= R0:
                    if r == R0:
                        pool.wait_ge(zero_rows, 32 * len(sums))
                    pool.wait_ge(carry_ready, r - R0 + 1)
                    pool.wait_ge(tout_dma, 16 * NCH * (r - R0 + 1))
                    pool.indirect_dma_start(sums[r][:, :], bass.IndirectOffsetOnAxis(cidx[:, :], 0),
                                            carry[:, :], None, bounds_check=TROWS - 1, oob_is_err=True,
                                            compute_op=ALU.add).then_inc(carry_done, 16)
                    pool.wait_ge(carry_done, 16 * (r - R0 + 1))

            pool.wait_ge(dn_out, 16 * (2 * NCH + 1))
            pool.wait_ge(idx_staged, NCH * ROUNDS + 2)
            for s in range(2):
                pool.wait_ge(g_full[s], 16 * CC * PAIRS * ROUNDS)
            with pool.Fori(0, PAIRS) as i:
                st.loop(i, 2)
                for s in range(2):
                    st.done(pool.tensor_copy(idxst[s][:, :], sidx[:, bass.ds(i * 2 * CC + s * CC, CC)]))
                for s in range(2):
                    pool.wait_ge(rows_ready, i * 2 + (s + 1))
                    pool.nop(nofuse=True)
                    for k in range(CC):
                        pool.indirect_dma_start(out[:, :], bass.IndirectOffsetOnAxis(idxst[s][:, k:k + 1], 0),
                                                g[s][:, k * ROW:k * ROW + F], None,
                                                bounds_check=N - 1, oob_is_err=False).then_inc(out_dma, 16)
                pool.wait_ge(out_dma, i * (32 * CC) + 32 * CC)
                pool.nop(nofuse=True)
                pool.drain().then_inc(rows_free, 1)
            st.end(PAIRS, "out rows")
            pool.wait_ge(out_dma, 16 * COLS)

        @block.scalar
        def _(act):
            def root(base, i, per, j, parts, cols):
                act.wait_ge(var_ready, i * per + (base + j + 1))
                nc.scalar.activation(sd[0:parts, 0:cols], var[0:parts, 0:cols], ACT.Sqrt,
                                     bias=lneps[0:parts, :], scale=1.0 / F).then_inc(sd_ready, 1)

            def sage(base, i, j, cols, half=None):
                def columns(q):
                    n = BATCHES[cols][q]
                    act.wait_ge(tp_ready, i * (QE * 2) + (QE * (base + j) + q + 1))
                    nc.scalar.activation(aht[q % 2][:, 0:n * P], tp[q % 2][:, 0:n * P], ACT.Copy).then_inc(aht_ready, 1)

                def hidden(q):
                    n, k = BATCHES[cols][q], QE * (base + j) + q + 1
                    act.wait_ge(m1_ready, i * (QE * 2) + k)
                    act.wait_ge(h1t_used, i * (QE * 2) + k)
                    nc.scalar.activation(h1t[q % 2][:, 0:n * P], m1[q % 2][:, 0:n * P], ACT.Relu, bias=b1b[:, :]).then_inc(h1t_ready, 1)

                if half != 1:
                    columns(0)
                    columns(1)
                    hidden(0)
                    columns(2)
                    hidden(1)
                if half != 0:
                    columns(3)
                    hidden(2)
                    hidden(3)

            act.wait_ge(consts, 3)
            act.wait_ge(weights_in, 16 * 12)
            for r in range(ADDS):
                with act.Fori(0, PAIRS) as i:
                    for s in range(2):
                        n = NCH * r + s
                        if r == 0:
                            root(0, i, 2, s, P, CC)
                        act.wait_ge(merged, i * 2 + (n + 1))
                        act.wait_ge(arow_free, i * 2 + (n + 1))
                        nc.scalar.activation(arow[s], m2[:, 0:CC * F], ACT.Copy).then_inc(arow_ready, 1)
            act.sem_inc(nt_ready, 2)
            with act.Fori(0, NPP // NB // 2) as i:
                for s in range(2):
                    act.wait_ge(nsum_ready, i * 2 + (s + 1))
                    ntv = v3(nt[s][0:NP_, :], ROW)
                    nc.scalar.activation(ntv[:, :, 0:F], v3(m2[0:NP_, 0:NB * F], F), ACT.Copy).then_inc(nsum_used, 1)
                    nc.scalar.activation(ntv[:, :, F:F + 2], v3(npt[s][0:NP_, :], 2), ACT.Copy).then_inc(nt_ready, 1)
                    act.wait_ge(nt_ready, i * 2 + (s + 3))
                    act.wait_ge(nsum_used, i * 2 + (s + 2))
                    act.dma_start(node_tab[:, :].rearrange("(p n) f -> p (n f)", p=NP_)[:, bass.ds(i * (2 * NB * ROW) + s * NB * ROW, NB * ROW)],
                                  nt[s][0:NP_, :]).then_inc(nt_out, 16)
                    act.wait_ge(nt_out, i * 32 + 16 * (s + 1))
                    act.nop(nofuse=True)
            def ln(r, i, c, side):
                root(ln_no(r, side, c), i, 2 * len(LN[r]), 0, NP_ if side in "Nn" else P, CC)

            def store(r, i, c):
                n = NCH * (r - R0) + c
                act.wait_ge(scan_done, i * 2 + (n + 1))
                act.wait_ge(tout_free, i * 2 + (n + 1))
                nc.scalar.activation(v3(tout[c % 2], F), sc[c % 2].rearrange("p (f t) -> p t f", t=CC),
                                     ACT.Copy).then_inc(tout_ready, 1)

            def step(r, i, c):
                nc.scalar.activation(km[c % 2].rearrange("p (f t) -> p f t", t=CC),
                                     keepz[:, bass.ds(i * 2 * CC + c * CC, CC)].unsqueeze(1).to_broadcast([P, F, CC]),
                                     ACT.Copy).then_inc(km_ready, 1)
                ln(r, i, c, "S")
                if c:
                    sage(mm_base[r], i, c - 1, CC, 1)
                if r != R0 + 1:
                    store(r, i, c)
                elif c:
                    store(r, i, c - 1)
                if r in ALL_NODES:
                    if c:
                        ln(r, i, c - 1, "n")
                    ln(r, i, c, "N")
                if r == R0 + 2:
                    ln(r, i, c, "D")
                sage(mm_base[r], i, c, CC, 0)

            for r in range(R0, ROUNDS):
                step(r, 0, 0)
                with act.Fori(0, PAIRS - 1) as i:
                    step(r, i, 1)
                    step(r, i, 2)
                step(r, 0, NCH - 1)
                sage(mm_base[r], 0, NCH - 1, CC, 1)
                if r == R0 + 1:
                    store(r, 0, NCH - 1)
                if r in ALL_NODES:
                    ln(r, 0, NCH - 1, "n")
                if r == R0:
                    root(ln_base["last"], 0, 0, 0, NP_, DC_LAST)
                    sage(mm_base["last"], 0, 0, DC_LAST)
                    root(ln_base["last"], 0, 0, 1, NP_, DC_LAST)
            with act.Fori(0, PAIRS) as i:
                for s in range(2):
                    root(ln_base[ROUNDS], i, 2, s, P, CC)

        @block.tensor
        def _(pe):
            pe.wait_ge(bad_ready, 1)
            nc.tensor.matmul(cp[0:1, 0:1], small[:, 0:1], ones[:, 0:1], start=True, stop=True).then_inc(bad_sum, 1)

            def sage(base, i, j, cols, both):
                at = lambda k: i * (QE * 2) + (QE * (base + j) + k + 1)
                col = [sum(BATCHES[cols][:q]) for q in range(QE)]
                pe.wait_ge(ah_ready, i * 2 + (base + j + 1))

                def columns(q):
                    for u in range(BATCHES[cols][q]):
                        ins = nc.tensor.transpose(tp[q % 2][:, u * P:(u + 1) * P], ah[:, (col[q] + u) * P:(col[q] + u + 1) * P], ident[:, :])
                    ins.then_inc(tp_ready, 1)

                def hidden(q):
                    n = BATCHES[cols][q]
                    pe.wait_ge(aht_ready, at(q))
                    nc.tensor.matmul(m1[q % 2][:, 0:n * P], w1b[:, :], aht[q % 2][:, 0:n * P], start=True, stop=True).then_inc(m1_ready, 1)

                def result(q):
                    pe.wait_ge(h1t_ready, at(q))
                    if q == 0:
                        pe.wait_ge(m2_free, i * 2 + (base + j + 1))
                    width = P if both else 2 * F
                    for u in range(BATCHES[cols][q]):
                        rhs = w2b[:, :] if both else w2b[:, :].rearrange("p (t f) -> p t f", f=2 * F)[:, :, F:2 * F]
                        ins = nc.tensor.matmul(m2[:, (col[q] + u) * width:(col[q] + u + 1) * width], h1t[q % 2][:, u * P:(u + 1) * P],
                                               rhs, start=True, stop=True)
                    ins.then_inc(h1t_used, 1)

                columns(0)
                columns(1)
                hidden(0)
                columns(2)
                hidden(1)
                result(0)
                columns(3)
                hidden(2)
                result(1)
                hidden(3)
                pe.sem_inc(ah_free, 1)
                result(2)
                result(3)

            pe.wait_ge(consts, 3)
            pe.wait_ge(cl_ready, 1)
            nc.tensor.transpose(cp[0:F, 128:256], pm_b[:, :], ident[:, :]).then_inc(clt_ready, 1)
            nc.tensor.transpose(cp[0:F, 0:P], state[:, :], ident[:, :]).then_inc(clt_ready, 1)
            pe.wait_ge(ct_ready, 1)
            nc.tensor.transpose(cp[:, 256:256 + F], carry_t[:, 0:P], ident[0:F, 0:F]).then_inc(cc_ready, 1)
            for r in range(ADDS):
                with pe.Fori(0, PAIRS) as i:
                    for s in range(2):
                        n = NCH * r + s
                        pe.wait_ge(srcst_ready, i * 2 + (n + 1))
                        for q in range(TILES4):
                            pe.wait_ge(sel_ready, i * (2 * TILES4) + (TILES4 * n + q + 1))
                            for u in range(4):
                                ins = nc.tensor.transpose(dup[(s + q) % 2][:, u * P:(u + 1) * P],
                                                          srcst[:, 4 * q + u:4 * q + u + 1].to_broadcast([P, P]), ident[:, :])
                            ins.then_inc(dup_ready, 1)
                        pe.wait_ge(amsg_ready, i * 2 + (n + 1))
                        pe.wait_ge(arow_ready, i * 2 + (n + 1))
                        for k in range(CC):
                            ins = nc.tensor.matmul(m2[:, k * F:(k + 1) * F], sel[:, k * P:(k + 1) * P], amsg[:, k * F:(k + 1) * F],
                                                   start=True, stop=True)
                        ins.then_inc(merged, 1)
            pe.wait_ge(arow_ready, NCH * ADDS + 1)
            with pe.Fori(0, NPP // NB // 2) as i:
                for s in range(2):
                    pe.wait_ge(nx_in[s], i * 48 + 48)
                    pe.wait_ge(nsum_used, i * 2 + (s + 1))
                    for o in range(0, NB, 16):
                        n = min(16, NB - o)
                        for b in range(BLK + 1):
                            rhs = (v3(nx[s][0:NP_, :], F)[:, o:o + n, :] if b == BLK else
                                   v3(na[s][0:NP_, :], AROW)[:, o:o + n, b * F:(b + 1) * F])
                            ins = nc.tensor.matmul(m2[0:NP_, o * F:(o + n) * F], ident[0:NP_, 0:NP_], rhs, start=b == 0, stop=b == BLK)
                    ins.then_inc(nsum_ready, 1)
            pe.wait_ge(weights_in, 16 * 12)
            for r in range(R0, ROUNDS):
                with pe.Fori(0, PAIRS) as i:
                    for s in range(2):
                        sage(mm_base[r], i, s, CC, MM[r] == "S")
                if r == R0:
                    sage(mm_base["last"], 0, 0, DC_LAST, False)
                pe.wait_ge(cl_ready, r - R0 + 2)
                nc.tensor.transpose(cp[0:F, 0:P], state[:, :], ident[:, :]).then_inc(clt_ready, 1)
                pe.wait_ge(ct_ready, r - R0 + 2)
                nc.tensor.transpose(cp[:, 256:256 + F], carry_t[:, 0:P], ident[0:F, 0:F]).then_inc(cc_ready, 1)

        @block.vector
        def _(dve):
            V = nc.vector
            st = Steps(dve, dve_s)
            done = st.done
            V.memset(src_i[:, :], 0).then_inc(edges_0, 1)
            V.memset(dst_i[:, :], N).then_inc(edges_0, 1)
            V.memset(wt[:, :], 0.0).then_inc(edges_0, 1)
            V.memset(zeros, 0.0).then_inc(zeros_in, 1)
            V.memset(zrow[:, :], 0.0).then_inc(zeros_in, 1)
            done(V.memset(w1b[:, :], 0.0))
            done(V.memset(w2b[:, :], 0.0))
            V.memset(ah[:, :], 0.0).then_inc(weights_0, 1)
            V.memset(lneps[:, :], LN_EPS).then_inc(consts, 1)
            done(V.memset(carry_t[:, :], 0.0))
            V.memset(state[:, :], 0.0).then_inc(consts, 1)
            dve.sem_inc(g_free, 2)
            dve.sem_inc(sel_ready, 2)
            dve.sem_inc(arow_ready, 1)
            dve.sem_inc(arow_free, 2)
            dve.sem_inc(nsum_used, 1)
            dve.sem_inc(h1t_used, 2)
            dve.sem_inc(ah_free, 1)
            dve.sem_inc(m2_free, 1)
            dve.sem_inc(tout_free, 2)
            dve.sem_inc(td_free, 2)
            done(V.memset(ones, 1.0))
            done(V.memset(dprev, -1))
            done(V.memset(dnext, -1))
            dve.wait_ge(edges_in, 16 * 6)

            def neighbours(k):
                done(V.tensor_copy(dprev[:, 1:COLS], dst_i[:, 0:COLS - 1]))
                if k:
                    done(V.tensor_copy(dnext[:, 0:COLS - 1], dst_i[:, 1:COLS]))
                dve.sem_inc(dst_ready, 1)
                dve.wait_ge(prev_in, 16 * (k + 1))
                if k:
                    dve.wait_ge(next_in, 16)

            neighbours(0)
            done(V.tensor_tensor(keep[:, :], dprev, dst_i[:, :], ALU.is_gt))
            V.tensor_reduce(small[:, 0:1], keep[:, :], axis=AX.X, op=ALU.add).then_inc(bad_ready, 1)
            dve.wait_ge(bad_sum, 1)
            done(V.tensor_scalar(small[0:1, 1:2], cp[0:1, 0:1], 0.5, None, ALU.is_gt))
            V.tensor_copy(flag[:, :], small[0:1, 1:2]).then_inc(flag_ready, 1)
            dve.wait_ge(flag_ready, 1)
            dve.wait_ge(iotas, 4)

            bad = dve.value_load(flag[0:1, 0:1], min_val=0, max_val=1)
            with dve.If(bad > 0):
                fb = Steps(dve, rank_steps)
                db = xs[:, 0:SB].bitcast(I32)
                gi = xs[:, SB:2 * SB].bitcast(I32)
                gf, cmpd = xd[:, 0:SB], xd[:, SB:2 * SB]
                dstf, thr, acc, rk = keep, keepz, last, cnt
                dve.wait_ge(sort_in, 1)
                fb.done(V.tensor_scalar(gf, gi, 2.0 ** -16, None, ALU.mult))
                fb.done(V.tensor_copy(dstf[:, :], dst_i[:, :]))
                fb.done(V.tensor_scalar(acc, epos[:, :], float(E), None, ALU.subtract))
                fb.done(V.scalar_tensor_tensor(rk, dstf[:, :], float(N), acc, ALU.is_equal, ALU.mult))
                for k in range(E // SB):
                    fb.done(V.tensor_scalar(thr[:, :], epos[:, :], float(-k * SB), 2.0 ** -16, ALU.add, ALU.mult))
                    dve.wait_ge(sort_dma, 16 * (k + 1))
                    with dve.Fori(0, COLS) as t:
                        fb.loop(t, 2)
                        one = bass.ds(t, 1)
                        fb.done(V.scalar_tensor_tensor(cmpd, db, dstf[:, one], gf, ALU.subtract, ALU.add))
                        fb.done(V.tensor_scalar(cmpd, cmpd, thr[:, one], None, ALU.is_lt, ALU.add, accum_out=acc[:, one]))
                    fb.end(COLS, "rank")
                    fb.done(V.tensor_tensor(rk, rk, acc, ALU.add))
                    dve.sem_inc(block_used, 1)
                V.tensor_copy(xs[:, 0:COLS], rk).then_inc(ranks_ready, 1)
                dve.wait_ge(ranks_ready, 1)
            dve.wait_ge(sorted_ready, 1)

            neighbours(1)
            done(V.tensor_tensor(keep[:, :], dprev, dst_i[:, :], ALU.is_equal))
            done(V.tensor_copy(keepz[:, :], keep[:, :]))
            done(V.memset(v3(keepz[:, :], CC)[:, :, 0], 0.0))
            done(V.tensor_tensor(last, dnext, dst_i[:, :], ALU.not_equal))
            done(V.tensor_tensor_scan(pm[:, :], keep[:, :], keep[:, :], 1.0, ALU.mult, ALU.mult))
            done(V.tensor_tensor_scan(cnt, keep[:, :], ones, 0.0, ALU.mult, ALU.add))
            done(V.tensor_copy(pm_b[:, :], pm[:, COLS - 1:COLS].to_broadcast([P, F])))
            V.tensor_copy(state[:, 0:1], cnt[:, COLS - 1:COLS]).then_inc(cl_ready, 1)

            def carries(n):
                dve.wait_ge(clt_ready, n + 2)
                if n == 0:
                    done(V.tensor_copy(pm_t[:, :], cp[0:F, 128:256]))
                done(V.tensor_copy(last_t[:, :], cp[0:F, 0:P]))
                V.tensor_tensor_scan(carry_t[:, 1:P + 1], pm_t[:, :], last_t[:, :], 0.0, ALU.mult, ALU.add).then_inc(ct_ready, 1)
                dve.wait_ge(cc_ready, n + 1)
                if n > 1:
                    dve.wait_ge(carry_done, 16 * (n - 1))
                done(V.tensor_copy(carry[:, :], cp[:, 256:256 + F]))

            carries(0)
            done(V.scalar_tensor_tensor(cnt, pm[:, :], carry[:, 0:1], cnt, ALU.mult, ALU.add))
            done(V.reciprocal(ic_d[:, :], cnt))
            done(V.tensor_reduce(small[:, 2:3], pm[:, :], axis=AX.X, op=ALU.add))
            done(V.tensor_scalar(small[:, 3:4], last[:, COLS - 1:COLS], -1.0, 1.0, ALU.mult, ALU.add))
            done(V.scalar_tensor_tensor(small[:, 4:5], small[:, 2:3], float(COLS), small[:, 3:4], ALU.is_equal, ALU.mult))
            done(V.tensor_scalar(small[:, 4:5], small[:, 4:5], -1.0, 1.0, ALU.mult, ALU.add))
            done(V.scalar_tensor_tensor(small[:, 4:5], small[:, 2:3], 0.5, small[:, 4:5], ALU.is_gt, ALU.mult))
            done(V.scalar_tensor_tensor(small[:, 5:6], epos[:, 0:1], -1.0, small[:, 2:3], ALU.add, ALU.add))
            done(V.tensor_tensor(small[:, 5:6], small[:, 5:6], ocol[:, :], ALU.subtract))
            done(V.scalar_tensor_tensor(cidx_f[:, :], small[:, 5:6], small[:, 4:5], ocol[:, :], ALU.mult, ALU.add))
            done(V.tensor_copy(cidx[:, :], cidx_f[:, :]))
            done(V.tensor_scalar(sidx[:, :], last, -NOWHERE, NOWHERE, ALU.mult, ALU.add))
            done(V.tensor_tensor(sidx[:, :], sidx[:, :], dst_i[:, :], ALU.add))
            done(V.tensor_scalar(gidx[:, 0:COLS], dst_i[:, :], float(N - 1), None, ALU.min))
            done(V.tensor_copy(gdst[:, 0:COLS], gidx[:, 0:COLS]))
            done(V.tensor_copy(gdst[:, COLS:], gidx[:, 0:2 * CC]))
            done(V.tensor_copy(gidx[:, COLS:2 * COLS], src_i[:, :]))
            for s in range(2):
                V.tensor_copy(idxst[s][:, :], gdst[:, s * CC:(s + 1) * CC]).then_inc(idx_staged, 1)
            dve.wait_ge(weights_in, 16 * 12)
            done(V.tensor_scalar(eps1[:, :], eps1[:, :], 1.0, None, ALU.add))
            dve.sem_inc(meta_ready, 1)

            def layernorm(xv, base, i, per, j, parts, cols):
                dve.nop(nofuse=True)
                xc3, sq3 = v3(xc[0:parts, 0:cols * F], F), v3(sq[0:parts, 0:cols * F], F)
                c = slice(0, cols)
                done(V.tensor_reduce(s1[0:parts, c], xv, axis=AX.X, op=ALU.add))
                done(V.tensor_scalar(mean[0:parts, c], s1[0:parts, c], 1.0 / F, None, ALU.mult))
                done(V.tensor_tensor(xc3, xv, bc(mean[0:parts, c], F, parts), ALU.subtract))
                done(V.tensor_tensor(sq3, xc3, xc3, ALU.mult))
                V.tensor_reduce(var[0:parts, c], sq3, axis=AX.X, op=ALU.add).then_inc(var_ready, 1)
                dve.wait_ge(sd_ready, i * per + (base + j + 1))
                done(V.reciprocal(rs[0:parts, c], sd[0:parts, c]))
                done(V.tensor_tensor(sq3, xc3, bc(rs[0:parts, c], F, parts), ALU.mult))
                return sq3

            def copy(o, i_):
                return V.tensor_scalar(o, i_, 1.0, None, ALU.mult)

            def m2_out(half, parts, cols):
                if half is None:
                    return v3(m2[0:parts, 0:cols * F], F)
                return m2[0:parts, 0:cols * 2 * F].rearrange("p (t f) -> p t f", f=2 * F)[:, :, half * F:(half + 1) * F]

            def sage_in(xn, agg, parts, cols, at):
                ahv = v3(ah[0:parts, 0:cols * 2 * F], 2 * F)
                dve.wait_ge(ah_free, at)
                if agg is not None:
                    V.tensor_tensor(ahv[:, :, 0:F], *agg, ALU.mult)
                V.tensor_scalar(ahv[:, :, F:2 * F], xn, 0.0, None, ALU.max).then_inc(ah_ready, 1)

            def sage_root(xv, out_half, parts, cols, at, msg_to=None):
                t3 = v3(xc[0:parts, 0:cols * F], F)
                dve.wait_ge(h1t_used, at)
                if msg_to is not None:
                    done(copy(msg_to, m2_out(0, parts, cols)))
                done(V.tensor_tensor(t3, m2_out(out_half, parts, cols), b2b[0:parts, :].unsqueeze(1).to_broadcast([parts, cols, F]), ALU.add))
                dve.sem_inc(m2_free, 1)
                done(V.tensor_tensor(xv, xv, t3, ALU.add))

            def nodes_1(s, i, k, ln_at, mm_at, cols):
                dve.wait_ge(dn_in, i * 2 + (k + 1))
                xn = layernorm(v3(dn[s][0:NP_, 0:cols * F], F), *ln_at, NP_, cols)
                sage_in(xn, None, NP_, cols, i * 2 + mm_at + 1)

            def nodes_2(s, i, ln_at, mm_at, cols):
                dn3 = v3(dn[s][0:NP_, 0:cols * F], F)
                sage_root(dn3, None, NP_, cols, i * (2 * QE) + (QE * (mm_at + 1) + 2))
                xn = layernorm(dn3, *ln_at, NP_, cols)
                done(V.tensor_scalar(xn, xn, 0.0, eps1[0:NP_, :], ALU.max, ALU.mult))
                done(V.tensor_tensor(dn3, dn3, xn, ALU.add))
                dve.sem_inc(dn_done, 1)

            per = {0: 27, 1: 2, 2: 2, 3: 2, 4: 29, 5: 12, 6: 23, 7: 27, 8: 12}
            srcf = gidx[:, COLS:2 * COLS]
            for r in range(ADDS):
                with dve.Fori(0, PAIRS) as i:
                    st.loop(i, 2 * per[r])
                    for s in range(2):
                        n = NCH * r + s
                        off = lambda wdt, o=0: bass.ds(i * (2 * CC * wdt) + (s * CC * wdt + o), CC * wdt)
                        D, wb = v3(xd[:, off(F)], F), bc(wt[:, off(1)], F)
                        gv, am, xc3 = v3(g[s][:, :], AROW), v3(amsg, F), v3(xc[:, :], F)
                        dve.wait_ge(g_full[s], i * (16 * CC) + 16 * CC * (PAIRS * r + 1))
                        copy(idxst[s][:, :], gdst[:, off(1, 2 * CC)]).then_inc(idx_staged, 1)
                        copy(srcst[:, :], srcf[:, off(1)]).then_inc(srcst_ready, 1)
                        if r == 0:
                            done(copy(D, gv[:, :, 0:F]))
                            dve.sem_inc(g_free, 1)
                            xn = layernorm(D, 0, i, 2, s, P, CC)
                            dve.wait_ge(arow_ready, i * 2 + (n + 1))
                            done(V.scalar_tensor_tensor(am, xn, 0.0, wb, ALU.max, ALU.mult))
                        else:
                            done(V.tensor_reduce(xc3, gv.rearrange("p t (b f) -> p t f b", f=F), axis=AX.X, op=ALU.add))
                            dve.sem_inc(g_free, 1)
                            dve.wait_ge(arow_ready, i * 2 + (n + 1))
                            done(V.tensor_tensor(am, xc3, wb, ALU.mult))
                        for q in range(TILES4):
                            batch = TILES4 * n + q
                            dve.wait_ge(dup_ready, i * (2 * TILES4) + (batch + 1))
                            V.tensor_tensor(v3(sel[:, 4 * q * P:4 * (q + 1) * P], P), v3(dup[(s + q) % 2][:, :], P),
                                            bc(srcst[:, 4 * q:4 * q + 4], P), ALU.is_equal).then_inc(sel_ready, 1)
                            dve.wait_ge(sel_ready, i * (2 * TILES4) + (batch + 3))
                            if r == 0:
                                done(V.tensor_tensor(lowsel, sel[:, 4 * q * P:4 * (q + 1) * P], low, ALU.mult))
                                done(V.tensor_reduce(rep[:, 4 * q:4 * q + 4], v3(lowsel, P), axis=AX.X, op=ALU.add))
                        if r == 0:
                            done(V.tensor_scalar(s1[:, :], srcst[:, :], pcol[:, :], None, ALU.subtract))
                            done(V.scalar_tensor_tensor(s1[:, :], rep[:, :], 0.0, s1[:, :], ALU.is_equal, ALU.mult))
                            done(V.tensor_scalar(s1[:, :], s1[:, :], pcol[:, :], None, ALU.add))
                            done(V.tensor_scalar(s1[:, :], s1[:, :], float(BLK), None, ALU.mult))
                            done(V.tensor_tensor(aidx[:, off(1)], s1[:, :], b4[:, :], ALU.add))
                        dve.sem_inc(amsg_ready, 1)
                        dve.wait_ge(arow_free, i * 2 + (n + 1))
                        copy(aidxst[s][:, :], aidx[:, off(1)]).then_inc(aidx_staged, 1)
                st.end(PAIRS, f"round {r}")

            with dve.Fori(0, PAIRS) as i:
                st.loop(i, 2 * per[TO_DST])
                for s in range(2):
                    off = lambda wdt, o=0: bass.ds(i * (2 * CC * wdt) + (s * CC * wdt + o), CC * wdt)
                    D, xc3 = v3(xd[:, off(F)], F), v3(xc[:, :], F)
                    dve.wait_ge(g_full[s], i * (16 * CC) + 16 * CC * (PAIRS * TO_DST + 1))
                    copy(idxst[s][:, :], gidx[:, off(1, 2 * CC)]).then_inc(idx_staged, 1)
                    done(V.tensor_reduce(xc3, g[s][:, :].rearrange("p (t b f) -> p t f b", f=F, b=BLK), axis=AX.X, op=ALU.add))
                    dve.sem_inc(g_free, 1)
                    done(V.tensor_tensor(D, D, xc3, ALU.add))
            st.end(PAIRS, f"round {TO_DST}")

            msg_tf = msg.rearrange("p (f t) -> p t f", t=CC)
            msg_ft = msg.rearrange("p (f t) -> p f t", t=CC)
            def step(r, i, c):
                s, n = c % 2, NCH * (r - R0) + c
                off = lambda wdt, o=0, c=c: bass.ds(i * (2 * CC * wdt) + (c * CC * wdt + o), CC * wdt)
                prev = off(F, 0, c - 1)
                gx = v3(g[s][:, 0:CC * ROW], ROW)
                gv = gx[:, :, 0:F]
                xc3 = v3(xc[:, :], F)
                ln_at = lambda side, c=c: (ln_no(r, side, c), i, 2 * len(LN[r]), 0)

                def scan(c):
                    s, n = c % 2, NCH * (r - R0) + c
                    done(V.scalar_tensor_tensor(msg_ft[:, :, 0], state[:, :], keep[:, bass.ds(i * 2 * CC + c * CC, 1)],
                                                msg_ft[:, :, 0], ALU.mult, ALU.add))
                    dve.wait_ge(km_ready, i * 2 + (n + 1))
                    dve.wait_ge(tout_free, i * 2 + (n + 1))
                    done(V.tensor_tensor_scan(sc[s], km[s], msg, 0.0, ALU.mult, ALU.add))
                    done(V.tensor_copy(state[:, :], sc[s].rearrange("p (f t) -> p f t", t=CC)[:, :, CC - 1]))
                    dve.sem_inc(scan_done, 1)

                if c < NCH:
                    cols = off(1)
                    X, D, wb = v3(xs[:, off(F)], F), v3(xd[:, off(F)], F), bc(wt[:, cols], F)
                    dve.wait_ge(g_full[s], i * (16 * CC) + 16 * CC * (PAIRS * r + c // 2 + 1))
                    copy(idxst[s][:, :], gidx[:, off(1, (COLS if r == R0 else 2 * COLS) + 2 * CC)]).then_inc(idx_staged, 1)
                    if r == R0:
                        done(copy(X, gv))
                        done(copy(ic_s[:, cols], gx[:, :, F + 1]))
                        done(copy(gidx[:, off(1, 2 * COLS)], gx[:, :, F]))
                    elif r == R0 + 2:
                        done(V.tensor_tensor(xc3, gv, bc(ic_s[:, cols], F), ALU.mult))
                        done(V.tensor_tensor(X, X, xc3, ALU.add))
                    elif r == R0 + 3:
                        done(V.tensor_tensor(X, X, gv, ALU.add))
                    if r != R0 + 1:
                        dve.sem_inc(g_free, 1)
                    xn = layernorm(X, *ln_at("S"), P, CC)
                    if r == R0:
                        done(V.tensor_scalar(msg_tf, xn, 0.0, None, ALU.max))
                    elif r == R0 + 1:
                        sage_in(xn, (gv, bc(ic_s[:, cols], F)), P, CC, i * 2 + (mm_base[r] + c + 1))
                        dve.wait_ge(ah_ready, i * 2 + (mm_base[r] + c + 1))
                        dve.sem_inc(g_free, 1)
                    elif r == R0 + 2:
                        dve.wait_ge(td_full, i * 2 + (c + 1))
                        done(V.scalar_tensor_tensor(xc3, xn, 0.0, v3(eat[s], F), ALU.max, ALU.add))
                        done(V.tensor_scalar(msg_tf, xc3, 0.0, None, ALU.max))
                        done(V.tensor_scalar(xn, xn, 0.0, eps1[:, :], ALU.max, ALU.mult))
                        done(V.tensor_tensor(X, X, xn, ALU.add))
                    else:
                        done(V.scalar_tensor_tensor(msg_tf, xn, 0.0, wb, ALU.max, ALU.mult))
                    if r != R0 + 1:
                        scan(c)
                if c:
                    if r == R0 + 1:
                        sage_root(v3(xs[:, prev], F), 1, P, CC, i * (2 * QE) + (QE * (mm_base[r] + c) + 2), msg_tf)
                        scan(c - 1)
                    elif r == R0 + 2:
                        sage_root(v3(xd[:, prev], F), None, P, CC, i * (2 * QE) + (QE * (mm_base[r] + c) + 2))
                    else:
                        nodes_2((c - 1) % 2, i, ln_at("n", c - 1), mm_base[r] + c - 1, CC)
                if c < NCH and r in ALL_NODES:
                    nodes_1(s, i, (ALL_NODES[r] and NCH + 1) + c, ln_at("N"), mm_base[r] + c, CC)
                elif c < NCH and r == R0 + 2:
                    xn = layernorm(D, *ln_at("D"), P, CC)
                    sage_in(xn, (v3(td[s], F), bc(ic_d[:, cols], F)), P, CC, i * 2 + (mm_base[r] + c + 1))
                    dve.wait_ge(ah_ready, i * 2 + (mm_base[r] + c + 1))
                    dve.sem_inc(td_free, 1)

            for r in range(R0, ROUNDS):
                done(V.memset(state[:, :], 0.0))
                if r == R0 + 3:
                    done(V.memset(ah[:, :], 0.0))
                step(r, 0, 0)
                with dve.Fori(0, PAIRS - 1) as i:
                    st.loop(i, 2 * per[r])
                    step(r, i, 1)
                    step(r, i, 2)
                st.end(PAIRS - 1, f"round {r}")
                step(r, 0, NCH - 1)
                step(r, 0, NCH)
                if r == R0:
                    done(V.tensor_copy(gidx[:, 3 * COLS:], gidx[:, 2 * COLS:2 * COLS + 2 * CC]))
                    nodes_1(0, 0, NCH, (ln_base["last"], 0, 0, 0), mm_base["last"], DC_LAST)
                    nodes_2(0, 0, (ln_base["last"], 0, 0, 1), mm_base["last"], DC_LAST)
                dve.sem_inc(cl_ready, 1)
                carries(r - R0 + 1)
                dve.sem_inc(carry_ready, 1)

            dve.sem_inc(rows_free, 1)
            with dve.Fori(0, PAIRS) as i:
                st.loop(i, 2 * per[ROUNDS])
                for s in range(2):
                    if s == 0:
                        dve.wait_ge(rows_free, i + 1)
                    cols = bass.ds(i * 2 * CC + s * CC, CC)
                    D, xc3 = v3(xd[:, bass.ds(i * (2 * W) + s * W, W)], F), v3(xc[:, :], F)
                    dve.wait_ge(td_full, i * 2 + (NCH + s + 1))
                    done(V.tensor_tensor(xc3, v3(td[s], F), bc(ic_d[:, cols], F), ALU.mult))
                    done(V.tensor_tensor(D, D, xc3, ALU.add))
                    xn = layernorm(D, ln_base[ROUNDS], i, 2, s, P, CC)
                    done(V.tensor_scalar(xn, xn, 0.0, eps1[:, :], ALU.max, ALU.mult))
                    done(V.tensor_tensor(D, D, xn, ALU.add))
                    done(V.tensor_tensor(D, D, v3(eat[s], F), ALU.add))
                    done(V.tensor_tensor(v3(g[s][:, 0:CC * ROW], ROW)[:, :, 0:F], D, v3(fin[s], F), ALU.add))
                    dve.sem_inc(rows_ready, 1)
                    dve.sem_inc(td_free, 1)
            st.end(PAIRS, f"round {ROUNDS}")


_INS = ['x', 'src', 'dst', 'edge_attr_32', 'edge_weight', 'L1_gnn_W1_l', 'L1_gnn_b1', 'L1_gnn_W1_r',
        'L1_gnn_W2_l', 'L1_gnn_b2', 'L1_gnn_W2_r', 'L2_gnn_eps']
_OUTS = [((100000, 32), 'float32')]


def kernel(**inputs):
    import numpy as _np
    import concourse.bacc as _bacc
    from concourse import mybir as _mybir
    from concourse.bass_utils import run_bass_kernel_spmd as _run

    nc = _bacc.Bacc("TRN2", target_bir_lowering=False, num_devices=1)
    arrays, args = {}, []
    for name in _INS:
        a = _np.ascontiguousarray(inputs[name])
        arrays[f"in_{name}_dram"] = a
        args.append(nc.dram_tensor(f"in_{name}_dram", a.shape, _mybir.dt.from_np(a.dtype), kind="ExternalInput").ap())
    for i, (shape, dtype) in enumerate(_OUTS):
        dt = _mybir.dt.from_np(_np.dtype(dtype))
        args.append(nc.dram_tensor(f"out_{i}_dram", shape, dt, kind="ExternalOutput").ap())
    gnn_kernel(nc, *args)
    r = _run(nc, [arrays], core_ids=[0])
    return r.results[0]["out_0_dram"]
```

```python
import concourse.bass as bass
from concourse import mybir
from contextlib import ExitStack

FP32 = mybir.dt.float32
I32 = mybir.dt.int32
BF16 = mybir.dt.bfloat16
ALU = mybir.AluOpType
ACT = mybir.ActivationFunctionType
AX = mybir.AxisListType

P = 128
N, F = 100000, 32
E = 50000
HID = 64
COLS = -(-E // (P * 28)) * 28
EP = P * COLS
CC = 28
NCH = COLS // CC
PAIRS = NCH // 2
FULL_P = E // COLS
REST = E - FULL_P * COLS
ROW = F + 2
ZROWS = 80
CARRY_ROWS = EP
ZERO_ROW = EP + P
TROWS = EP + P + ZROWS
NP_, NPP = 125, 800
NOWHERE = float(1 << 20)
SB = 6250
LN_EPS = 1e-5
ADDS = 3
TO_DST = ADDS
R0 = ADDS + 1
ROUNDS = R0 + 4
BLK = 2
AROW = BLK * F
AROWS = -(-(N + P) // (P * PAIRS)) * P * PAIRS
CLEARS = 2 * NCH
ZW = AROWS * AROW // P // CLEARS
NB = 40
PER_ROW = CC // BLK
TILES4 = CC // 4
DC_LAST = NPP - 2 * NCH * CC


class Steps:

    def __init__(self, eng, sem):
        self.eng, self.sem, self.base, self.reg, self.per, self.n = eng, sem, 0, None, 0, 0

    def loop(self, reg, per):
        self.reg, self.per, self.n = reg, per, 0

    def end(self, times, where):
        assert self.n == self.per, (where, self.n, self.per)
        self.base, self.reg, self.n = self.base + times * self.per, None, 0

    def done(self, ins):
        ins.then_inc(self.sem, 1)
        self.n += 1
        self.eng.wait_ge(self.sem, self.base + self.n if self.reg is None else self.reg * self.per + (self.base + self.n))
        if self.reg is None:
            self.base, self.n = self.base + self.n, 0


def gnn_kernel(nc, x, src, dst, ea, w, W1l, b1, W1r, W2l, b2, W2r, eps, out):
    with ExitStack() as ctx:
        def sb(name, shape, dt=FP32):
            return ctx.enter_context(nc.sbuf_tensor(name, shape, dt))

        def ps(name, shape):
            return ctx.enter_context(nc.psum_tensor(name, shape, FP32))

        def sem(name):
            return ctx.enter_context(nc.semaphore(name))

        adds = [nc.dram_tensor(f"adds{r}", [AROWS * BLK, F], FP32) for r in range(ADDS)]
        by_node = [a[:, :].rearrange("(n b) f -> n (b f)", b=BLK) for a in adds]
        node_tab = nc.dram_tensor("node_tab", [N, ROW], FP32)
        sums = {r: nc.dram_tensor(f"sums{r}", [TROWS, F], FP32) for r in range(R0, ROUNDS)}
        ea_pad = nc.dram_tensor("ea_pad", [EP, F], FP32)
        ea_perm = nc.dram_tensor("ea_perm", [EP, F], FP32)
        rec_perm = nc.dram_tensor("rec_perm", [EP, 4], I32)

        xs = sb("xs", [P, COLS * F])
        xd = sb("xd", [P, COLS * F])
        W = CC * F
        late = sb("late", [P, 7 * W + 3 * COLS])
        cut = lambda k, n=1: late[:, k * W:(k + n) * W]
        msg, km, sc, tout = cut(0), [cut(1), cut(2)], [cut(3), cut(4)], [cut(5), cut(6)]
        zeros = late[:, 0:ZW]
        prep = [late[:, 7 * W + k * COLS:7 * W + (k + 1) * COLS] for k in range(3)]
        last, cnt, ones = prep
        nx = [late[:, k * NB * F:(k + 1) * NB * F] for k in range(2)]
        npos = late[0:NP_, 2 * NB * (F + ROW):2 * NB * (F + ROW) + 2 * NPP]
        dst_hi, dst_lo, carry_over = prep
        nt = [late[:, 2 * NB * F + k * NB * ROW:2 * NB * F + (k + 1) * NB * ROW] for k in range(2)]
        sel = xs[:, 0:CC * P]
        arow = [xs[:, CC * P + k * W:CC * P + (k + 1) * W] for k in range(2)]
        low = xs[:, CC * P + 2 * W:CC * P + 2 * W + 4 * P]
        lowsel = xs[:, CC * P + 2 * W + 4 * P:CC * P + 2 * W + 8 * P]
        amsg = xs[:, CC * P + 2 * W + 8 * P:CC * P + 3 * W + 8 * P]
        o = CC * P + 3 * W + 8 * P
        seq = xs[:, o:o + NPP]
        zpos = xs[:, o + NPP:o + 2 * NPP]
        ncnt, nrank, nones = (xs[0:NP_, o + k * NPP:o + (k + 1) * NPP] for k in (2, 3, 4))
        hot_lo = [xs[:, o + 5 * NPP + k * NPP // 2:o + 5 * NPP + (k + 1) * NPP // 2].bitcast(BF16) for k in range(2)]
        na = [xs[:, k * NB * AROW:(k + 1) * NB * AROW] for k in range(2)]
        src_i, dst_i = sb("src_i", [P, COLS], I32), sb("dst_i", [P, COLS], I32)
        wt = sb("wt", [P, COLS])
        keep, keepz = sb("keep", [P, COLS]), sb("keepz", [P, COLS])
        pm = sb("pm", [P, COLS])
        ic_s = sb("ic_s", [P, COLS])
        ic_d = sb("ic_d", [P, COLS])
        epos = sb("epos", [P, COLS])
        sidx = sb("sidx", [P, COLS])
        gdst = sb("gdst", [P, COLS + 2 * CC])
        gidx = sb("gidx", [P, 3 * COLS + 2 * CC])
        aidx = sb("aidx", [P, COLS])
        idxst = [sb(f"idxst{s}", [P, CC], I32) for s in range(2)]
        aidxst = [sb(f"aidxst{s}", [P, CC], I32) for s in range(2)]
        srcst = sb("srcst", [P, CC])
        b4, rep = sb("b4", [P, CC]), sb("rep", [P, CC])
        g = [sb(f"g{s}", [P, CC * max(AROW, ROW + 2 * F)]) for s in range(2)]
        dprev, dnext = (g[1][:, 2 * W + k * COLS:2 * W + (k + 1) * COLS].bitcast(I32) for k in range(2))
        td = [g[s][:, CC * ROW:CC * ROW + W] for s in range(2)]
        eat = [g[s][:, CC * ROW + W:CC * ROW + 2 * W] for s in range(2)]
        state = sb("state", [P, F])
        carry = sb("carry", [P, F])
        carry_t = sb("carry_t", [F, P + 1])
        last_t = sb("last_t", [F, P])
        pm_t = sb("pm_t", [F, P])
        pm_b = sb("pm_b", [P, F])
        cidx_f, cidx = sb("cidx_f", [P, 1]), sb("cidx", [P, 1], I32)
        small = sb("small", [P, 8])
        flag = sb("flag", [1, 1], I32)
        xc, sq = sb("xc", [P, W]), sb("sq", [P, W])
        s1, mean = sb("s1", [P, CC]), sb("mean", [P, CC])
        var, sd, rs = sb("var", [P, CC]), sb("sd", [P, CC]), sb("rs", [P, CC])
        ah = sb("ah", [P, CC * 2 * F])
        aht, h1t = [sb(f"aht{k}", [P, 512]) for k in range(2)], [sb(f"h1t{k}", [P, 512]) for k in range(2)]
        w1b, w2b = sb("w1b", [P, P]), sb("w2b", [P, P])
        b1b, b2b, eps1, lneps = sb("b1b", [P, 1]), sb("b2b", [P, F]), sb("eps1", [P, 1]), sb("lneps", [P, 1])
        ident = sb("ident", [P, P])
        zrow = sb("zrow", [P, F])
        dn = eat
        fin = sc
        hot_hi = [sb(f"hot_hi{k}", [P, NP_ + 1], BF16) for k in range(2)]
        ocol, pcol = sb("ocol", [P, 1]), sb("pcol", [P, 1])

        tp, m1 = [ps(f"tp{k}", [P, 512]) for k in range(2)], [ps(f"m1{k}", [P, 512]) for k in range(2)]
        cp = m1[1]
        m2 = ps("m2", [P, 2048])
        dup = tp

        edges_in, edges_0 = sem("edges_in"), sem("edges_0")
        weights_in, weights_0, consts = sem("weights_in"), sem("weights_0"), sem("consts")
        prev_in, next_in, dst_ready = sem("prev_in"), sem("next_in"), sem("dst_ready")
        bad_ready, bad_sum, flag_ready = sem("bad_ready"), sem("bad_sum"), sem("flag_ready")
        ea_copied, zeros_in, zero_rows = sem("ea_copied"), sem("zeros_in"), sem("zero_rows")
        iotas, sort_in, ranks_ready, block_used, sorted_ready = (sem("iotas"), sem("sort_in"), sem("ranks_ready"),
                                                                 sem("block_used"), sem("sorted_ready"))
        sort_dma, rank_steps = sem("sort_dma"), sem("rank_steps")
        dve_s, pool_s = sem("dve_s"), sem("pool_s")
        adds_clear = [sem(f"adds_clear{r}") for r in range(ADDS)]
        adds_done = [sem(f"adds_done{b}") for b in range(BLK)]
        low_ready, srcst_ready, dup_ready, sel_ready, amsg_ready, merged, arow_ready, arow_free = (
            sem("low_ready"), sem("srcst_ready"), sem("dup_ready"), sem("sel_ready"), sem("amsg_ready"), sem("merged"),
            sem("arow_ready"), sem("arow_free"))
        aidx_staged, added = sem("aidx_staged"), sem("added")
        seq_ready, hot_0, hist_0, hot_ready, hot_used = (sem("seq_ready"), sem("hot_0"), sem("hist_0"), sem("hot_ready"),
                                                         sem("hot_used"))
        totals_ready, after_ready, npos_ready = sem("totals_ready"), sem("after_ready"), sem("npos_ready")
        nx_in = [sem(f"nx_in{s}") for s in range(2)]
        nsum_ready, nsum_used, nt_ready, nt_out = sem("nsum_ready"), sem("nsum_used"), sem("nt_ready"), sem("nt_out")
        node_ready = sem("node_ready")
        dn_dma, dn_in, dn_done, dn_out = sem("dn_dma"), sem("dn_in"), sem("dn_done"), sem("dn_out")
        var_ready, sd_ready = sem("var_ready"), sem("sd_ready")
        ah_ready, tp_ready, aht_ready, m1_ready, h1t_ready, m2_free = (
            sem("ah_ready"), sem("tp_ready"), sem("aht_ready"), sem("m1_ready"), sem("h1t_ready"), sem("m2_free"))
        ah_free, h1t_used = sem("ah_free"), sem("h1t_used")
        g_full = [sem(f"g_full{s}") for s in range(2)]
        g_free, idx_staged = sem("g_free"), sem("idx_staged")
        km_ready, scan_done, tout_ready, tout_free = sem("km_ready"), sem("scan_done"), sem("tout_ready"), sem("tout_free")
        tout_dma = sem("tout_dma")
        td_dma, td_full, td_free = sem("td_dma"), sem("td_full"), sem("td_free")
        last_dma, last_full = sem("last_dma"), sem("last_full")
        cl_ready, clt_ready, ct_ready, cc_ready, carry_ready, carry_done = (
            sem("cl_ready"), sem("clt_ready"), sem("ct_ready"), sem("cc_ready"), sem("carry_ready"), sem("carry_done"))
        rows_ready, out_dma = sem("rows_ready"), [sem(f"out_dma{s}") for s in range(2)]

        LN = {0: "D", R0: "SNn", R0 + 1: "S", R0 + 2: "SD", R0 + 3: "SNn", ROUNDS: "D"}
        MM = {R0: "N", R0 + 1: "S", R0 + 2: "D", R0 + 3: "N"}
        ALL_NODES = {R0: 0, R0 + 3: NCH}
        ln_base, mm_base = {}, {}
        a, b = 0, 0
        for r in range(ROUNDS + 1):
            ln_base[r], mm_base[r] = a, b
            a, b = a + NCH * len(LN.get(r, "")), b + NCH * len(MM.get(r, ""))
            if r == R0:
                ln_base["last"], mm_base["last"] = a, b
                a, b = a + 2, b + 1
        BATCHES = {CC: (4, 4, 4, 2), DC_LAST: (2, 2, 2, 2)}
        QE = 4

        def ln_no(r, side, c0):
            if r in ALL_NODES and side == "n":
                return ln_base[r] + 3 * c0 + (3 if c0 < NCH - 1 else 2)
            if r in ALL_NODES:
                return ln_base[r] + (0 if c0 == 0 else 2 + 3 * (c0 - 1)) + (0 if side == "S" else 1 if c0 == 0 else 2)
            return ln_base[r] + len(LN[r]) * c0 + LN[r].index(side)

        def cleared(table):
            return table[:, :].rearrange("(p n) f -> p (n f)", p=P)

        def v3(ap, inner):
            return ap.rearrange("p (t f) -> p t f", f=inner)

        def bc(ap, n, parts=P):
            return ap.unsqueeze(2).to_broadcast([parts, ap.shape[1], n])

        block = ctx.enter_context(nc.Block())

        @block.sync
        def _(sp):
            sp.wait_ge(edges_0, 3)
            for tile, dram in ((src_i, src), (dst_i, dst), (wt, w)):
                sp.dma_start(tile[0:FULL_P, :], dram[0:FULL_P * COLS].rearrange("(p t) -> p t", t=COLS)).then_inc(edges_in, 16)
                sp.dma_start(tile[FULL_P:FULL_P + 1, 0:REST],
                             dram[FULL_P * COLS:E].rearrange("(p t) -> p t", p=1)).then_inc(edges_in, 16)
            sp.wait_ge(weights_0, 1)
            for t in range(2):
                o = t * 2 * F
                sp.dma_start(w1b[o:o + F, t * HID:(t + 1) * HID], W1l).then_inc(weights_in, 16)
                sp.dma_start(w1b[o + F:o + 2 * F, t * HID:(t + 1) * HID], W1r).then_inc(weights_in, 16)
                sp.dma_start(w2b[t * HID:(t + 1) * HID, o:o + F], W2l).then_inc(weights_in, 16)
                sp.dma_start(w2b[t * HID:(t + 1) * HID, o + F:o + 2 * F], W2r).then_inc(weights_in, 16)
                sp.dma_start(b1b[t * HID:(t + 1) * HID, :], b1.rearrange("(p a) -> p a", a=1)).then_inc(weights_in, 16)
            sp.dma_start(b2b[:, :], b2.rearrange("(a f) -> a f", a=1).to_broadcast([P, F])).then_inc(weights_in, 16)
            sp.dma_start(eps1[:, :], eps.rearrange("(a f) -> a f", a=1).to_broadcast([P, 1])).then_inc(weights_in, 16)

            sp.wait_ge(dst_ready, 1)
            sp.dma_start(dprev[1:P, 0:1], dst_i[0:P - 1, COLS - 1:COLS]).then_inc(prev_in, 16)
            sp.wait_ge(zeros_in, 2)
            sp.dma_start(ea_pad[0:E, :], ea).then_inc(ea_copied, 16)
            sp.dma_start(ea_pad[E:E + P, :], zrow[:, :]).then_inc(ea_copied, 16)
            sp.dma_start(ea_pad[E + P:EP, :], zrow[0:EP - E - P, :]).then_inc(ea_copied, 16)
            sp.wait_ge(dst_ready, 2)
            sp.dma_start(dprev[1:P, 0:1], dst_i[0:P - 1, COLS - 1:COLS]).then_inc(prev_in, 16)
            sp.dma_start(dnext[0:P - 1, COLS - 1:COLS], dst_i[1:P, 0:1]).then_inc(next_in, 16)
            for t in sums.values():
                sp.dma_start(t[ZERO_ROW:TROWS, :], zrow[0:ZROWS, :]).then_inc(zero_rows, 16)
                sp.dma_start(t[CARRY_ROWS:CARRY_ROWS + P, :], zrow[:, :]).then_inc(zero_rows, 16)
            for r in range(ADDS - 1):
                av = cleared(adds[r + 1])
                with sp.Fori(0, PAIRS) as i:
                    for c in range(2):
                        sp.wait_ge(amsg_ready, i * 2 + (NCH * r + c + 1))
                        for k in range(2 * c, 2 * c + 2):
                            sp.dma_start(av[:, bass.ds(i * (4 * ZW) + k * ZW, ZW)], zeros).then_inc(adds_clear[r + 1], 16)
                            sp.wait_ge(adds_clear[r + 1], i * 64 + 16 * (k + 1))
                            sp.nop(nofuse=True)

            sp.wait_ge(added, ADDS)
            xv, tv = x.rearrange("(p n) f -> p n f", p=NP_), node_tab[:, :].rearrange("(p n) f -> p n f", p=NP_)
            av = by_node[ADDS - 1][0:N, :].rearrange("(p n) f -> p (n f)", p=NP_)
            with sp.Fori(0, NPP // NB // 2) as i:
                for s in range(2):
                    n = bass.ds(i * 2 * NB + s * NB, NB)
                    sp.wait_ge(nt_ready, i * 2 + (s + 1))
                    sp.dma_start(na[s][0:NP_, :], av[:, bass.ds(i * (2 * NB * AROW) + s * NB * AROW, NB * AROW)]).then_inc(nx_in[s], 16)
                    sp.dma_start(v3(nx[s][0:NP_, :], F), xv[:, n, :]).then_inc(nx_in[s], 16)

            ov = out.rearrange("(p n) f -> p n f", p=NP_)

            def cols_of(t):
                return t[0:EP, :].rearrange("(p t) f -> p (t f)", p=P)

            def load_nodes(s, nodes, width, i, k):
                sp.dma_start(v3(dn[s][0:NP_, 0:width * F], F), tv[:, nodes, 0:F]).then_inc(dn_dma, 16)
                sp.wait_ge(dn_dma, i * 32 + 16 * (k + 1))
                sp.sem_inc(dn_in, 1)

            def store_nodes(s, nodes, width, i, k):
                sp.wait_ge(dn_done, i * 2 + (k + 1))
                sp.dma_start(ov[:, nodes, :], v3(dn[s][0:NP_, 0:width * F], F)).then_inc(dn_out, 16)
                sp.wait_ge(dn_out, i * 32 + 16 * (k + 1))

            def store_sums(r, i, c):
                sp.wait_ge(tout_ready, i * 2 + (NCH * (r - R0) + c + 1))
                sp.dma_start(cols_of(sums[r])[:, bass.ds(i * (2 * W) + c * W, W)], tout[c % 2]).then_inc(tout_dma, 16)
                sp.wait_ge(tout_dma, i * 32 + 16 * (NCH * (r - R0) + c + 1))
                sp.sem_inc(tout_free, 1)

            def nodes_of(r, i, c):
                return bass.ds(i * (2 * CC) + (ALL_NODES[r] + c) * CC, CC)

            def step(r, i, c):
                s, k = c % 2, (ALL_NODES.get(r, 0) and NCH + 1) + c
                at = bass.ds(i * (2 * W) + c * W, W)
                if r in ALL_NODES:
                    load_nodes(s, nodes_of(r, i, c), CC, i, k)
                if r == R0 + 2:
                    sp.wait_ge(td_free, i * 2 + (c + 1))
                    sp.dma_start(td[s], cols_of(sums[R0])[:, at]).then_inc(td_dma, 16)
                    sp.dma_start(eat[s], cols_of(ea_pad)[:, at]).then_inc(td_dma, 16)
                    sp.wait_ge(td_dma, i * 64 + 32 * (c + 1))
                    sp.sem_inc(td_full, 1)
                if r != R0 + 1:
                    store_sums(r, i, c)
                elif c:
                    store_sums(r, i, c - 1)
                if r in ALL_NODES and c:
                    store_nodes((c - 1) % 2, nodes_of(r, i, c - 1), CC, i, k - 1)
                sp.nop(nofuse=True)

            for r in range(R0, ROUNDS):
                if r == R0:
                    sp.wait_ge(node_ready, 1)
                    sp.wait_ge(g_free, NCH * R0 + 2)
                step(r, 0, 0)
                with sp.Fori(0, PAIRS - 1) as i:
                    step(r, i, 1)
                    step(r, i, 2)
                step(r, 0, NCH - 1)
                if r == R0 + 1:
                    store_sums(r, 0, NCH - 1)
                if r in ALL_NODES:
                    store_nodes(1, nodes_of(r, 0, NCH - 1), CC, 0, (ALL_NODES[r] and NCH + 1) + NCH - 1)
                if r == R0:
                    nodes = slice(NPP - DC_LAST, NPP)
                    load_nodes(0, nodes, DC_LAST, 0, NCH)
                    store_nodes(0, nodes, DC_LAST, 0, NCH)
            def load_sage(i, c):
                sp.wait_ge(td_free, i * 2 + (NCH + c + 1))
                sp.dma_start(td[c % 2], cols_of(sums[R0 + 1])[:, bass.ds(i * (2 * W) + c * W, W)]).then_inc(td_dma, 16)
                sp.wait_ge(td_dma, i * 32 + (32 * NCH + 16 * (c + 1)))
                sp.sem_inc(td_full, 1)

            def load_last(i, c):
                for tile, r in ((eat[c % 2], R0 + 2), (fin[c % 2], R0 + 3)):
                    sp.dma_start(tile, cols_of(sums[r])[:, bass.ds(i * (2 * W) + c * W, W)]).then_inc(last_dma, 16)
                sp.wait_ge(last_dma, i * 64 + 32 * (c + 1))
                sp.sem_inc(last_full, 1)

            load_sage(0, 0)
            load_sage(0, 1)
            sp.wait_ge(carry_done, 64)
            load_last(0, 0)
            load_last(0, 1)
            with sp.Fori(0, PAIRS - 1) as i:
                for c in (2, 3):
                    load_sage(i, c)
                    load_last(i, c)
                sp.nop(nofuse=True)
            for s in range(2):
                sp.wait_ge(out_dma[s], 16 * CC * PAIRS)

        @block.gpsimd
        def _(pool):
            st = Steps(pool, pool_s)
            pool.iota(epos[:, :], [[1, COLS]], base=0, channel_multiplier=COLS, allow_small_or_imprecise_dtypes=True).then_inc(iotas, 1)
            st.done(pool.memset(ident[:, :], 0.0))
            pool.affine_select(out=ident[:, :], in_=ident[:, :], compare_op=ALU.not_equal, fill=1.0, base=0,
                               pattern=[[-1, P]], channel_multiplier=1).then_inc(consts, 1)
            pool.iota(ocol[:, :], [[0, 1]], base=CARRY_ROWS, channel_multiplier=1, allow_small_or_imprecise_dtypes=True).then_inc(iotas, 1)
            pool.iota(b4[:, :], [[0, PER_ROW], [1, BLK]], base=0, channel_multiplier=0, allow_small_or_imprecise_dtypes=True).then_inc(iotas, 1)
            pool.iota(pcol[:, :], [[0, 1]], base=N, channel_multiplier=1, allow_small_or_imprecise_dtypes=True).then_inc(iotas, 1)

            pool.wait_ge(flag_ready, 1)
            bad = pool.value_load(flag[0:1, 0:1], min_val=0, max_val=1)
            with pool.If(bad > 0):
                fb = Steps(pool, sort_in)
                pool.wait_ge(ea_copied, 48)
                db = xs[:, 0:SB].bitcast(I32)
                gi = xs[:, 2 * SB - SB:2 * SB].bitcast(I32)
                fb.done(pool.iota(gi, [[1, SB]], base=0, channel_multiplier=0))
                for k in range(E // SB):
                    if k:
                        pool.wait_ge(block_used, k)
                    pool.dma_start(db, dst[k * SB:(k + 1) * SB].rearrange("(a f) -> a f", a=1).to_broadcast([P, SB])).then_inc(sort_dma, 16)
                    pool.wait_ge(sort_dma, 16 * (k + 1))
                pool.wait_ge(ranks_ready, 1)
                rank, rec = xs[:, 0:COLS], xs[:, COLS:COLS + CC * 4]
                ear, ri = xs[:, 2 * COLS:2 * COLS + CC * F], idxst[0]
                rec3 = v3(rec, 4)
                fb.done(pool.memset(rec, 0.0))
                eav = ea_pad[:, :].rearrange("(p t) f -> p (t f)", p=P)
                dbase = 16 * (E // SB)
                moved = 16 * (2 * CC + 1)
                with pool.Fori(0, NCH) as i:
                    fb.loop(i, 4)
                    cols = bass.ds(i * CC, CC)
                    pool.dma_start(ear, eav[:, bass.ds(i * (CC * F), CC * F)]).then_inc(sort_dma, 16)
                    fb.done(pool.tensor_copy(ri[:, :], rank[:, cols]))
                    fb.done(pool.tensor_copy(rec3[:, :, 0].bitcast(I32), src_i[:, cols]))
                    fb.done(pool.tensor_copy(rec3[:, :, 1].bitcast(I32), dst_i[:, cols]))
                    fb.done(pool.tensor_copy(rec3[:, :, 2], wt[:, cols]))
                    pool.wait_ge(sort_dma, i * moved + (dbase + 16))
                    pool.nop(nofuse=True)
                    for k in range(CC):
                        at = bass.IndirectOffsetOnAxis(ri[:, k:k + 1], 0)
                        pool.indirect_dma_start(ea_perm[:, :], at, ear[:, k * F:(k + 1) * F], None).then_inc(sort_dma, 16)
                        pool.indirect_dma_start(rec_perm[:, :], at, rec[:, 4 * k:4 * k + 4].bitcast(I32), None).then_inc(sort_dma, 16)
                    pool.wait_ge(sort_dma, i * moved + (dbase + moved))
                    pool.nop(nofuse=True)
                fb.end(NCH, "sort")
                total = dbase + moved * NCH
                pool.dma_start(ea_pad[:, :], ea_perm[:, :]).then_inc(sort_dma, 16)
                pool.dma_start(xd[:, 0:4 * COLS].bitcast(I32), rec_perm[:, :].rearrange("(p t) f -> p (t f)", p=P)).then_inc(sort_dma, 16)
                pool.wait_ge(sort_dma, total + 32)
                got = v3(xd[:, 0:4 * COLS], 4)
                fb.done(pool.tensor_copy(src_i[:, :], got[:, :, 0].bitcast(I32)))
                fb.done(pool.tensor_copy(dst_i[:, :], got[:, :, 1].bitcast(I32)))
                fb.done(pool.tensor_copy(wt[:, :], got[:, :, 2]))
            pool.drain().then_inc(sorted_ready, 1)

            def start_gather(r, i, c):
                pool.wait_ge(idx_staged, i * 2 + (NCH * r + c + 1))
                pool.wait_ge(g_free, i * 2 + (NCH * r + c + 1))
                pool.nop(nofuse=True)

            def gather_column(r, s, k):
                tab, width, pitch = ((x[:, :], F, AROW) if r == 0 else (by_node[r - 1], AROW, AROW) if r <= TO_DST
                                     else (node_tab[:, :], ROW, ROW) if r == R0 else (sums[r - 1][:, :], F, ROW))
                pool.indirect_dma_start(g[s][:, k * pitch:k * pitch + width], None, tab,
                                        bass.IndirectOffsetOnAxis(idxst[s][:, k:k + 1], 0)).then_inc(g_full[s], 16)

            def gather(r, i, c):
                start_gather(r, i, c)
                for k in range(CC):
                    gather_column(r, c % 2, k)

            def start_add(r, i, c):
                n = NCH * r + c
                pool.wait_ge(aidx_staged, i * 2 + (n + 1))
                pool.wait_ge(arow_ready, i * 2 + (n + 2))
                pool.nop(nofuse=True)

            def add_column(r, i, c, k):
                n, s, b = NCH * r + c, c % 2, k % BLK
                if n or k >= BLK:
                    pool.wait_ge(adds_done[b], i * (32 * PER_ROW) + 16 * (PER_ROW * n + k // BLK))
                    pool.nop(nofuse=True)
                if c and k == BLK - 1:
                    pool.sem_inc(arow_free, 1)
                pool.indirect_dma_start(adds[r][:, :], bass.IndirectOffsetOnAxis(aidxst[s][:, k:k + 1], 0),
                                        arow[s][:, k * F:(k + 1) * F], None, bounds_check=AROWS * BLK - 1,
                                        oob_is_err=True, compute_op=ALU.add).then_inc(adds_done[b], 16)

            def add_and_gather(r, i, c):
                start_gather(r, i, c + 2)
                start_add(r, i, c)
                for k in range(CC):
                    gather_column(r, c % 2, k)
                    add_column(r, i, c, k)

            for r in range(ADDS):
                gather(r, 0, 0)
                if r == 0:
                    st.done(pool.memset(low, 1.0))
                    pool.affine_select(out=v3(low, P), in_=v3(low, P), compare_op=ALU.is_gt, fill=0.0, base=0,
                                       pattern=[[0, 4], [-1, P]], channel_multiplier=1).then_inc(low_ready, 1)
                    pool.iota(seq, [[1, NPP]], base=0, channel_multiplier=0, allow_small_or_imprecise_dtypes=True).then_inc(seq_ready, 1)
                    pool.iota(v3(zpos, ZROWS), [[0, NPP // ZROWS], [1, ZROWS]], base=ZERO_ROW, channel_multiplier=0,
                              allow_small_or_imprecise_dtypes=True).then_inc(seq_ready, 1)
                gather(r, 0, 1)
                pool.wait_ge(adds_clear[r], 16 * CLEARS)
                add_and_gather(r, 0, 0)
                add_and_gather(r, 0, 1)
                with pool.Fori(0, PAIRS - 2) as i:
                    add_and_gather(r, i, 2)
                    add_and_gather(r, i, 3)
                for c in range(NCH - 2, NCH):
                    start_add(r, 0, c)
                    for k in range(CC):
                        add_column(r, 0, c, k)
                for b in range(BLK):
                    pool.wait_ge(adds_done[b], 16 * PER_ROW * NCH * (r + 1))
                pool.sem_inc(arow_free, 1)
                pool.sem_inc(added, 1)

            for r in range(TO_DST, ROUNDS):
                if r == R0:
                    pool.wait_ge(nt_out, 16 * (NPP // NB))
                    pool.sem_inc(node_ready, 1)
                with pool.Fori(0, PAIRS) as i:
                    for s in range(2):
                        gather(r, i, s)
                if r >= R0:
                    if r == R0:
                        pool.wait_ge(zero_rows, 32 * len(sums))
                    pool.wait_ge(carry_ready, r - R0 + 1)
                    pool.wait_ge(tout_dma, 16 * NCH * (r - R0 + 1))
                    pool.indirect_dma_start(sums[r][:, :], bass.IndirectOffsetOnAxis(cidx[:, :], 0),
                                            carry[:, :], None, bounds_check=TROWS - 1, oob_is_err=True,
                                            compute_op=ALU.add).then_inc(carry_done, 16)
                    pool.wait_ge(carry_done, 16 * (r - R0 + 1))

            pool.wait_ge(dn_out, 16 * (2 * NCH + 1))
            pool.wait_ge(idx_staged, NCH * ROUNDS + 2)
            for s in range(2):
                pool.wait_ge(g_full[s], 16 * CC * PAIRS * ROUNDS)
            def put_rows(i, c):
                s = c % 2
                if c >= 2:
                    pool.wait_ge(out_dma[s], i * (16 * CC) + 16 * CC)
                    pool.nop(nofuse=True)
                st.done(pool.tensor_copy(idxst[s][:, :], sidx[:, bass.ds(i * 2 * CC + c * CC, CC)]))
                pool.wait_ge(rows_ready, i * 2 + (c + 1))
                pool.nop(nofuse=True)
                for k in range(CC):
                    pool.indirect_dma_start(out[:, :], bass.IndirectOffsetOnAxis(idxst[s][:, k:k + 1], 0),
                                            g[s][:, k * ROW:k * ROW + F], None,
                                            bounds_check=N - 1, oob_is_err=False).then_inc(out_dma[s], 16)

            put_rows(0, 0)
            put_rows(0, 1)
            with pool.Fori(0, PAIRS - 1) as i:
                st.loop(i, 2)
                put_rows(i, 2)
                put_rows(i, 3)
            st.end(PAIRS - 1, "out rows")
            for s in range(2):
                pool.wait_ge(out_dma[s], 16 * CC * PAIRS)

        @block.scalar
        def _(act):
            def root(base, i, per, j, parts, cols):
                act.wait_ge(var_ready, i * per + (base + j + 1))
                nc.scalar.activation(sd[0:parts, 0:cols], var[0:parts, 0:cols], ACT.Sqrt,
                                     bias=lneps[0:parts, :], scale=1.0 / F).then_inc(sd_ready, 1)

            def sage(base, i, j, cols, half=None):
                def columns(q):
                    n = BATCHES[cols][q]
                    act.wait_ge(tp_ready, i * (QE * 2) + (QE * (base + j) + q + 1))
                    nc.scalar.activation(aht[q % 2][:, 0:n * P], tp[q % 2][:, 0:n * P], ACT.Copy).then_inc(aht_ready, 1)

                def hidden(q):
                    n, k = BATCHES[cols][q], QE * (base + j) + q + 1
                    act.wait_ge(m1_ready, i * (QE * 2) + k)
                    act.wait_ge(h1t_used, i * (QE * 2) + k)
                    nc.scalar.activation(h1t[q % 2][:, 0:n * P], m1[q % 2][:, 0:n * P], ACT.Relu, bias=b1b[:, :]).then_inc(h1t_ready, 1)

                if half != 1:
                    columns(0)
                    columns(1)
                    hidden(0)
                    columns(2)
                    hidden(1)
                if half != 0:
                    columns(3)
                    hidden(2)
                    hidden(3)

            act.wait_ge(zeros_in, 2)
            for k in range(CLEARS):
                act.dma_start(cleared(adds[0])[:, k * ZW:(k + 1) * ZW], zeros).then_inc(adds_clear[0], 16)
                if k < 4:
                    act.wait_ge(adds_clear[0], 16 * (k + 1))
            act.wait_ge(consts, 3)
            act.wait_ge(weights_in, 16 * 12)
            for r in range(ADDS):
                with act.Fori(0, PAIRS) as i:
                    for s in range(2):
                        n = NCH * r + s
                        if r == 0:
                            root(0, i, 2, s, P, CC)
                        act.wait_ge(merged, i * 2 + (n + 1))
                        act.wait_ge(arow_free, i * 2 + (n + 1))
                        nc.scalar.activation(arow[s], m2[:, 0:CC * F], ACT.Copy).then_inc(arow_ready, 1)
            act.wait_ge(npos_ready, 1)
            act.sem_inc(nt_ready, 2)
            with act.Fori(0, NPP // NB // 2) as i:
                for s in range(2):
                    act.wait_ge(nsum_ready, i * 2 + (s + 1))
                    ntv = v3(nt[s][0:NP_, :], ROW)
                    nc.scalar.activation(ntv[:, :, 0:F], v3(m2[0:NP_, 0:NB * F], F), ACT.Copy).then_inc(nsum_used, 1)
                    nc.scalar.activation(ntv[:, :, F:F + 2], v3(npos[:, bass.ds(i * (4 * NB) + 2 * s * NB, 2 * NB)], 2), ACT.Copy).then_inc(nt_ready, 1)
                    act.wait_ge(nt_ready, i * 2 + (s + 3))
                    act.wait_ge(nsum_used, i * 2 + (s + 2))
                    act.dma_start(node_tab[:, :].rearrange("(p n) f -> p (n f)", p=NP_)[:, bass.ds(i * (2 * NB * ROW) + s * NB * ROW, NB * ROW)],
                                  nt[s][0:NP_, :]).then_inc(nt_out, 16)
                    act.wait_ge(nt_out, i * 32 + 16 * (s + 1))
                    act.nop(nofuse=True)
            def ln(r, i, c, side):
                root(ln_no(r, side, c), i, 2 * len(LN[r]), 0, NP_ if side in "Nn" else P, CC)

            def store(r, i, c):
                n = NCH * (r - R0) + c
                act.wait_ge(scan_done, i * 2 + (n + 1))
                act.wait_ge(tout_free, i * 2 + (n + 1))
                nc.scalar.activation(v3(tout[c % 2], F), sc[c % 2].rearrange("p (f t) -> p t f", t=CC),
                                     ACT.Copy).then_inc(tout_ready, 1)

            def step(r, i, c):
                nc.scalar.activation(km[c % 2].rearrange("p (f t) -> p f t", t=CC),
                                     keepz[:, bass.ds(i * 2 * CC + c * CC, CC)].unsqueeze(1).to_broadcast([P, F, CC]),
                                     ACT.Copy).then_inc(km_ready, 1)
                ln(r, i, c, "S")
                if c:
                    sage(mm_base[r], i, c - 1, CC, 1)
                if r != R0 + 1:
                    store(r, i, c)
                elif c:
                    store(r, i, c - 1)
                if r in ALL_NODES:
                    if c:
                        ln(r, i, c - 1, "n")
                    ln(r, i, c, "N")
                if r == R0 + 2:
                    ln(r, i, c, "D")
                sage(mm_base[r], i, c, CC, 0)

            for r in range(R0, ROUNDS):
                step(r, 0, 0)
                with act.Fori(0, PAIRS - 1) as i:
                    step(r, i, 1)
                    step(r, i, 2)
                step(r, 0, NCH - 1)
                sage(mm_base[r], 0, NCH - 1, CC, 1)
                if r == R0 + 1:
                    store(r, 0, NCH - 1)
                if r in ALL_NODES:
                    ln(r, 0, NCH - 1, "n")
                if r == R0:
                    root(ln_base["last"], 0, 0, 0, NP_, DC_LAST)
                    sage(mm_base["last"], 0, 0, DC_LAST)
                    root(ln_base["last"], 0, 0, 1, NP_, DC_LAST)
            with act.Fori(0, PAIRS) as i:
                for s in range(2):
                    root(ln_base[ROUNDS], i, 2, s, P, CC)

        @block.tensor
        def _(pe):
            pe.wait_ge(bad_ready, 1)
            nc.tensor.matmul(cp[0:1, 0:1], small[:, 0:1], ones[:, 0:1], start=True, stop=True).then_inc(bad_sum, 1)

            def sage(base, i, j, cols, both):
                at = lambda k: i * (QE * 2) + (QE * (base + j) + k + 1)
                col = [sum(BATCHES[cols][:q]) for q in range(QE)]
                pe.wait_ge(ah_ready, i * 2 + (base + j + 1))

                def columns(q):
                    for u in range(BATCHES[cols][q]):
                        ins = nc.tensor.transpose(tp[q % 2][:, u * P:(u + 1) * P], ah[:, (col[q] + u) * P:(col[q] + u + 1) * P], ident[:, :])
                    ins.then_inc(tp_ready, 1)

                def hidden(q):
                    n = BATCHES[cols][q]
                    pe.wait_ge(aht_ready, at(q))
                    nc.tensor.matmul(m1[q % 2][:, 0:n * P], w1b[:, :], aht[q % 2][:, 0:n * P], start=True, stop=True).then_inc(m1_ready, 1)

                def result(q):
                    pe.wait_ge(h1t_ready, at(q))
                    if q == 0:
                        pe.wait_ge(m2_free, i * 2 + (base + j + 1))
                    width = P if both else 2 * F
                    for u in range(BATCHES[cols][q]):
                        rhs = w2b[:, :] if both else w2b[:, :].rearrange("p (t f) -> p t f", f=2 * F)[:, :, F:2 * F]
                        ins = nc.tensor.matmul(m2[:, (col[q] + u) * width:(col[q] + u + 1) * width], h1t[q % 2][:, u * P:(u + 1) * P],
                                               rhs, start=True, stop=True)
                    ins.then_inc(h1t_used, 1)

                columns(0)
                columns(1)
                hidden(0)
                columns(2)
                hidden(1)
                result(0)
                columns(3)
                hidden(2)
                result(1)
                hidden(3)
                pe.sem_inc(ah_free, 1)
                result(2)
                result(3)

            pe.wait_ge(consts, 3)
            pe.wait_ge(cl_ready, 1)
            nc.tensor.transpose(cp[0:F, 128:256], pm_b[:, :], ident[:, :]).then_inc(clt_ready, 1)
            nc.tensor.transpose(cp[0:F, 0:P], state[:, :], ident[:, :]).then_inc(clt_ready, 1)
            pe.wait_ge(ct_ready, 1)
            nc.tensor.transpose(cp[:, 256:256 + F], carry_t[:, 0:P], ident[0:F, 0:F]).then_inc(cc_ready, 1)
            def count(k, at, start, stop):
                pe.wait_ge(*at)
                for h in range(2):
                    ins = nc.tensor.matmul(m1[h][0:NP_, 0:NPP // 2], hot_hi[k % 2][:, 0:NP_],
                                           hot_lo[k % 2][:, h * NPP // 2:(h + 1) * NPP // 2], start=start, stop=stop)
                return ins

            for r in range(ADDS):
                if r == 1:
                    count(0, (hot_0, 4), True, False).then_inc(hist_0, 1)
                with pe.Fori(0, PAIRS) as i:
                    for s in range(2):
                        n = NCH * r + s
                        pe.wait_ge(srcst_ready, i * 2 + (n + 1))
                        for q in range(TILES4):
                            pe.wait_ge(sel_ready, i * (2 * TILES4) + (TILES4 * n + q + 1))
                            for u in range(4):
                                ins = nc.tensor.transpose(dup[(s + q) % 2][:, u * P:(u + 1) * P],
                                                          srcst[:, 4 * q + u:4 * q + u + 1].to_broadcast([P, P]), ident[:, :])
                            ins.then_inc(dup_ready, 1)
                        pe.wait_ge(amsg_ready, i * 2 + (n + 1))
                        pe.wait_ge(arow_ready, i * 2 + (n + 1))
                        for k in range(CC):
                            ins = nc.tensor.matmul(m2[:, k * F:(k + 1) * F], sel[:, k * P:(k + 1) * P], amsg[:, k * F:(k + 1) * F],
                                                   start=True, stop=True)
                        ins.then_inc(merged, 1)
                        if r == 1:
                            for k in range(CC):
                                count(k, (hot_ready, i * (4 * CC) + 2 * (s * CC + k + 1)), False, False).then_inc(hot_used, 1)
                if r == 1:
                    count(0, (hot_0, 5), False, True).then_inc(hist_0, 1)
                    pe.wait_ge(totals_ready, 1)
                    nc.tensor.matmul(m1[0][0:NP_, NPP // 2:NPP // 2 + 1], low[0:NP_, 0:NP_], nrank[:, NPP - 1:NPP],
                                     start=True, stop=True).then_inc(after_ready, 1)
            pe.wait_ge(arow_ready, NCH * ADDS + 1)
            with pe.Fori(0, NPP // NB // 2) as i:
                for s in range(2):
                    pe.wait_ge(nx_in[s], i * 32 + 32)
                    pe.wait_ge(nsum_used, i * 2 + (s + 1))
                    for o in range(0, NB, 16):
                        n = min(16, NB - o)
                        for b in range(BLK + 1):
                            rhs = (v3(nx[s][0:NP_, :], F)[:, o:o + n, :] if b == BLK else
                                   v3(na[s][0:NP_, :], AROW)[:, o:o + n, b * F:(b + 1) * F])
                            ins = nc.tensor.matmul(m2[0:NP_, o * F:(o + n) * F], ident[0:NP_, 0:NP_], rhs, start=b == 0, stop=b == BLK)
                    ins.then_inc(nsum_ready, 1)
            pe.wait_ge(weights_in, 16 * 12)
            def carries(r):
                pe.wait_ge(cl_ready, r - R0 + 2)
                nc.tensor.transpose(cp[0:F, 0:P], state[:, :], ident[:, :]).then_inc(clt_ready, 1)
                pe.wait_ge(ct_ready, r - R0 + 2)
                nc.tensor.transpose(cp[:, 256:256 + F], carry_t[:, 0:P], ident[0:F, 0:F]).then_inc(cc_ready, 1)

            for r in range(R0, ROUNDS):
                with pe.Fori(0, PAIRS - 1) as i:
                    for s in range(2):
                        sage(mm_base[r], i, s, CC, MM[r] == "S")
                sage(mm_base[r], 0, NCH - 2, CC, MM[r] == "S")
                if r != R0 + 1:
                    carries(r)
                sage(mm_base[r], 0, NCH - 1, CC, MM[r] == "S")
                if r == R0 + 1:
                    carries(r)
                if r == R0:
                    sage(mm_base["last"], 0, 0, DC_LAST, False)

        @block.vector
        def _(dve):
            V = nc.vector
            st = Steps(dve, dve_s)
            done = st.done
            V.memset(src_i[:, :], 0).then_inc(edges_0, 1)
            V.memset(dst_i[:, :], N).then_inc(edges_0, 1)
            V.memset(wt[:, :], 0.0).then_inc(edges_0, 1)
            V.memset(zeros, 0.0).then_inc(zeros_in, 1)
            V.memset(zrow[:, :], 0.0).then_inc(zeros_in, 1)
            done(V.memset(w1b[:, :], 0.0))
            done(V.memset(w2b[:, :], 0.0))
            V.memset(ah[:, :], 0.0).then_inc(weights_0, 1)
            V.memset(lneps[:, :], LN_EPS).then_inc(consts, 1)
            done(V.memset(carry_t[:, :], 0.0))
            V.memset(state[:, :], 0.0).then_inc(consts, 1)
            dve.sem_inc(g_free, 2)
            dve.sem_inc(sel_ready, 2)
            dve.sem_inc(arow_ready, 1)
            dve.sem_inc(arow_free, 2)
            dve.sem_inc(nsum_used, 1)
            dve.sem_inc(hot_used, 2)
            dve.sem_inc(h1t_used, 2)
            dve.sem_inc(ah_free, 1)
            dve.sem_inc(m2_free, 1)
            dve.sem_inc(tout_free, 2)
            dve.sem_inc(td_free, 2)
            done(V.memset(ones, 1.0))
            done(V.memset(dprev, -1))
            done(V.memset(dnext, -1))
            dve.wait_ge(edges_in, 16 * 6)

            def neighbours(k):
                done(V.tensor_copy(dprev[:, 1:COLS], dst_i[:, 0:COLS - 1]))
                if k:
                    done(V.tensor_copy(dnext[:, 0:COLS - 1], dst_i[:, 1:COLS]))
                dve.sem_inc(dst_ready, 1)
                dve.wait_ge(prev_in, 16 * (k + 1))
                if k:
                    dve.wait_ge(next_in, 16)

            neighbours(0)
            done(V.tensor_tensor(keep[:, :], dprev, dst_i[:, :], ALU.is_gt))
            V.tensor_reduce(small[:, 0:1], keep[:, :], axis=AX.X, op=ALU.add).then_inc(bad_ready, 1)
            dve.wait_ge(bad_sum, 1)
            done(V.tensor_scalar(small[0:1, 1:2], cp[0:1, 0:1], 0.5, None, ALU.is_gt))
            V.tensor_copy(flag[:, :], small[0:1, 1:2]).then_inc(flag_ready, 1)
            dve.wait_ge(flag_ready, 1)
            dve.wait_ge(iotas, 4)

            bad = dve.value_load(flag[0:1, 0:1], min_val=0, max_val=1)
            with dve.If(bad > 0):
                fb = Steps(dve, rank_steps)
                db = xs[:, 0:SB].bitcast(I32)
                gi = xs[:, SB:2 * SB].bitcast(I32)
                gf, cmpd = xd[:, 0:SB], xd[:, SB:2 * SB]
                dstf, thr, acc, rk = keep, keepz, last, cnt
                dve.wait_ge(sort_in, 1)
                fb.done(V.tensor_scalar(gf, gi, 2.0 ** -16, None, ALU.mult))
                fb.done(V.tensor_copy(dstf[:, :], dst_i[:, :]))
                fb.done(V.tensor_scalar(acc, epos[:, :], float(E), None, ALU.subtract))
                fb.done(V.scalar_tensor_tensor(rk, dstf[:, :], float(N), acc, ALU.is_equal, ALU.mult))
                for k in range(E // SB):
                    fb.done(V.tensor_scalar(thr[:, :], epos[:, :], float(-k * SB), 2.0 ** -16, ALU.add, ALU.mult))
                    dve.wait_ge(sort_dma, 16 * (k + 1))
                    with dve.Fori(0, COLS) as t:
                        fb.loop(t, 2)
                        one = bass.ds(t, 1)
                        fb.done(V.scalar_tensor_tensor(cmpd, db, dstf[:, one], gf, ALU.subtract, ALU.add))
                        fb.done(V.tensor_scalar(cmpd, cmpd, thr[:, one], None, ALU.is_lt, ALU.add, accum_out=acc[:, one]))
                    fb.end(COLS, "rank")
                    fb.done(V.tensor_tensor(rk, rk, acc, ALU.add))
                    dve.sem_inc(block_used, 1)
                V.tensor_copy(xs[:, 0:COLS], rk).then_inc(ranks_ready, 1)
                dve.wait_ge(ranks_ready, 1)
            dve.wait_ge(sorted_ready, 1)

            neighbours(1)
            done(V.tensor_tensor(keep[:, :], dprev, dst_i[:, :], ALU.is_equal))
            done(V.tensor_copy(keepz[:, :], keep[:, :]))
            done(V.memset(v3(keepz[:, :], CC)[:, :, 0], 0.0))
            done(V.tensor_tensor(last, dnext, dst_i[:, :], ALU.not_equal))
            done(V.tensor_tensor_scan(pm[:, :], keep[:, :], keep[:, :], 1.0, ALU.mult, ALU.mult))
            done(V.tensor_tensor_scan(cnt, keep[:, :], ones, 0.0, ALU.mult, ALU.add))
            done(V.tensor_copy(pm_b[:, :], pm[:, COLS - 1:COLS].to_broadcast([P, F])))
            V.tensor_copy(state[:, 0:1], cnt[:, COLS - 1:COLS]).then_inc(cl_ready, 1)

            def carries(n):
                dve.wait_ge(clt_ready, n + 2)
                if n == 0:
                    done(V.tensor_copy(pm_t[:, :], cp[0:F, 128:256]))
                done(V.tensor_copy(last_t[:, :], cp[0:F, 0:P]))
                V.tensor_tensor_scan(carry_t[:, 1:P + 1], pm_t[:, :], last_t[:, :], 0.0, ALU.mult, ALU.add).then_inc(ct_ready, 1)
                dve.wait_ge(cc_ready, n + 1)
                if n > 1:
                    dve.wait_ge(carry_done, 16 * (n - 1))
                done(V.tensor_copy(carry[:, :], cp[:, 256:256 + F]))

            carries(0)
            done(V.scalar_tensor_tensor(cnt, pm[:, :], carry[:, 0:1], cnt, ALU.mult, ALU.add))
            done(V.reciprocal(ic_d[:, :], cnt))
            done(V.tensor_reduce(small[:, 2:3], pm[:, :], axis=AX.X, op=ALU.add))
            done(V.tensor_scalar(small[:, 3:4], last[:, COLS - 1:COLS], -1.0, 1.0, ALU.mult, ALU.add))
            done(V.scalar_tensor_tensor(small[:, 4:5], small[:, 2:3], float(COLS), small[:, 3:4], ALU.is_equal, ALU.mult))
            done(V.tensor_scalar(small[:, 4:5], small[:, 4:5], -1.0, 1.0, ALU.mult, ALU.add))
            done(V.scalar_tensor_tensor(small[:, 4:5], small[:, 2:3], 0.5, small[:, 4:5], ALU.is_gt, ALU.mult))
            done(V.scalar_tensor_tensor(small[:, 5:6], epos[:, 0:1], -1.0, small[:, 2:3], ALU.add, ALU.add))
            done(V.tensor_tensor(small[:, 5:6], small[:, 5:6], ocol[:, :], ALU.subtract))
            done(V.scalar_tensor_tensor(cidx_f[:, :], small[:, 5:6], small[:, 4:5], ocol[:, :], ALU.mult, ALU.add))
            done(V.tensor_copy(cidx[:, :], cidx_f[:, :]))
            done(V.tensor_scalar(sidx[:, :], last, -NOWHERE, NOWHERE, ALU.mult, ALU.add))
            done(V.tensor_tensor(sidx[:, :], sidx[:, :], dst_i[:, :], ALU.add))
            done(V.tensor_scalar(gidx[:, 0:COLS], dst_i[:, :], float(N - 1), None, ALU.min))
            done(V.tensor_copy(gdst[:, 0:COLS], gidx[:, 0:COLS]))
            done(V.tensor_copy(gdst[:, COLS:], gidx[:, 0:2 * CC]))
            done(V.tensor_copy(gidx[:, COLS:2 * COLS], src_i[:, :]))
            for s in range(2):
                V.tensor_copy(idxst[s][:, :], gdst[:, s * CC:(s + 1) * CC]).then_inc(idx_staged, 1)
            dve.wait_ge(weights_in, 16 * 12)
            done(V.tensor_scalar(eps1[:, :], eps1[:, :], 1.0, None, ALU.add))
            quot = aidx[:, :].bitcast(I32)
            done(V.tensor_scalar(dst_lo, dst_i[:, :], 1.0, None, ALU.mult))
            done(V.tensor_scalar(dst_hi, dst_lo, 1.0 / NPP, 0.5 / NPP - 0.5, ALU.mult, ALU.add))
            done(V.tensor_copy(quot, dst_hi))
            done(V.tensor_copy(dst_hi, quot))
            done(V.scalar_tensor_tensor(dst_lo, dst_hi, -float(NPP), dst_lo, ALU.mult, ALU.add))
            for off_by, test in ((-1.0, (0.0, ALU.is_lt)), (1.0, (float(NPP), ALU.is_ge))):
                done(V.tensor_scalar(carry_over, dst_lo, test[0], None, test[1]))
                done(V.scalar_tensor_tensor(dst_hi, carry_over, off_by, dst_hi, ALU.mult, ALU.add))
                done(V.scalar_tensor_tensor(dst_lo, carry_over, -off_by * NPP, dst_lo, ALU.mult, ALU.add))
            for k in range(2):
                V.memset(hot_lo[k], 0.0).then_inc(hot_0, 1)
                V.memset(hot_hi[k][:, :], 0.0).then_inc(hot_0, 1)

            def positions():
                dve.wait_ge(hot_used, COLS + 2)
                V.memset(hot_hi[0][:, :], 0.0).then_inc(hot_0, 1)
                dve.wait_ge(hist_0, 2)
                for h in range(2):
                    done(V.tensor_copy(ncnt[:, h * NPP // 2:(h + 1) * NPP // 2], m1[h][0:NP_, 0:NPP // 2]))
                done(V.memset(nones, 1.0))
                V.tensor_tensor_scan(nrank, nones, ncnt, 0.0, ALU.mult, ALU.add).then_inc(totals_ready, 1)
                dve.wait_ge(after_ready, 1)
                done(V.tensor_tensor(small[0:NP_, 6:7], m1[0][0:NP_, NPP // 2:NPP // 2 + 1], nrank[:, NPP - 1:NPP], ALU.add))
                done(V.tensor_scalar(small[0:NP_, 6:7], small[0:NP_, 6:7], -1.0, float(E - 1), ALU.mult, ALU.add))
                done(V.tensor_scalar(nrank, nrank, small[0:NP_, 6:7], None, ALU.add))
                done(V.tensor_tensor(nrank, nrank, zpos[0:NP_, :], ALU.subtract))
                done(V.scalar_tensor_tensor(nrank, ncnt, 0.5, nrank, ALU.is_gt, ALU.mult))
                dve.wait_ge(adds_clear[ADDS - 1], 16 * CLEARS)
                done(V.tensor_tensor(v3(npos, 2)[:, :, 0], nrank, zpos[0:NP_, :], ALU.add))
                done(V.tensor_scalar(ncnt, ncnt, 1.0, None, ALU.max))
                V.reciprocal(v3(npos, 2)[:, :, 1], ncnt).then_inc(npos_ready, 1)

            def layernorm(xv, base, i, per, j, parts, cols):
                dve.nop(nofuse=True)
                xc3, sq3 = v3(xc[0:parts, 0:cols * F], F), v3(sq[0:parts, 0:cols * F], F)
                c = slice(0, cols)
                done(V.tensor_reduce(s1[0:parts, c], xv, axis=AX.X, op=ALU.add))
                done(V.tensor_scalar(mean[0:parts, c], s1[0:parts, c], 1.0 / F, None, ALU.mult))
                done(V.tensor_tensor(xc3, xv, bc(mean[0:parts, c], F, parts), ALU.subtract))
                done(V.tensor_tensor(sq3, xc3, xc3, ALU.mult))
                V.tensor_reduce(var[0:parts, c], sq3, axis=AX.X, op=ALU.add).then_inc(var_ready, 1)
                dve.wait_ge(sd_ready, i * per + (base + j + 1))
                done(V.reciprocal(rs[0:parts, c], sd[0:parts, c]))
                done(V.tensor_tensor(sq3, xc3, bc(rs[0:parts, c], F, parts), ALU.mult))
                return sq3

            def copy(o, i_):
                return V.tensor_scalar(o, i_, 1.0, None, ALU.mult)

            def m2_out(half, parts, cols):
                if half is None:
                    return v3(m2[0:parts, 0:cols * F], F)
                return m2[0:parts, 0:cols * 2 * F].rearrange("p (t f) -> p t f", f=2 * F)[:, :, half * F:(half + 1) * F]

            def sage_in(xn, agg, parts, cols, at):
                ahv = v3(ah[0:parts, 0:cols * 2 * F], 2 * F)
                dve.wait_ge(ah_free, at)
                if agg is not None:
                    V.tensor_tensor(ahv[:, :, 0:F], *agg, ALU.mult)
                V.tensor_scalar(ahv[:, :, F:2 * F], xn, 0.0, None, ALU.max).then_inc(ah_ready, 1)

            def sage_root(xv, out_half, parts, cols, at, msg_to=None):
                t3 = v3(xc[0:parts, 0:cols * F], F)
                dve.wait_ge(h1t_used, at)
                if msg_to is not None:
                    done(copy(msg_to, m2_out(0, parts, cols)))
                done(V.tensor_tensor(t3, m2_out(out_half, parts, cols), b2b[0:parts, :].unsqueeze(1).to_broadcast([parts, cols, F]), ALU.add))
                dve.sem_inc(m2_free, 1)
                done(V.tensor_tensor(xv, xv, t3, ALU.add))

            def nodes_1(s, i, k, ln_at, mm_at, cols):
                dve.wait_ge(dn_in, i * 2 + (k + 1))
                xn = layernorm(v3(dn[s][0:NP_, 0:cols * F], F), *ln_at, NP_, cols)
                sage_in(xn, None, NP_, cols, i * 2 + mm_at + 1)

            def nodes_2(s, i, ln_at, mm_at, cols):
                dn3 = v3(dn[s][0:NP_, 0:cols * F], F)
                sage_root(dn3, None, NP_, cols, i * (2 * QE) + (QE * (mm_at + 1) + 2))
                xn = layernorm(dn3, *ln_at, NP_, cols)
                done(V.tensor_scalar(xn, xn, 0.0, eps1[0:NP_, :], ALU.max, ALU.mult))
                done(V.tensor_tensor(dn3, dn3, xn, ALU.add))
                dve.sem_inc(dn_done, 1)

            per = {0: 27, 1: 2, 2: 2, 3: 2, 4: 29, 5: 12, 6: 23, 7: 27, 8: 12}
            srcf = gidx[:, COLS:2 * COLS]
            for r in range(ADDS):
                if r == 0:
                    dve.wait_ge(low_ready, 1)
                if r == 1:
                    dve.wait_ge(hist_0, 1)
                    dve.wait_ge(seq_ready, 2)
                with dve.Fori(0, PAIRS) as i:
                    st.loop(i, 2 * per[r])
                    for s in range(2):
                        n = NCH * r + s
                        off = lambda wdt, o=0: bass.ds(i * (2 * CC * wdt) + (s * CC * wdt + o), CC * wdt)
                        D, wb = v3(xd[:, off(F)], F), bc(wt[:, off(1)], F)
                        gv, am, xc3 = v3(g[s][:, 0:CC * AROW], AROW), v3(amsg, F), v3(xc[:, :], F)
                        dve.wait_ge(g_full[s], i * (16 * CC) + 16 * CC * (PAIRS * r + 1))
                        copy(idxst[s][:, :], gdst[:, off(1, 2 * CC)]).then_inc(idx_staged, 1)
                        copy(srcst[:, :], srcf[:, off(1)]).then_inc(srcst_ready, 1)
                        if r == 0:
                            done(copy(D, gv[:, :, 0:F]))
                            dve.sem_inc(g_free, 1)
                            xn = layernorm(D, 0, i, 2, s, P, CC)
                            dve.wait_ge(arow_ready, i * 2 + (n + 1))
                            done(V.scalar_tensor_tensor(am, xn, 0.0, wb, ALU.max, ALU.mult))
                        else:
                            done(V.tensor_reduce(xc3, gv.rearrange("p t (b f) -> p t f b", f=F), axis=AX.X, op=ALU.add))
                            dve.sem_inc(g_free, 1)
                            dve.wait_ge(arow_ready, i * 2 + (n + 1))
                            done(V.tensor_tensor(am, xc3, wb, ALU.mult))
                        for q in range(TILES4):
                            batch = TILES4 * n + q
                            dve.wait_ge(dup_ready, i * (2 * TILES4) + (batch + 1))
                            V.tensor_tensor(v3(sel[:, 4 * q * P:4 * (q + 1) * P], P), v3(dup[(s + q) % 2][:, :], P),
                                            bc(srcst[:, 4 * q:4 * q + 4], P), ALU.is_equal).then_inc(sel_ready, 1)
                            dve.wait_ge(sel_ready, i * (2 * TILES4) + (batch + 3))
                            if r == 0:
                                done(V.tensor_tensor(lowsel, sel[:, 4 * q * P:4 * (q + 1) * P], low, ALU.mult))
                                done(V.tensor_reduce(rep[:, 4 * q:4 * q + 4], v3(lowsel, P), axis=AX.X, op=ALU.add))
                        if r == 0:
                            done(V.tensor_scalar(s1[:, :], srcst[:, :], pcol[:, :], None, ALU.subtract))
                            done(V.scalar_tensor_tensor(s1[:, :], rep[:, :], 0.0, s1[:, :], ALU.is_equal, ALU.mult))
                            done(V.tensor_scalar(s1[:, :], s1[:, :], pcol[:, :], None, ALU.add))
                            done(V.tensor_scalar(s1[:, :], s1[:, :], float(BLK), None, ALU.mult))
                            done(V.tensor_tensor(aidx[:, off(1)], s1[:, :], b4[:, :], ALU.add))
                        dve.sem_inc(amsg_ready, 1)
                        dve.wait_ge(arow_free, i * 2 + (n + 1))
                        copy(aidxst[s][:, :], aidx[:, off(1)]).then_inc(aidx_staged, 1)
                        if r == 1:
                            for k in range(CC):
                                one = bass.ds(i * (2 * CC) + (s * CC + k), 1)
                                dve.wait_ge(hot_used, i * (2 * CC) + (s * CC + k + 1))
                                V.tensor_scalar(hot_lo[k % 2], seq, dst_lo[:, one], None, ALU.is_equal).then_inc(hot_ready, 1)
                                V.tensor_scalar(hot_hi[k % 2][:, 0:NP_], seq[:, 0:NP_], dst_hi[:, one], None,
                                                ALU.is_equal).then_inc(hot_ready, 1)
                st.end(PAIRS, f"round {r}")
                if r == 1:
                    positions()

            with dve.Fori(0, PAIRS) as i:
                st.loop(i, 2 * per[TO_DST])
                for s in range(2):
                    off = lambda wdt, o=0: bass.ds(i * (2 * CC * wdt) + (s * CC * wdt + o), CC * wdt)
                    D, xc3 = v3(xd[:, off(F)], F), v3(xc[:, :], F)
                    dve.wait_ge(g_full[s], i * (16 * CC) + 16 * CC * (PAIRS * TO_DST + 1))
                    copy(idxst[s][:, :], gidx[:, off(1, 2 * CC)]).then_inc(idx_staged, 1)
                    done(V.tensor_reduce(xc3, g[s][:, 0:CC * AROW].rearrange("p (t b f) -> p t f b", f=F, b=BLK), axis=AX.X, op=ALU.add))
                    dve.sem_inc(g_free, 1)
                    done(V.tensor_tensor(D, D, xc3, ALU.add))
            st.end(PAIRS, f"round {TO_DST}")

            def carry_on(r):
                dve.sem_inc(cl_ready, 1)
                carries(r - R0 + 1)
                dve.sem_inc(carry_ready, 1)

            msg_tf = msg.rearrange("p (f t) -> p t f", t=CC)
            msg_ft = msg.rearrange("p (f t) -> p f t", t=CC)
            def step(r, i, c):
                s, n = c % 2, NCH * (r - R0) + c
                off = lambda wdt, o=0, c=c: bass.ds(i * (2 * CC * wdt) + (c * CC * wdt + o), CC * wdt)
                prev = off(F, 0, c - 1)
                gx = v3(g[s][:, 0:CC * ROW], ROW)
                gv = gx[:, :, 0:F]
                xc3 = v3(xc[:, :], F)
                ln_at = lambda side, c=c: (ln_no(r, side, c), i, 2 * len(LN[r]), 0)

                def scan(c):
                    s, n = c % 2, NCH * (r - R0) + c
                    done(V.scalar_tensor_tensor(msg_ft[:, :, 0], state[:, :], keep[:, bass.ds(i * 2 * CC + c * CC, 1)],
                                                msg_ft[:, :, 0], ALU.mult, ALU.add))
                    dve.wait_ge(km_ready, i * 2 + (n + 1))
                    dve.wait_ge(tout_free, i * 2 + (n + 1))
                    done(V.tensor_tensor_scan(sc[s], km[s], msg, 0.0, ALU.mult, ALU.add))
                    done(V.tensor_copy(state[:, :], sc[s].rearrange("p (f t) -> p f t", t=CC)[:, :, CC - 1]))
                    dve.sem_inc(scan_done, 1)

                if c < NCH:
                    cols = off(1)
                    X, D, wb = v3(xs[:, off(F)], F), v3(xd[:, off(F)], F), bc(wt[:, cols], F)
                    dve.wait_ge(g_full[s], i * (16 * CC) + 16 * CC * (PAIRS * r + c // 2 + 1))
                    copy(idxst[s][:, :], gidx[:, off(1, (COLS if r == R0 else 2 * COLS) + 2 * CC)]).then_inc(idx_staged, 1)
                    if r == R0:
                        done(copy(X, gv))
                        done(copy(ic_s[:, cols], gx[:, :, F + 1]))
                        done(copy(gidx[:, off(1, 2 * COLS)], gx[:, :, F]))
                    elif r == R0 + 2:
                        done(V.tensor_tensor(xc3, gv, bc(ic_s[:, cols], F), ALU.mult))
                        done(V.tensor_tensor(X, X, xc3, ALU.add))
                    elif r == R0 + 3:
                        done(V.tensor_tensor(X, X, gv, ALU.add))
                    if r != R0 + 1:
                        dve.sem_inc(g_free, 1)
                    xn = layernorm(X, *ln_at("S"), P, CC)
                    if r == R0:
                        done(V.tensor_scalar(msg_tf, xn, 0.0, None, ALU.max))
                    elif r == R0 + 1:
                        sage_in(xn, (gv, bc(ic_s[:, cols], F)), P, CC, i * 2 + (mm_base[r] + c + 1))
                        dve.wait_ge(ah_ready, i * 2 + (mm_base[r] + c + 1))
                        dve.sem_inc(g_free, 1)
                    elif r == R0 + 2:
                        dve.wait_ge(td_full, i * 2 + (c + 1))
                        done(V.scalar_tensor_tensor(xc3, xn, 0.0, v3(eat[s], F), ALU.max, ALU.add))
                        done(V.tensor_scalar(msg_tf, xc3, 0.0, None, ALU.max))
                        done(V.tensor_scalar(xn, xn, 0.0, eps1[:, :], ALU.max, ALU.mult))
                        done(V.tensor_tensor(X, X, xn, ALU.add))
                    else:
                        done(V.scalar_tensor_tensor(msg_tf, xn, 0.0, wb, ALU.max, ALU.mult))
                    if r != R0 + 1:
                        scan(c)
                    if r != R0 + 1 and c == NCH - 1:
                        carry_on(r)
                if c:
                    if r == R0 + 1:
                        sage_root(v3(xs[:, prev], F), 1, P, CC, i * (2 * QE) + (QE * (mm_base[r] + c) + 2), msg_tf)
                        scan(c - 1)
                    elif r == R0 + 2:
                        sage_root(v3(xd[:, prev], F), None, P, CC, i * (2 * QE) + (QE * (mm_base[r] + c) + 2))
                    else:
                        nodes_2((c - 1) % 2, i, ln_at("n", c - 1), mm_base[r] + c - 1, CC)
                if c < NCH and r in ALL_NODES:
                    nodes_1(s, i, (ALL_NODES[r] and NCH + 1) + c, ln_at("N"), mm_base[r] + c, CC)
                elif c < NCH and r == R0 + 2:
                    xn = layernorm(D, *ln_at("D"), P, CC)
                    sage_in(xn, (v3(td[s], F), bc(ic_d[:, cols], F)), P, CC, i * 2 + (mm_base[r] + c + 1))
                    dve.wait_ge(ah_ready, i * 2 + (mm_base[r] + c + 1))
                    dve.sem_inc(td_free, 1)

            for r in range(R0, ROUNDS):
                done(V.memset(state[:, :], 0.0))
                if r == R0 + 3:
                    done(V.memset(ah[:, :], 0.0))
                step(r, 0, 0)
                with dve.Fori(0, PAIRS - 1) as i:
                    st.loop(i, 2 * per[r])
                    step(r, i, 1)
                    step(r, i, 2)
                st.end(PAIRS - 1, f"round {r}")
                step(r, 0, NCH - 1)
                step(r, 0, NCH)
                if r == R0:
                    done(V.tensor_copy(gidx[:, 3 * COLS:], gidx[:, 2 * COLS:2 * COLS + 2 * CC]))
                    nodes_1(0, 0, NCH, (ln_base["last"], 0, 0, 0), mm_base["last"], DC_LAST)
                    nodes_2(0, 0, (ln_base["last"], 0, 0, 1), mm_base["last"], DC_LAST)
                if r == R0 + 1:
                    carry_on(r)

            def rows_1(i, c):
                s, cols = c % 2, bass.ds(i * 2 * CC + c * CC, CC)
                D, xc3 = v3(xd[:, bass.ds(i * (2 * W) + c * W, W)], F), v3(xc[:, :], F)
                dve.wait_ge(td_full, i * 2 + (NCH + c + 1))
                done(V.tensor_tensor(xc3, v3(td[s], F), bc(ic_d[:, cols], F), ALU.mult))
                done(V.tensor_tensor(D, D, xc3, ALU.add))
                xn = layernorm(D, ln_base[ROUNDS], i, 2, c, P, CC)
                done(V.tensor_scalar(xn, xn, 0.0, eps1[:, :], ALU.max, ALU.mult))
                done(V.tensor_tensor(D, D, xn, ALU.add))

            def rows_2(i, c):
                s = c % 2
                D = v3(xd[:, bass.ds(i * (2 * W) + c * W, W)], F)
                dve.wait_ge(last_full, i * 2 + (c + 1))
                done(V.tensor_tensor(D, D, v3(eat[s], F), ALU.add))
                if c >= 2:
                    dve.wait_ge(out_dma[s], i * (16 * CC) + 16 * CC)
                done(V.tensor_tensor(v3(g[s][:, 0:CC * ROW], ROW)[:, :, 0:F], D, v3(fin[s], F), ALU.add))
                dve.sem_inc(rows_ready, 1)
                dve.sem_inc(td_free, 1)

            for c in range(2):
                rows_1(0, c)
                rows_2(0, c)
            with dve.Fori(0, PAIRS - 1) as i:
                st.loop(i, 2 * per[ROUNDS])
                for c in (2, 3):
                    rows_1(i, c)
                    rows_2(i, c)
            st.end(PAIRS - 1, f"round {ROUNDS}")


_INS = ['x', 'src', 'dst', 'edge_attr_32', 'edge_weight', 'L1_gnn_W1_l', 'L1_gnn_b1', 'L1_gnn_W1_r',
        'L1_gnn_W2_l', 'L1_gnn_b2', 'L1_gnn_W2_r', 'L2_gnn_eps']
_OUTS = [((100000, 32), 'float32')]


def kernel(**inputs):
    import numpy as _np
    import concourse.bacc as _bacc
    from concourse import mybir as _mybir
    from concourse.bass_utils import run_bass_kernel_spmd as _run

    nc = _bacc.Bacc("TRN2", target_bir_lowering=False, num_devices=1)
    arrays, args = {}, []
    for name in _INS:
        a = _np.ascontiguousarray(inputs[name])
        arrays[f"in_{name}_dram"] = a
        args.append(nc.dram_tensor(f"in_{name}_dram", a.shape, _mybir.dt.from_np(a.dtype), kind="ExternalInput").ap())
    for i, (shape, dtype) in enumerate(_OUTS):
        dt = _mybir.dt.from_np(_np.dtype(dtype))
        args.append(nc.dram_tensor(f"out_{i}_dram", shape, dt, kind="ExternalOutput").ap())
    gnn_kernel(nc, *args)
    r = _run(nc, [arrays], core_ids=[0])
    return r.results[0]["out_0_dram"]
```
